# Optimizing a Trainium2 kernel written in Bass

```python
import numpy as np
import jax
import jax.numpy as jnp

def _softmax(x, axis=-1):
    return jax.nn.softmax(x, axis=axis)

def _gelu(x):
    return jax.nn.gelu(x, approximate=True)

def _silu(x):
    return jax.nn.silu(x)

def _sigmoid(x):
    return jax.nn.sigmoid(x)

def _layernorm(x, axis=-1, eps=1e-05):
    m = jnp.mean(x, axis=axis, keepdims=True)
    v = jnp.var(x, axis=axis, keepdims=True)
    return (x - m) / jnp.sqrt(v + eps)

def _scatter_add(tgt, idx, src, axis=0):
    return tgt.at[idx].add(src)

def _segment_sum(src, seg, n):
    return jax.ops.segment_sum(src, seg, n)
kernel_name = 'mk_prb_d1_jaxref_r8_7efaf9'

def setup_inputs(seed: int=0):
    np.random.seed(seed)
    _w = jnp.asarray

    def _L0_attn_setup():
        import jax, jax.numpy as jnp
        import numpy as np
        import math
        N_HEADS = 16
        FACTOR = 5
        key = jax.random.key(seed)
        ks = jax.random.split(key, 9)
        B, T, D = (2, 256, 128)
        s = D ** (-0.5)
        return {'x': jax.random.normal(ks[0], (B, T, D), dtype=jnp.float32), 'Wq': jax.random.normal(ks[1], (D, D), dtype=jnp.float32) * s, 'bq': jnp.zeros((D,), dtype=jnp.float32), 'Wk': jax.random.normal(ks[2], (D, D), dtype=jnp.float32) * s, 'bk': jnp.zeros((D,), dtype=jnp.float32), 'Wv': jax.random.normal(ks[3], (D, D), dtype=jnp.float32) * s, 'bv': jnp.zeros((D,), dtype=jnp.float32), 'Wo': jax.random.normal(ks[4], (D, D), dtype=jnp.float32) * s, 'bo': jnp.zeros((D,), dtype=jnp.float32)}
    _L0_attn_in = _L0_attn_setup()

    def _L0_ffn_setup():
        import jax, jax.numpy as jnp
        import numpy as np
        import math
        MAX_NORM = 0.95
        CURVATURE = 1.0
        TOP_K = 2
        EPS = 1e-07

        def _project_to_ball(x):
            norm = jnp.clip(jnp.linalg.norm(x, axis=-1, keepdims=True), EPS, None)
            scale = jnp.where(norm > MAX_NORM, MAX_NORM / norm, jnp.ones_like(norm))
            return x * scale
        key = jax.random.key(seed)
        ks = jax.random.split(key, 8)
        B, N, D, E, F = (2, 256, 128, 8, 512)
        x = jax.random.normal(ks[0], (B, N, D), dtype=jnp.float32)
        c = jax.random.normal(ks[1], (E, D), dtype=jnp.float32)
        centroids = c / jnp.linalg.norm(c, axis=-1, keepdims=True) * 0.5
        Wp = jax.random.normal(ks[2], (D, D), dtype=jnp.float32) * 0.02
        bp = jnp.zeros((D,), dtype=jnp.float32)
        W1 = jax.random.normal(ks[3], (E, D, F), dtype=jnp.float32) * 0.02
        b1 = jnp.zeros((E, F), dtype=jnp.float32)
        W2 = jax.random.normal(ks[4], (E, F, D), dtype=jnp.float32) * 0.02
        b2 = jnp.zeros((E, D), dtype=jnp.float32)
        return {'x': x, 'centroids': centroids, 'Wp': Wp, 'bp': bp, 'W1': W1, 'b1': b1, 'W2': W2, 'b2': b2}
    _L0_ffn_in = _L0_ffn_setup()
    _d = {'L0_attn_x': _L0_attn_in['x'], 'L0_attn_Wq': _L0_attn_in['Wq'], 'L0_attn_bq': _L0_attn_in['bq'], 'L0_attn_Wk': _L0_attn_in['Wk'], 'L0_attn_bk': _L0_attn_in['bk'], 'L0_attn_Wv': _L0_attn_in['Wv'], 'L0_attn_bv': _L0_attn_in['bv'], 'L0_attn_Wo': _L0_attn_in['Wo'], 'L0_attn_bo': _L0_attn_in['bo'], 'L0_ffn_centroids': _L0_ffn_in['centroids'], 'L0_ffn_Wp': _L0_ffn_in['Wp'], 'L0_ffn_bp': _L0_ffn_in['bp'], 'L0_ffn_W1': _L0_ffn_in['W1'], 'L0_ffn_b1': _L0_ffn_in['b1'], 'L0_ffn_W2': _L0_ffn_in['W2'], 'L0_ffn_b2': _L0_ffn_in['b2']}
    _x0 = _d['L0_attn_x']
    _d['L0_attn_x'] = jax.random.normal(jax.random.fold_in(jax.random.key(seed), 1), (32, 256, 128), dtype=_x0.dtype)
    del _x0
    return _d

def reference(L0_attn_x, L0_attn_Wq, L0_attn_bq, L0_attn_Wk, L0_attn_bk, L0_attn_Wv, L0_attn_bv, L0_attn_Wo, L0_attn_bo, L0_ffn_centroids, L0_ffn_Wp, L0_ffn_bp, L0_ffn_W1, L0_ffn_b1, L0_ffn_W2, L0_ffn_b2):

    def _L0_attn_ref(x, Wq, bq, Wk, bk, Wv, bv, Wo, bo):
        import jax, jax.numpy as jnp
        import numpy as np
        import math
        N_HEADS = 16
        FACTOR = 5
        B, T, D = x.shape
        H = N_HEADS
        Hd = D // H
        scale = Hd ** (-0.5)

        def proj(W, b):
            return (x @ W + b).reshape(B, T, H, Hd).transpose(0, 2, 1, 3)
        q = proj(Wq, bq)
        k = proj(Wk, bk)
        v = proj(Wv, bv)
        q_norm = jnp.sum(jnp.abs(q), axis=-1)
        u = min(int(FACTOR * math.log(T)), T)
        _, index = jax.lax.top_k(q_norm, u)
        scores = jnp.einsum('bhqd,bhkd->bhqk', q, k) * scale
        causal = jnp.tril(jnp.ones((T, T), dtype=bool))
        scores = jnp.where(causal, scores, -jnp.inf)
        sel_scores = jnp.take_along_axis(scores, index[..., None], axis=2)
        sel_attn = jax.nn.softmax(sel_scores, axis=-1)
        sel_out = jnp.einsum('bhut,bhtd->bhud', sel_attn, v)
        attn_output = jnp.zeros_like(q)
        bI = jnp.arange(B)[:, None, None]
        hI = jnp.arange(H)[None, :, None]
        attn_output = attn_output.at[bI, hI, index].set(sel_out)
        out = attn_output.transpose(0, 2, 1, 3).reshape(B, T, D)
        return out @ Wo + bo

    def _L0_ffn_ref(x, centroids, Wp, bp, W1, b1, W2, b2):
        import jax, jax.numpy as jnp
        import numpy as np
        import math
        MAX_NORM = 0.95
        CURVATURE = 1.0
        TOP_K = 2
        EPS = 1e-07

        def _project_to_ball(x):
            norm = jnp.clip(jnp.linalg.norm(x, axis=-1, keepdims=True), EPS, None)
            scale = jnp.where(norm > MAX_NORM, MAX_NORM / norm, jnp.ones_like(norm))
            return x * scale
        B, N, D = x.shape
        E = centroids.shape[0]
        x_hyper = _project_to_ball(x @ Wp + bp)
        c_proj = _project_to_ball(centroids)
        x_norm_sq = jnp.sum(x_hyper * x_hyper, axis=-1)
        c_norm_sq = jnp.sum(c_proj * c_proj, axis=-1)
        x_norm_sq = jnp.clip(x_norm_sq, None, 0.99)
        c_norm_sq = jnp.clip(c_norm_sq, None, 0.99)
        dot = jnp.einsum('bnd,ed->bne', x_hyper, c_proj)
        diff_sq = jnp.maximum(x_norm_sq[..., None] + c_norm_sq - 2.0 * dot, 0.0)
        denom = (1.0 - x_norm_sq)[..., None] * (1.0 - c_norm_sq) + EPS
        arg = jnp.clip(1.0 + 2.0 * diff_sq / denom, 1.0 + EPS, None)
        dist = jnp.arccosh(arg)
        routing_logits = -dist / math.sqrt(CURVATURE)
        top_v, top_i = jax.lax.top_k(routing_logits, TOP_K)
        top_w = jax.nn.softmax(top_v, axis=-1)
        comb = jnp.sum(jax.nn.one_hot(top_i, E, dtype=x.dtype) * top_w[..., None], axis=2)
        h = jax.nn.gelu(jnp.einsum('bnd,edf->bnef', x, W1) + b1, approximate=False)
        y = jnp.einsum('bnef,efd->bned', h, W2) + b2
        out = jnp.einsum('bne,bned->bnd', comb, y)
        return out
    x = L0_attn_x
    xn = _layernorm(x, axis=-1)
    x = x + _L0_attn_ref(xn, L0_attn_Wq, L0_attn_bq, L0_attn_Wk, L0_attn_bk, L0_attn_Wv, L0_attn_bv, L0_attn_Wo, L0_attn_bo) + _L0_ffn_ref(xn, L0_ffn_centroids, L0_ffn_Wp, L0_ffn_bp, L0_ffn_W1, L0_ffn_b1, L0_ffn_W2, L0_ffn_b2)
    return x

_drawn_inputs = setup_inputs


def setup_inputs(seed=0):
    import zlib

    import numpy as np

    out = dict(_drawn_inputs(seed))
    spreads = {'L0_attn_bq': (0.0, 0.1),
     'L0_attn_bk': (0.0, 0.8),
     'L0_attn_bv': (0.0, 0.1),
     'L0_attn_bo': (0.0, 0.1),
     'L0_ffn_bp': (0.0, 0.1),
     'L0_ffn_b1': (0.0, 0.451),
     'L0_ffn_b2': (0.0, 0.1)}
    factors = {}
    for name, (base, spread) in spreads.items():
        noise = np.random.default_rng([zlib.crc32(name.encode()), seed]).standard_normal(out[name].shape)
        drawn = base * np.exp(spread * noise) if base else spread * noise
        out[name] = jnp.asarray(drawn.astype(out[name].dtype))
    for name, factor in factors.items():
        out[name] = (out[name] * factor).astype(out[name].dtype)
    return out
```

```python
import concourse.bass as bass
from concourse import mybir
from contextlib import ExitStack
import math

F32 = mybir.dt.float32
F32R = mybir.dt.float32r
BF16 = mybir.dt.bfloat16
I32 = mybir.dt.int32
U32 = mybir.dt.uint32
ALU = mybir.AluOpType
ACT = mybir.ActivationFunctionType
AX = mybir.AxisListType

P = 128
B, T, D = 32, 256, 128
H, HD = 16, 8
TOP_Q = min(int(5 * math.log(T)), T)
E, F = 8, 512
LN_EPS, EPS, MAX_NORM, MAX_SQ = 1e-5, 1e-7, 0.95, 0.99
TC = T // P
NT = B * TC
NTOK = B * T
HG = 4
NG = H // HG
SL = HG * TOP_Q
NS = H * TOP_Q
GB = P // H
QB = B // GB
FC = F // P
TILE = 256
PT_TILES = 2 * NTOK // TILE + E
LIST = PT_TILES * TILE
NOWHERE = 1 << 20
SCALE = HD ** -0.5
BIG = 1e30
G0 = 2 * D
X0 = G0 + E
NP = X0 + D
KEEP = X0
BO0 = NP
NBR = NP + D
NB1 = E * (FC + 1)


def wait_alone(eng, sem, value, carried):
    eng.wait_ge(sem, value)
    if not isinstance(value, int):
        eng.sem_inc(carried, 1)


class Chain:

    def __init__(self, eng, sem, carried=None):
        self.eng, self.sem, self.carried, self.base, self.n, self.it, self.per = eng, sem, carried, 0, 0, 0, 0

    def turn(self, it, per):
        self.it, self.per, self.n = it, per, 0

    def __call__(self, ins):
        self.n += 1
        ins.then_inc(self.sem, 1)
        wait_alone(self.eng, self.sem, self.it * self.per + (self.base + self.n), self.carried)

    def leave(self, turns):
        assert self.n == self.per or turns == 1, (self.n, self.per)
        self.base += turns * self.n
        self.turn(0, 0)


class Space:

    def __init__(self, nc, stack, stage):
        self.nc, self.stack, self.stage = nc, stack, stage

    def sb(self, name, shape, dt=F32):
        return self.stack.enter_context(self.nc.sbuf_tensor(f"{self.stage}_{name}", shape, dt))

    def ps(self, name, shape, dt=F32):
        return self.stack.enter_context(self.nc.psum_tensor(f"{self.stage}_{name}", shape, dt))

    def sem(self, name):
        return self.stack.enter_context(self.nc.semaphore(f"{self.stage}_{name}"))


def ds(start, size):
    return bass.ds(start, size)


def prepare(nc, k, a):
    with ExitStack() as stack:
        s = Space(nc, stack, "prepare")
        cent = s.sb("cent", [E, D])
        cent_sq = s.sb("cent_sq", [E, D])
        cn = s.sb("cn", [E, 4])
        mhalf = s.sb("mhalf", [P, 1])
        wp_t = s.sb("wp_t", [D, D])
        c_t = s.sb("c_t", [D, E])
        c_tsq = s.sb("c_tsq", [D, E])
        bias_rows = s.sb("bias_rows", [NB1 + 2, P])
        ones_f = s.sb("ones_f", [P, P])
        row = s.sb("row", [1, NBR])
        rest = s.sb("rest", [1, NBR])
        parts = s.sb("parts", [1, 3, NBR], BF16)
        ramp_i = s.sb("ramp_i", [P, T], I32)
        ps_wt = s.ps("ps_wt", [P, P])
        ps_ct = s.ps("ps_ct", [P, E])
        ps_m = s.ps("ps_m", [P, 3, E])
        ps_b = s.ps("ps_b", [P, NB1 + 2])
        loaded, consts, chain_v, chain_g = s.sem("loaded"), s.sem("consts"), s.sem("chain_v"), s.sem("chain_g")
        cn_ready, cscale_ready, cproj_ready = s.sem("cn_ready"), s.sem("cscale_ready"), s.sem("cproj_ready")
        tposed, t_copied, products, parts_ready, parts_moved = (s.sem(n) for n in (
            "tposed", "t_copied", "products", "parts_ready", "parts_moved"))
        block = stack.enter_context(nc.Block())
        loads = [
            (cent[:, :], a["centroids"]), (k.w_proj[:, X0:NP], a["Wp"]), (k.w_proj[:, 0:D], a["Wq"]),
            (k.w_proj[:, D:2 * D], a["Wv"]), (k.wk[:, :], a["Wk"]), (k.wo[:, :], a["Wo"]),
            (bias_rows[NB1:NB1 + 1, :], a["bk"].rearrange("(o d) -> o d", o=1)),
            (bias_rows[NB1 + 1:NB1 + 2, :], a["bp"].rearrange("(o d) -> o d", o=1)),
            (row[:, 0:D], a["bq"].rearrange("(o d) -> o d", o=1)),
            (row[:, D:2 * D], a["bv"].rearrange("(o d) -> o d", o=1)),
            (row[:, X0:NP], a["bp"].rearrange("(o d) -> o d", o=1)),
            (row[:, BO0:NBR], a["bo"].rearrange("(o d) -> o d", o=1)),
        ]
        for e in range(E):
            at = e * (FC + 1)
            loads.append((bias_rows[at:at + FC, :], a["b1"][e, :].rearrange("(c p) -> c p", p=P)))
            loads.append((bias_rows[at + FC:at + FC + 1, :], a["b2"][e:e + 1, :]))

        @block.sync
        def _(sp):
            for dst, src in loads:
                sp.dma_start(dst, src).then_inc(loaded, 16)
            sp.wait_ge(loaded, 16 * len(loads))
            sp.wait_ge(parts_ready, 1)
            for j in range(3):
                sp.dma_start(k.bias3[j:j + 1, :], parts[:, j, :]).then_inc(parts_moved, 16)
            sp.wait_ge(parts_moved, 48)

        @block.gpsimd
        def _(g):
            chain = Chain(g, chain_g)
            g.memset(mhalf[:, :], -0.5)
            g.memset(k.pow_mhalf[:, :], -0.5)
            g.memset(k.pow_half[:, :], 0.5)
            g.memset(ones_f[:, :], 1.0)
            g.memset(k.ident[:, :], 0.0)
            g.memset(k.head_mask[:, :, :, :], 1.0)
            g.memset(k.slot_mask[:, :, :], 1.0)
            g.memset(k.before[:, :], 1.0)
            g.memset(k.ones_bf[:, :], 1.0)
            g.iota(ramp_i[:, :], pattern=[[1, T]], base=0, channel_multiplier=0)
            g.iota(k.expert_id[:, :], pattern=[[1, E]], base=0, channel_multiplier=0,
                   allow_small_or_imprecise_dtypes=True)
            g.iota(k.tile_start[:, :], pattern=[[TILE, PT_TILES]], base=0, channel_multiplier=0,
                   allow_small_or_imprecise_dtypes=True)
            g.iota(k.token_id[:, :, :, 0], pattern=[[P, NT], [0, 2]], base=0, channel_multiplier=1)
            g.iota(k.token_id[:, :, :, 1], pattern=[[P, NT], [NTOK, 2]], base=0, channel_multiplier=1)
            g.iota(k.token_in_batch[:, :], pattern=[[P, TC]], base=0, channel_multiplier=1,
                   allow_small_or_imprecise_dtypes=True)
            g.iota(k.list_init[:, :, 0], pattern=[[0, LIST // P]], base=0, channel_multiplier=0)
            chain(g.iota(k.list_init[:, :, 1], pattern=[[0, LIST // P]], base=NOWHERE, channel_multiplier=0))
            g.tensor_copy(k.token_row[:, :], ramp_i[:, :])
            g.tensor_scalar(k.causal_ramp[:, :], ramp_i[:, :], -BIG, None, ALU.mult)
            g.affine_select(out=k.ident[:, :], in_=k.ident[:, :], compare_op=ALU.not_equal, fill=1.0,
                            base=0, pattern=[[-1, P]], channel_multiplier=1)
            g.affine_select(out=k.before[:, :], in_=k.before[:, :], compare_op=ALU.is_gt, fill=0.0,
                            base=0, pattern=[[1, P]], channel_multiplier=-1)
            g.affine_select(out=k.head_mask[:, :, :, :], in_=k.head_mask[:, :, :, :], compare_op=ALU.is_ge, fill=0.0,
                            base=0, pattern=[[-HD * HG, NG], [-HD, HG], [0, TOP_Q]], channel_multiplier=1)
            chain(g.affine_select(out=k.slot_mask[:, :, :], in_=k.slot_mask[:, :, :], compare_op=ALU.is_ge, fill=0.0,
                                  base=0, pattern=[[-TOP_Q, HG], [0, HD]], channel_multiplier=1))
            g.affine_select(out=k.head_mask[:, :, :, :], in_=k.head_mask[:, :, :, :], compare_op=ALU.is_ge, fill=0.0,
                            base=HD - 1, pattern=[[HD * HG, NG], [HD, HG], [0, TOP_Q]], channel_multiplier=-1)
            g.affine_select(out=k.slot_mask[:, :, :], in_=k.slot_mask[:, :, :], compare_op=ALU.is_ge, fill=0.0,
                            base=TOP_Q - 1, pattern=[[TOP_Q, HG], [0, HD]], channel_multiplier=-1).then_inc(consts, 1)
            g.wait_ge(cn_ready, 1)
            g.tensor_tensor(cn[:, 2:3], cn[:, 1:2], mhalf[0:E, :], ALU.pow).then_inc(cscale_ready, 1)

        @block.vector
        def _(v):
            chain = Chain(v, chain_v, k.carried_v)
            v.wait_ge(loaded, 16 * len(loads))
            chain(v.tensor_tensor(cent_sq[:, :], cent[:, :], cent[:, :], ALU.mult))
            chain(v.tensor_reduce(cn[:, 0:1], cent_sq[:, :], AX.X, ALU.add))
            v.tensor_scalar(cn[:, 1:2], cn[:, 0:1], EPS * EPS, None, ALU.max).then_inc(cn_ready, 1)
            v.wait_ge(cscale_ready, 1)
            chain(v.tensor_scalar(cn[:, 3:4], cn[:, 2:3], MAX_NORM, 1.0, ALU.mult, ALU.min))
            v.tensor_scalar(cent_sq[:, :], cent[:, :], cn[:, 3:4], None, ALU.mult).then_inc(cproj_ready, 1)
            v.wait_ge(tposed, 1)
            v.tensor_copy(wp_t[:, :], ps_wt[:, :])
            v.tensor_copy(k.b_cols[:, :], ps_b[:, :])
            chain(v.tensor_copy(c_t[:, :], ps_ct[:, :]))
            v.tensor_tensor(c_tsq[:, :], c_t[:, :], c_t[:, :], ALU.mult).then_inc(t_copied, 1)
            v.wait_ge(products, 1)
            v.tensor_copy(k.w_proj[:, G0:X0], ps_m[:, 0, :])
            v.tensor_scalar(k.cent_sq[:, :], ps_m[:, 1, :], MAX_SQ, None, ALU.min)
            chain(v.tensor_copy(row[:, G0:X0], ps_m[0:1, 2, :]))
            chain(v.tensor_copy(parts[:, 0, :], row[:, :]))
            chain(v.tensor_tensor(rest[:, :], row[:, :], parts[:, 0, :], ALU.subtract))
            chain(v.tensor_copy(parts[:, 1, :], rest[:, :]))
            chain(v.tensor_tensor(rest[:, :], rest[:, :], parts[:, 1, :], ALU.subtract))
            v.tensor_copy(parts[:, 2, :], rest[:, :]).then_inc(parts_ready, 1)
            v.memset(k.sel_hi[:, :].bitcast(U32), 0)
            v.memset(k.sel_lo[:, :].bitcast(U32), 0)

        @block.tensor
        def _(pe):
            pe.wait_ge(consts, 1)
            pe.wait_ge(loaded, 16 * len(loads))
            pe.wait_ge(cproj_ready, 1)
            pe.transpose(ps_wt[:, :], k.w_proj[:, X0:NP], k.ident[:, :])
            pe.transpose(ps_b[:, :], bias_rows[:, :], k.ident[0:NB1 + 2, 0:NB1 + 2])
            pe.transpose(ps_ct[:, :], cent_sq[:, :], k.ident[0:E, 0:E]).then_inc(tposed, 1)
            pe.wait_ge(t_copied, 1)
            pe.matmul(ps_m[:, 0, :], wp_t[:, :], c_t[:, :], start=True, stop=True)
            pe.matmul(ps_m[:, 1, :], ones_f[:, :], c_tsq[:, :], start=True, stop=True)
            pe.matmul(ps_m[0:1, 2, :], k.b_cols[:, NB1 + 1:NB1 + 2], c_t[:, :], start=True, stop=True).then_inc(products, 1)


def project(nc, k, a):
    turns = B // 2
    with ExitStack() as stack:
        s = Space(nc, stack, "project")
        x_in = s.sb("x_in", [P, 2, TC, D])
        xn = s.sb("xn", [P, 2, TC, D])
        xn_t = s.sb("xn_t", [P, 2, T])
        stats = s.sb("stats", [P, 2, TC, 6])
        mv = s.sb("mv", [P, 2, TC, 2])
        var = s.sb("var", [P, 2, TC])
        rstd = s.sb("rstd", [P, 2, TC])
        sq = s.sb("sq", [P, 2, TC, D])
        ps_xt = [s.ps(f"ps_xt{i}", [P, T]) for i in range(2)]
        ps_pr = [s.ps(f"ps_pr{i}", [P, TC, 512]) for i in range(2)]
        ps_k = [s.ps(f"ps_k{i}", [P, T]) for i in range(2)]
        x_loaded = [s.sem(f"x_loaded{i}") for i in range(2)]
        xn_stored = [s.sem(f"xn_stored{i}") for i in range(2)]
        var_ready, rstd_ready, xn_made, x_tposed, xt_copied, projected, kept, chain_v = (s.sem(n) for n in (
            "var_ready", "rstd_ready", "xn_made", "x_tposed", "xt_copied", "projected", "kept", "chain_v"))
        block = stack.enter_context(nc.Block())
        x_d = a["x"].rearrange("b (c p) d -> p b c d", p=P)
        xn_d = k.xn_dram[:, :].rearrange("(b c p) d -> p b c d", p=P, c=TC)

        @block.sync
        def _(sp):
            for i in range(2):
                sp.dma_start(x_in[:, i, :, :], x_d[:, i, :, :]).then_inc(x_loaded[i], 16)

            def turn(it, more):
                for i in range(2):
                    sp.wait_ge(xn_made, it * 2 + (i + 1))
                    sp.dma_start(xn_d[:, ds(it * 2 + i, 1), :, :].rearrange("p b c d -> p (b c) d"),
                                 xn[:, i, :, :]).then_inc(xn_stored[i], 16)
                    if more:
                        sp.dma_start(x_in[:, i, :, :], x_d[:, ds(it * 2 + (i + 2), 1), :, :].rearrange("p b c d -> p (b c) d")
                                     ).then_inc(x_loaded[i], 16)

            with sp.Fori(0, turns - 1) as it:
                turn(it, True)
            turn(turns - 1, False)
            for i in range(2):
                sp.wait_ge(xn_stored[i], 16 * turns)

        @block.gpsimd
        def _(g):
            with g.Fori(0, turns) as it:
                for i in range(2):
                    g.wait_ge(var_ready, it * 2 + (i + 1))
                    g.tensor_tensor(rstd[:, i, :], var[:, i, :], k.pow_mhalf[:, 0:TC], ALU.pow).then_inc(rstd_ready, 1)

        @block.vector
        def _(v):
            chain = Chain(v, chain_v, k.carried_v)
            per = 4

            def norm(it, first):
                chain.turn(it, per)
                for i in range(2):
                    v.wait_ge(x_loaded[i], it * 16 + 16)
                    for c in range(TC):
                        last = v.bn_stats(stats[:, i, c, :], x_in[:, i, c, :])
                    chain(last)
                    for c in range(TC):
                        last = v.bn_aggr(mv[:, i, c, :], stats[:, i, c, :])
                    chain(last)
                    v.tensor_scalar(var[:, i, :], mv[:, i, :, 1], LN_EPS, None, ALU.add).then_inc(var_ready, 1)
                for i in range(2):
                    if not first:
                        v.wait_ge(xn_stored[i], it * 16)
                        v.wait_ge(x_tposed, it * 2 + (i - 1))
                    v.wait_ge(rstd_ready, it * 2 + (i + 1))
                    for c in range(TC):
                        last = v.tensor_scalar(xn[:, i, c, :], x_in[:, i, c, :], mv[:, i, c, 0:1], rstd[:, i, c:c + 1],
                                               ALU.subtract, ALU.mult)
                    last.then_inc(xn_made, 1)

            def sums(it):
                for i in range(2):
                    v.wait_ge(kept, it * 2 + (i + 1))
                    q = k.qvg[:, ds(it * 4 + 2 * i, 2), 0:D].rearrange("p c (h d) -> p c h d", d=HD)
                    v.tensor_reduce(k.q_norm[:, :, ds(it * 2 + i, 1), :].rearrange("p c b h -> p (c b) h"), q, AX.X, ALU.add,
                                    apply_absolute_value=True)

            norm(0, True)
            with v.Fori(0, turns - 1) as it:
                norm(it + 1, False)
                sums(it)
            sums(turns - 1)

        @block.tensor
        def _(pe):
            def turn(it, first):
                for i in range(2):
                    pe.wait_ge(xn_made, it * 2 + (i + 1))
                    if not first:
                        pe.wait_ge(xt_copied, it * 2 + (i - 1))
                    for c in range(TC):
                        last = pe.transpose(ps_xt[i][:, c * P:(c + 1) * P], xn[:, i, c, :], k.ident[:, :])
                    last.then_inc(x_tposed, 1)
                for i in range(2):
                    pe.wait_ge(xt_copied, it * 2 + (i + 1))
                    if not first:
                        pe.wait_ge(kept, it * 2 + (i - 1))
                    for c in range(TC):
                        pe.matmul(ps_pr[i][:, c, 0:NP], k.ones_bf[0:3, :], k.bias3[:, 0:NP], start=True, stop=False)
                        pe.matmul(ps_pr[i][:, c, 0:NP], xn_t[:, i, c * P:(c + 1) * P], k.w_proj[:, :], start=False, stop=True)
                    pe.matmul(ps_k[i][:, :], k.wk[:, :], xn_t[:, i, :], start=True, stop=True).then_inc(projected, 1)

            turn(0, True)
            with pe.Fori(1, turns) as it:
                turn(it, False)

        @block.scalar
        def _(act):
            def turn(it, first):
                for i in range(2):
                    act.wait_ge(x_tposed, it * 2 + (i + 1))
                    if not first:
                        act.wait_ge(projected, it * 2 + (i - 1))
                    act.activation(xn_t[:, i, :], ps_xt[i][:, :], ACT.Copy).then_inc(xt_copied, 1)
                for i in range(2):
                    act.wait_ge(projected, it * 2 + (i + 1))
                    act.activation(k.qvg[:, ds(it * 4 + 2 * i, 2), :], ps_pr[i][:, :, 0:KEEP], ACT.Copy)
                    act.activation(k.k_t[:, ds(it * (2 * T) + i * T, T)], ps_k[i][:, :], ACT.Identity, bias=k.b_cols[:, NB1:NB1 + 1])
                    for c in range(TC):
                        last = act.activation(sq[:, i, c, :], ps_pr[i][:, c, X0:NP], ACT.Square,
                                              accum_out=k.norm_sq[:, ds(it * 4 + (2 * i + c), 1)])
                    last.then_inc(kept, 1)

            turn(0, True)
            with act.Fori(1, turns) as it:
                turn(it, False)


def route(nc, k):
    with ExitStack() as stack:
        s = Space(nc, stack, "route")
        qn_t = s.sb("qn_t", [P, QB, T])
        top8 = s.sb("top8", [P, QB, 8])
        idx_u = s.sb("idx_u", [P, QB, 32], U32)
        idx_f = s.sb("idx_f", [P, QB, TOP_Q])
        idx_rows = s.sb("idx_rows", [P, SL])
        n2 = s.sb("n2", [P, NT])
        xs = s.sb("xs", [P, NT])
        xsq = s.sb("xsq", [P, NT])
        omx = s.sb("omx", [P, NT])
        omc = s.sb("omc", [P, E])
        t1 = s.sb("t1", [P, NT, E])
        t2 = s.sb("t2", [P, NT, E])
        nega = s.sb("nega", [P, NT, E])
        best = s.sb("best", [P, 2, NT])
        pick = s.sb("pick", [P, 2, NT])
        hot = s.sb("hot", [P, 2, NT, E])
        both = s.sb("both", [P, NT, E], BF16)
        rad = s.sb("rad", [P, 2, NT])
        root = s.sb("root", [P, 2, NT])
        u = s.sb("u", [P, 2, NT])
        usum = s.sb("usum", [P, NT])
        cnt = s.sb("cnt", [P, NT, E])
        run = s.sb("run", [P, E, NT])
        zero64 = s.sb("zero64", [P, NT])
        tiles_i = s.sb("tiles_i", [P, E], I32)
        tiles_f = s.sb("tiles_f", [P, E])
        ends = s.sb("ends", [P, E])
        starts = s.sb("starts", [P, E])
        ge = s.sb("ge", [1, PT_TILES, E])
        te_f = s.sb("te_f", [1, PT_TILES])
        ps_qn = s.ps("ps_qn", [P, QB, T])
        ps_idx = s.ps("ps_idx", [P, P])
        ps_rank = s.ps("ps_rank", [P, NT * E])
        ps_cnt = s.ps("ps_cnt", [P, NT * E])
        qn_tposed, qn_copied, idx_made, idx_stored, idx_loaded, idx_tposed, chain_v = (s.sem(n) for n in (
            "qn_tposed", "qn_copied", "idx_made", "idx_stored", "idx_loaded", "idx_tposed", "chain_v"))
        n2_ready, xs_ready, rad_ready, root_ready, both_ready, ranked, list_inited = (s.sem(n) for n in (
            "n2_ready", "xs_ready", "rad_ready", "root_ready", "both_ready", "ranked", "list_inited"))
        block = stack.enter_context(nc.Block())

        @block.sync
        def _(sp):
            sp.dma_start(k.list_dram[:, :].rearrange("(p n) c -> p n c", p=P), k.list_init[:, :, :].bitcast(U32)).then_inc(list_inited, 16)
            sp.wait_ge(idx_made, 1)
            sp.dma_start(k.idx_dram[:, :].rearrange("(g p) r -> p g r", p=P), idx_f[:, :, :]).then_inc(idx_stored, 16)
            sp.wait_ge(idx_stored, 16)
            sp.dma_start(idx_rows[:, :], k.idx_dram[:, :].rearrange("(n j) r -> n (j r)", j=HG)).then_inc(idx_loaded, 16)
            sp.wait_ge(idx_loaded, 16)
            sp.wait_ge(list_inited, 16)

        @block.tensor
        def _(pe):
            for g in range(QB):
                for c in range(TC):
                    last = pe.transpose(ps_qn[:, g, c * P:(c + 1) * P],
                                        k.q_norm[:, c, g * GB:(g + 1) * GB, :].rearrange("p b h -> p (b h)"), k.ident[:, :])
            last.then_inc(qn_tposed, 1)
            pe.wait_ge(both_ready, 1)
            pair_mask = both[:, :, :].rearrange("p n e -> p (n e)")
            pe.matmul(ps_rank[:, :], k.before[:, :], pair_mask, start=True, stop=True)
            pe.matmul(ps_cnt[:, :], k.ones_bf[:, :], pair_mask, start=True, stop=True).then_inc(ranked, 1)
            pe.wait_ge(idx_loaded, 16)
            pe.transpose(ps_idx[0:SL, :], idx_rows[:, :], k.ident[:, :]).then_inc(idx_tposed, 1)

        @block.scalar
        def _(act):
            act.wait_ge(qn_tposed, 1)
            act.activation(qn_t[:, :, :], ps_qn[:, :, :], ACT.Copy).then_inc(qn_copied, 1)

        @block.gpsimd
        def _(g):
            g.wait_ge(n2_ready, 1)
            g.tensor_tensor(xs[:, :], n2[:, :], k.pow_mhalf[:, 0:NT], ALU.pow).then_inc(xs_ready, 1)
            g.wait_ge(rad_ready, 1)
            g.tensor_tensor(root[:, :, :].rearrange("p s n -> p (s n)"), rad[:, :, :].rearrange("p s n -> p (s n)"),
                            k.pow_half[:, :], ALU.pow).then_inc(root_ready, 1)

        @block.vector
        def _(v):
            chain = Chain(v, chain_v, k.carried_v)
            dots = k.qvg[:, :, G0:X0]

            def over_experts(ap):
                return ap.unsqueeze(2).to_broadcast([P, NT, E])

            def over_tokens(ap):
                return ap.unsqueeze(1).to_broadcast([P, NT, E])

            v.tensor_scalar(n2[:, :], k.norm_sq[:, :], EPS * EPS, None, ALU.max).then_inc(n2_ready, 1)
            v.wait_ge(qn_copied, 1)
            for r in range(0, TOP_Q, 8):
                for g in range(QB):
                    chain(v.max(top8[:, g, :], qn_t[:, g, :]))
                    last = v.max_index(idx_u[:, g, r:r + 8], top8[:, g, :], qn_t[:, g, :])
                    chain(last)
                    if r + 8 < TOP_Q:
                        chain(v.match_replace(qn_t[:, g, :], top8[:, g, :], qn_t[:, g, :], -1.0))
            v.tensor_copy(idx_f[:, :, :], idx_u[:, :, 0:TOP_Q]).then_inc(idx_made, 1)
            v.wait_ge(xs_ready, 1)
            chain(v.tensor_scalar(xs[:, :], xs[:, :], MAX_NORM, 1.0, ALU.mult, ALU.min))
            chain(v.tensor_tensor(xsq[:, :], xs[:, :], xs[:, :], ALU.mult))
            chain(v.tensor_tensor(xsq[:, :], xsq[:, :], k.norm_sq[:, :], ALU.mult))
            chain(v.tensor_scalar(xsq[:, :], xsq[:, :], MAX_SQ, None, ALU.min))
            v.tensor_scalar(omx[:, :], xsq[:, :], -1.0, 1.0, ALU.mult, ALU.add)
            v.tensor_scalar(omc[:, :], k.cent_sq[:, :], -1.0, 1.0, ALU.mult, ALU.add)
            v.tensor_tensor(t2[:, :, :], over_experts(xsq[:, :]), over_tokens(k.cent_sq[:, :]), ALU.add)
            chain(v.tensor_tensor(t1[:, :, :], dots, over_experts(xs[:, :]), ALU.mult))
            chain(v.scalar_tensor_tensor(t2[:, :, :], t1[:, :, :], -2.0, t2[:, :, :], ALU.mult, ALU.add))
            v.tensor_scalar(t2[:, :, :], t2[:, :, :], 0.0, 2.0, ALU.max, ALU.mult)
            chain(v.tensor_tensor(t1[:, :, :], over_experts(omx[:, :]), over_tokens(omc[:, :]), ALU.mult))
            chain(v.tensor_scalar(t1[:, :, :], t1[:, :, :], EPS, None, ALU.add))
            chain(v.reciprocal(t1[:, :, :], t1[:, :, :]))
            chain(v.tensor_tensor(t1[:, :, :], t1[:, :, :], t2[:, :, :], ALU.mult))
            chain(v.tensor_scalar(t1[:, :, :], t1[:, :, :], 1.0, 1.0 + EPS, ALU.add, ALU.max))
            chain(v.tensor_scalar(nega[:, :, :], t1[:, :, :], -1.0, None, ALU.mult))
            for j in range(2):
                chain(v.tensor_reduce(best[:, j, :], nega[:, :, :], AX.X, ALU.max))
                chain(v.tensor_tensor(t2[:, :, :], nega[:, :, :], over_experts(best[:, j, :]), ALU.is_equal))
                chain(v.scalar_tensor_tensor(t2[:, :, :], t2[:, :, :], -float(E), over_tokens(k.expert_id[:, :]), ALU.mult, ALU.add))
                chain(v.tensor_reduce(pick[:, j, :], t2[:, :, :], AX.X, ALU.min))
                chain(v.tensor_scalar(pick[:, j, :], pick[:, j, :], float(E), None, ALU.add))
                chain(v.tensor_tensor(hot[:, j, :, :], over_experts(pick[:, j, :]), over_tokens(k.expert_id[:, :]), ALU.is_equal))
                if j == 0:
                    chain(v.scalar_tensor_tensor(nega[:, :, :], hot[:, 0, :, :], -BIG, nega[:, :, :], ALU.mult, ALU.add))
            v.tensor_tensor(both[:, :, :], hot[:, 0, :, :], hot[:, 1, :, :], ALU.add).then_inc(both_ready, 1)
            chain(v.tensor_scalar(rad[:, :, :], best[:, :, :], -1.0, -1.0, ALU.mult, ALU.add))
            chain(v.tensor_scalar(u[:, :, :], best[:, :, :], -1.0, 1.0, ALU.mult, ALU.add))
            v.tensor_tensor(rad[:, :, :], rad[:, :, :], u[:, :, :], ALU.mult).then_inc(rad_ready, 1)
            v.memset(zero64[:, :], 0.0)
            v.wait_ge(ranked, 1)
            chain(v.tensor_copy(cnt[:, :, :].rearrange("p n e -> p (n e)"), ps_cnt[:, :]))
            for e in range(E):
                last = v.tensor_tensor_scan(run[:, e, :], cnt[:, :, e], zero64[:, :], 0.0, ALU.add, ALU.add)
            chain(last)
            chain(v.tensor_scalar(tiles_i[:, :], run[:, :, NT - 1], float(TILE - 1), None, ALU.add))
            chain(v.tensor_scalar(tiles_i[:, :], tiles_i[:, :], int(math.log2(TILE)), int(math.log2(TILE)),
                                  ALU.arith_shift_right, ALU.logical_shift_left))
            chain(v.tensor_copy(tiles_f[:, :], tiles_i[:, :]))
            chain(v.tensor_tensor_scan(ends[:, :], tiles_f[:, :], zero64[:, 0:E], 0.0, ALU.add, ALU.add))
            chain(v.tensor_tensor(starts[:, :], ends[:, :], tiles_f[:, :], ALU.subtract))
            chain(v.tensor_tensor(t1[:, :, :], run[:, :, :].rearrange("p e n -> p n e"), cnt[:, :, :], ALU.subtract))
            chain(v.tensor_tensor(t1[:, :, :].rearrange("p n e -> p (n e)"), t1[:, :, :].rearrange("p n e -> p (n e)"), ps_rank[:, :], ALU.add))
            chain(v.tensor_tensor(t1[:, :, :], t1[:, :, :], over_tokens(starts[:, :]), ALU.add))
            for j in range(2):
                chain(v.tensor_tensor(t2[:, :, :], t1[:, :, :], hot[:, j, :, :], ALU.mult))
                chain(v.tensor_reduce(pick[:, j, :], t2[:, :, :], AX.X, ALU.add))
            v.tensor_copy(k.place[:, :, :], pick[:, :, :].rearrange("p s n -> p n s"))
            chain(v.tensor_tensor(ge[:, :, :], k.tile_start[:, :].unsqueeze(2).to_broadcast([1, PT_TILES, E]),
                                  starts[0:1, :].unsqueeze(1).to_broadcast([1, PT_TILES, E]), ALU.is_ge))
            chain(v.tensor_reduce(te_f[:, :], ge[:, :, :], AX.X, ALU.add))
            v.tensor_scalar(k.tile_expert[:, :], te_f[:, :], -1.0, None, ALU.add)
            v.wait_ge(root_ready, 1)
            chain(v.tensor_tensor(u[:, :, :], root[:, :, :], best[:, :, :], ALU.subtract))
            chain(v.reciprocal(u[:, :, :], u[:, :, :]))
            chain(v.tensor_tensor(usum[:, :], u[:, 0, :], u[:, 1, :], ALU.add))
            chain(v.reciprocal(usum[:, :], usum[:, :]))
            for j in range(2):
                v.tensor_tensor(k.pair_weight[:, j, :], u[:, j, :], usum[:, :], ALU.mult)
            v.wait_ge(idx_tposed, 1)
            chain(v.tensor_copy(k.idx_col[:, :], ps_idx[0:SL, :]))
            v.tensor_scalar(k.causal_off[:, :], k.idx_col[:, :], 0.5, BIG, ALU.add, ALU.mult)


def attend(nc, k, a):
    with ExitStack() as stack:
        s = Space(nc, stack, "attend")
        idx_row = s.sb("idx_row", [P, 2, NS])
        q_hi = s.sb("q_hi", [P, 2, TC, D], F32R)
        q_lo = s.sb("q_lo", [P, 2, TC, D], F32R)
        v_b = s.sb("v_b", [P, 2, TC, D])
        pick = s.sb("pick_slots", [P, 2, TC, NS], F32R)
        q_sel = s.sb("q_sel", [P, 2, NS])
        masked = s.sb("masked", [SL, 2, NG, T])
        probs = s.sb("probs", [SL, 2, NG, T])
        mx = s.sb("mx", [SL, 2, NG])
        nmx = s.sb("nmx", [SL, 2, NG])
        den = s.sb("den", [SL, 2, NG])
        rden = s.sb("rden", [SL, 2, NG])
        p_t = s.sb("p_t", [P, 2, TC, NS])
        o_t = s.sb("o_t", [P, 2, NS])
        sel1 = s.sb("sel1", [SL, NG, HG * HD])
        sel2 = s.sb("sel2", [SL, NG, HG * HD])
        place_back = s.sb("place_back", [SL, 2, NG, T], F32R)
        at = s.sb("at", [P, 2, T])
        x_in = s.sb("x_again", [P, 2, TC, D])
        list_idx = s.sb("list_idx", [P, 4, 1], U32)
        list_val = s.sb("list_val", [P, 4, 2], U32)
        ps_q = s.ps("ps_q", [P, NS])
        ps_s = s.ps("ps_s", [SL, NG, T])
        ps_p = s.ps("ps_p", [P, TC, 512])
        ps_v = s.ps("ps_v", [P, NS])
        ps_o = s.ps("ps_o", [SL, 512])
        own_o = ps_o[:, :].rearrange("p (g w) -> p g w", g=NG)[:, :, 0:HG * HD]
        ps_a = s.ps("ps_a", [P, 2, T])
        ps_at = ps_a[:, 0, :]
        ps_out = ps_a[:, 1, :]
        row_loaded = [s.sem(f"row_loaded{i}") for i in range(2)]
        x_loaded = [s.sem(f"x_loaded{i}") for i in range(2)]
        list_done = [s.sem(f"list_done{i}") for i in range(4)]
        names = ("staged pick_made q_gathered q_masked scored s_masked maxed exped p_tposed p_copied "
                 "valued o_copied o_tposed sel_made placed at_copied out_ps based back_made "
                 "chain_v chain_g list_staged").split()
        (staged, pick_made, q_gathered, q_masked, scored, s_masked, maxed, exped, p_tposed, p_copied,
         valued, o_copied, o_tposed, sel_made, placed, at_copied, out_ps, based, back_made,
         chain_v, chain_g, list_staged) = (s.sem(n) for n in names)
        block = stack.enter_context(nc.Block())
        x_d = a["x"].rearrange("b (c p) d -> p b c d", p=P)
        idx_d = k.idx_dram[:, :].rearrange("(b h) r -> b (h r)", h=H)
        turns = B // 2


        @block.sync
        def _(sp):
            def turn(it, first):
                for i in range(2):
                    if not first:
                        sp.wait_ge(pick_made, it * 2 + (i - 1))
                    sp.dma_start(idx_row[:, i, :], idx_d[ds(it * 2 + i, 1), :].to_broadcast([P, NS])).then_inc(row_loaded[i], 16)
                    if not first:
                        sp.wait_ge(based, it * 2 + (i - 1))
                    sp.dma_start(x_in[:, i, :, :], x_d[:, ds(it * 2 + i, 1), :, :].rearrange("p b c d -> p (b c) d")
                                 ).then_inc(x_loaded[i], 16)
            turn(0, True)
            with sp.Fori(1, turns) as it:
                turn(it, False)

        @block.gpsimd
        def _(g):
            def stage(it, i, first):
                q = k.qvg[:, ds(it * 4 + 2 * i, 2), 0:D]
                if not first:
                    g.wait_ge(q_gathered, it * 2 + (i - 1))
                g.tensor_copy(q_hi[:, i, :, :], q).then_inc(chain_g, 1)
                wait_alone(g, chain_g, it * 2 + (i + 1), k.carried_g)
                g.tensor_tensor(q_lo[:, i, :, :], q, q_hi[:, i, :, :].bitcast(F32), ALU.subtract)
                if not first:
                    g.wait_ge(valued, it * 2 + (i - 1))
                g.tensor_copy(v_b[:, i, :, :], k.qvg[:, ds(it * 4 + 2 * i, 2), D:2 * D]).then_inc(staged, 1)

            def scatter(it, i, first):
                for j in range(4):
                    n, half = 2 * i + j // 2, j % 2
                    if not first:
                        g.wait_ge(list_done[j], it * 32 + 16 * i)
                    g.tensor_copy(list_idx[:, j, :], k.place[:, ds(it * 4 + n, 1), half]).then_inc(list_staged, 1)
                    g.tensor_copy(list_val[:, j, :], k.token_id[:, ds(it * 4 + n, 1), half, :].rearrange("p n c -> p (n c)")).then_inc(list_staged, 1)
                    wait_alone(g, list_staged, it * 16 + (8 * i + 2 * j + 2), k.carried_g)
                    g.indirect_dma_start(out=k.list_dram[:, :], out_offset=bass.IndirectOffsetOnAxis(ap=list_idx[:, j, :], axis=0),
                                         in_=list_val[:, j, :], in_offset=None).then_inc(list_done[j], 16)

            stage(0, 0, True)
            scatter(0, 0, True)
            stage(0, 1, True)
            scatter(0, 1, False)
            with g.Fori(1, turns) as it:
                for i in range(2):
                    stage(it, i, False)
                    scatter(it, i, False)
            for j in range(4):
                g.wait_ge(list_done[j], 32 * turns)

        def pairs(turn_of, eng):
            turn_of(0, 0, True)
            turn_of(0, 1, True)
            with eng.Fori(1, turns) as it:
                turn_of(it, 0, False)
                turn_of(it, 1, False)

        @block.vector
        def _(v):
            chain = Chain(v, chain_v, k.carried_v)

            def select(it, i, first):
                v.wait_ge(row_loaded[i], it * 16 + 16)
                if not first:
                    v.wait_ge(q_gathered, it * 2 + (i - 1))
                for c in range(TC):
                    last = v.tensor_scalar(pick[:, i, c, :], idx_row[:, i, :], k.token_in_batch[:, c:c + 1], None, ALU.is_equal)
                last.then_inc(pick_made, 1)

            def mask_q(it, i, first):
                v.wait_ge(q_gathered, it * 2 + (i + 1))
                if not first:
                    v.wait_ge(scored, it * 2 + (i - 1))
                v.tensor_tensor(q_sel[:, i, :], ps_q[:, :], k.head_mask[:, :, :, :].rearrange("p g j r -> p (g j r)"),
                                ALU.mult).then_inc(q_masked, 1)

            def maxes(it, i, first):
                v.wait_ge(scored, it * 2 + (i + 1))
                if not first:
                    v.wait_ge(exped, it * 2 + (i - 1))
                for g in range(NG):
                    last = v.scalar_tensor_tensor(masked[:, i, g, :], k.causal_ramp[0:SL, :], k.causal_off[:, ds(it * (2 * NG) + (i * NG + g), 1)],
                                                  ps_s[:, g, :], ALU.add, ALU.min)
                last.then_inc(s_masked, 1)
                v.wait_ge(s_masked, it * 2 + (i + 1))
                chain(v.tensor_reduce(mx[:, i, :], masked[:, i, :, :], AX.X, ALU.max))
                v.tensor_scalar(nmx[:, i, :], mx[:, i, :], -SCALE, None, ALU.mult).then_inc(maxed, 1)

            def back(it, i, first):
                if not first:
                    v.wait_ge(placed, it * 2 + (i - 1))
                for g in range(NG):
                    last = v.tensor_scalar(place_back[:, i, g, :], k.token_row[0:SL, :], k.idx_col[:, ds(it * (2 * NG) + (i * NG + g), 1)],
                                           None, ALU.is_equal)
                last.then_inc(back_made, 1)

            def normalise(it, i, first):
                v.wait_ge(exped, it * 2 + (i + 1))
                chain(v.reciprocal(rden[:, i, :], den[:, i, :]))
                v.wait_ge(o_tposed, it * 2 + (i + 1))
                chain(v.tensor_tensor(sel1[:, :, :], own_o, rden[:, i, :].unsqueeze(2).to_broadcast([SL, NG, HG * HD]), ALU.mult))
                chain(v.tensor_tensor(sel2[:, :, :], sel1[:, :, :], k.slot_mask[:, :, :].rearrange("p j d -> p (j d)").unsqueeze(1)
                                      .to_broadcast([SL, NG, HG * HD]), ALU.mult))
                if not first or i == 1:
                    v.wait_ge(placed, it * 2 + i)
                chain(v.tensor_copy(k.own(k.sel_hi), sel2[:, :, :]))
                v.tensor_tensor(k.own(k.sel_lo), sel2[:, :, :], k.own(k.sel_hi).bitcast(F32), ALU.subtract).then_inc(sel_made, 1)

            def base(it, i, first):
                v.wait_ge(x_loaded[i], it * 16 + 16)
                v.wait_ge(out_ps, it * 2 + (i + 1))
                v.tensor_tensor(k.qvg[:, ds(it * 4 + 2 * i, 2), 0:D], ps_out.rearrange("p (c d) -> p c d", d=D),
                                x_in[:, i, :, :], ALU.add).then_inc(based, 1)

            def whole(it, i, first):
                chain.turn(it * 2 + i, 5)
                select(it, i, first)
                mask_q(it, i, first)
                back(it, i, first)
                maxes(it, i, first)
                normalise(it, i, first)
                base(it, i, first)
                assert chain.n == 5, chain.n

            pairs(whole, v)

        @block.scalar
        def _(act):
            def whole(it, i, first):
                act.wait_ge(maxed, it * 2 + (i + 1))
                if not first:
                    act.wait_ge(p_tposed, it * 2 + (i - 1))
                for g in range(NG):
                    last = act.activation(probs[:, i, g, :], masked[:, i, g, :], ACT.Exp, bias=nmx[:, i, g:g + 1], scale=SCALE,
                                          accum_out=den[:, i, g:g + 1])
                last.then_inc(exped, 1)
                act.wait_ge(p_tposed, it * 2 + (i + 1))
                act.activation(p_t[:, i, :, :], ps_p[:, :, 0:NS], ACT.Copy).then_inc(p_copied, 1)
                act.wait_ge(valued, it * 2 + (i + 1))
                act.activation(o_t[:, i, :], ps_v[:, :], ACT.Copy).then_inc(o_copied, 1)
                act.wait_ge(placed, it * 2 + (i + 1))
                act.activation(at[:, i, :], ps_at, ACT.Copy).then_inc(at_copied, 1)

            pairs(whole, act)

        @block.tensor
        def _(pe):
            def scores(it, i, first):
                pe.wait_ge(staged, it * 2 + (i + 1))
                pe.wait_ge(pick_made, it * 2 + (i + 1))
                if not first or i == 1:
                    pe.wait_ge(q_masked, it * 2 + i)
                for n, half in enumerate((q_hi, q_lo)):
                    for c in range(TC):
                        last = pe.matmul(ps_q[:, :], half[:, i, c, :], pick[:, i, c, :], start=(n + c == 0), stop=(n + c == TC))
                last.then_inc(q_gathered, 1)
                pe.wait_ge(q_masked, it * 2 + (i + 1))
                if not first or i == 1:
                    pe.wait_ge(s_masked, it * 2 + i)
                for g in range(NG):
                    last = pe.matmul(ps_s[:, g, :], q_sel[:, i, g * SL:(g + 1) * SL], k.k_t[:, ds(it * (2 * T) + i * T, T)],
                                     start=True, stop=True)
                last.then_inc(scored, 1)

            def values(it, i, first):
                pe.wait_ge(exped, it * 2 + (i + 1))
                if not first or i == 1:
                    pe.wait_ge(p_copied, it * 2 + i)
                for g in range(NG):
                    for c in range(TC):
                        last = pe.transpose(ps_p[:, c, g * SL:(g + 1) * SL], probs[:, i, g, c * P:(c + 1) * P], k.ident[0:SL, 0:SL])
                last.then_inc(p_tposed, 1)
                pe.wait_ge(p_copied, it * 2 + (i + 1))
                if not first or i == 1:
                    pe.wait_ge(o_copied, it * 2 + i)
                for c in range(TC):
                    last = pe.matmul(ps_v[:, :], v_b[:, i, c, :], p_t[:, i, c, :], start=(c == 0), stop=(c == TC - 1))
                last.then_inc(valued, 1)
                pe.wait_ge(o_copied, it * 2 + (i + 1))
                if not first or i == 1:
                    pe.wait_ge(sel_made, it * 2 + i)
                for g in range(NG):
                    last = pe.transpose(ps_o[:, 96 * g:96 * g + P], o_t[:, i, g * SL:(g + 1) * SL], k.ident[:, :])
                last.then_inc(o_tposed, 1)

            def output(it, i, first):
                pe.wait_ge(sel_made, it * 2 + (i + 1))
                pe.wait_ge(back_made, it * 2 + (i + 1))
                if not first or i == 1:
                    pe.wait_ge(based, it * 2 + i)
                for n, half in enumerate((k.sel_hi, k.sel_lo)):
                    for g in range(NG):
                        last = pe.matmul(ps_at, half[:, g * P:(g + 1) * P], place_back[:, i, g, :],
                                         start=(n + g == 0), stop=(n == 1 and g == NG - 1))
                last.then_inc(placed, 1)
                pe.wait_ge(at_copied, it * 2 + (i + 1))
                for c in range(TC):
                    part = ps_out[:, c * P:(c + 1) * P]
                    pe.matmul(part, k.ones_bf[0:3, :], k.bias3[:, BO0:NBR], start=True, stop=False)
                    last = pe.matmul(part, at[:, i, c * P:(c + 1) * P], k.wo[:, :], start=False, stop=True)
                last.then_inc(out_ps, 1)

            def whole(it, i, first):
                scores(it, i, first)
                values(it, i, first)
                output(it, i, first)

            pairs(whole, pe)


def experts(nc, k, a):
    RING = 4
    turns = PT_TILES // RING
    with ExitStack() as stack:
        s = Space(nc, stack, "experts")
        entry = s.sb("entry", [P, RING, 2, 2], U32)
        rows = s.sb("rows", [P, RING, 2, D])
        w1 = s.sb("w1", [P, 2, F])
        w2 = s.sb("w2", [P, 2, FC, D])
        bias = s.sb("bias", [P, 2, FC + 1])
        x_t = s.sb("x_t", [P, 2, TILE])
        h_t = s.sb("h_t", [P, 2, FC, TILE])
        y_t = s.sb("y_t", [P, 2, TILE])
        y_rows = s.sb("y_rows", [P, RING, 2, D])
        ps_x = s.ps("ps_x", [P, TILE])
        ps_h = [s.ps(f"ps_h{i}", [P, FC, TILE]) for i in range(2)]
        ps_y = s.ps("ps_y", [P, TILE])
        ps_r = s.ps("ps_r", [P, 2, D])
        entry_loaded = [s.sem(f"entry_loaded{i}") for i in range(RING)]
        gathered = [s.sem(f"gathered{i}") for i in range(RING)]
        scattered = [s.sem(f"scattered{i}") for i in range(RING)]
        w1_loaded = [s.sem(f"w1_loaded{i}") for i in range(2)]
        w2_loaded = [s.sem(f"w2_loaded{i}") for i in range(2)]
        b_loaded = [s.sem(f"b_loaded{i}") for i in range(2)]
        x_tposed, xt_copied, upped, gelued, downed, yt_copied, y_tposed, y_copied, issued = (s.sem(n) for n in (
            "x_tposed", "xt_copied", "upped", "gelued", "downed", "yt_copied", "y_tposed", "y_copied", "issued"))
        block = stack.enter_context(nc.Block())
        list_d = k.list_dram[:, :].rearrange("(t h p) c -> p t h c", h=2, p=P)
        w1_d = a["W1"].rearrange("e d f -> d e f")
        w2_d = a["W2"].rearrange("e (c p) d -> p e c d", p=P)


        def ring(turn_of, eng):
            turn_of(0, True)
            with eng.Fori(1, turns) as it:
                turn_of(it, False)

        @block.sync
        def _(sp):
            def turn(it, first):
                for r in range(RING):
                    i = r % 2
                    e = sp.value_load(k.tile_expert[:, ds(it * RING + r, 1)], min_val=0, max_val=E - 1)
                    if not first:
                        sp.wait_ge(scattered[r], it * 32)
                    sp.dma_start(entry[:, r, :, :], list_d[:, ds(it * RING + r, 1), :, :].rearrange("p t h c -> p (t h) c")
                                 ).then_inc(entry_loaded[r], 16)
                    if not first or r >= 2:
                        sp.wait_ge(upped, it * RING + (r - 1))
                    sp.dma_start(w1[:, i, :], w1_d[:, ds(e, 1), :].rearrange("d e f -> d (e f)")).then_inc(w1_loaded[i], 16)
                    if not first or r >= 2:
                        sp.wait_ge(yt_copied, it * RING + (r - 1))
                    sp.dma_start(w2[:, i, :, :], w2_d[:, ds(e, 1), :, :].rearrange("p e c d -> p (e c) d")).then_inc(w2_loaded[i], 16)
                    sp.dma_start(bias[:, i, :], k.b_cols[:, ds(e * (FC + 1), FC + 1)]).then_inc(b_loaded[i], 16)
            ring(turn, sp)

        @block.gpsimd
        def _(g):
            def gather(it, r, first):
                wait_alone(g, entry_loaded[r], it * 16 + 16, k.carried_g)
                if not first:
                    wait_alone(g, x_tposed, it * RING + (r + 1 - RING), k.carried_g)
                for h in range(2):
                    g.indirect_dma_start(out=rows[:, r, h, :], out_offset=None, in_=k.xn_dram[:, :],
                                         in_offset=bass.IndirectOffsetOnAxis(ap=entry[:, r, h, 0:1], axis=0)).then_inc(gathered[r], 16)

            def scatter(it, r):
                wait_alone(g, y_copied, it * RING + (r + 1), k.carried_g)
                for h in range(2):
                    g.indirect_dma_start(out=k.y_dram[:, :], out_offset=bass.IndirectOffsetOnAxis(ap=entry[:, r, h, 1:2], axis=0),
                                         in_=y_rows[:, r, h, :], in_offset=None,
                                         bounds_check=2 * NTOK - 1, oob_is_err=False).then_inc(scattered[r], 16)

            for r in range(3):
                gather(0, r, True)

            def turn(it, first, last):
                for r in range(RING):
                    if r == 0:
                        gather(it, 3, first)
                    elif not last:
                        gather(it + 1, r - 1, False)
                    scatter(it, r)

            turn(0, True, False)
            with g.Fori(1, turns - 1) as it:
                turn(it, False, False)
            turn(turns - 1, False, True)
            for r in range(RING):
                g.wait_ge(scattered[r], 32 * turns)

        @block.tensor
        def _(pe):
            def turn_in(it, r, first):
                pe.wait_ge(gathered[r], it * 32 + 32)
                if not first or r >= 1:
                    pe.wait_ge(xt_copied, it * RING + r)
                for h in range(2):
                    last = pe.transpose(ps_x[:, h * P:(h + 1) * P], rows[:, r, h, :], k.ident[:, :])
                last.then_inc(x_tposed, 1)

            def up(it, r, first):
                i = r % 2
                pe.wait_ge(xt_copied, it * RING + (r + 1))
                pe.wait_ge(w1_loaded[i], it * 32 + 16 * (r // 2 + 1))
                if not first or r >= 2:
                    pe.wait_ge(gelued, it * RING + (r - 1))
                for c in range(FC):
                    last = pe.matmul(ps_h[i][:, c, :], w1[:, i, c * P:(c + 1) * P], x_t[:, i, :], start=True, stop=True)
                last.then_inc(upped, 1)

            def down(it, r, first):
                i = r % 2
                pe.wait_ge(gelued, it * RING + (r + 1))
                pe.wait_ge(w2_loaded[i], it * 32 + 16 * (r // 2 + 1))
                if not first or r >= 1:
                    pe.wait_ge(yt_copied, it * RING + r)
                for c in range(FC):
                    last = pe.matmul(ps_y[:, :], w2[:, i, c, :], h_t[:, i, c, :], start=(c == 0), stop=(c == FC - 1))
                last.then_inc(downed, 1)

            def turn_out(it, r, first):
                i = r % 2
                pe.wait_ge(yt_copied, it * RING + (r + 1))
                if not first or r >= 1:
                    pe.wait_ge(y_copied, it * RING + r)
                for h in range(2):
                    last = pe.transpose(ps_r[:, h, :], y_t[:, i, h * P:(h + 1) * P], k.ident[:, :])
                last.then_inc(y_tposed, 1)

            turn_in(0, 0, True)

            def turn(it, first, last):
                for r in range(RING):
                    up(it, r, first)
                    if r < RING - 1:
                        turn_in(it, r + 1, first)
                    elif not last:
                        turn_in(it + 1, 0, False)
                    down(it, r, first) if False else None
                    if r >= 1:
                        down(it, r - 1, first)
                        if r >= 2:
                            turn_out(it, r - 2, first)
                        elif not first:
                            turn_out(it - 1, RING - 1, False)
                    elif not first:
                        down(it - 1, RING - 1, False)
                        turn_out(it - 1, RING - 2, False)

            turn(0, True, False)
            with pe.Fori(1, turns - 1) as it:
                turn(it, False, False)
            turn(turns - 1, False, True)
            down(turns - 1, RING - 1, False)
            turn_out(turns - 1, RING - 2, False)
            turn_out(turns - 1, RING - 1, False)

        @block.scalar
        def _(act):
            def turn(it, first):
                for r in range(RING):
                    i = r % 2
                    act.wait_ge(upped, it * RING + (r + 1))
                    act.wait_ge(b_loaded[i], it * 32 + 16 * (r // 2 + 1))
                    if not first or r >= 2:
                        act.wait_ge(downed, it * RING + (r - 1))
                    for c in range(FC):
                        last = act.activation(h_t[:, i, c, :], ps_h[i][:, c, :], ACT.Gelu, bias=bias[:, i, c:c + 1])
                    last.then_inc(gelued, 1)
            ring(turn, act)

        @block.vector
        def _(v):
            def x_copy(it, r, first):
                i = r % 2
                v.wait_ge(x_tposed, it * RING + (r + 1))
                if not first or r >= 2:
                    v.wait_ge(upped, it * RING + (r - 1))
                v.tensor_copy(x_t[:, i, :], ps_x[:, :]).then_inc(xt_copied, 1)

            def y_add(it, r, first):
                i = r % 2
                v.wait_ge(downed, it * RING + (r + 1))
                v.wait_ge(b_loaded[i], it * 32 + 16 * (r // 2 + 1))
                if not first or r >= 2:
                    v.wait_ge(y_tposed, it * RING + (r - 1))
                v.tensor_scalar(y_t[:, i, :], ps_y[:, :], bias[:, i, FC:FC + 1], None, ALU.add).then_inc(yt_copied, 1)

            def y_copy(it, r, first):
                v.wait_ge(y_tposed, it * RING + (r + 1))
                if not first:
                    v.wait_ge(scattered[r], it * 32)
                v.tensor_copy(y_rows[:, r, :, :], ps_r[:, :, :]).then_inc(y_copied, 1)

            x_copy(0, 0, True)

            def turn(it, first, last):
                for r in range(RING):
                    if r < RING - 1:
                        x_copy(it, r + 1, first)
                    elif not last:
                        x_copy(it + 1, 0, False)
                    if r >= 1:
                        y_add(it, r - 1, first)
                        if r >= 2:
                            y_copy(it, r - 2, first)
                        elif not first:
                            y_copy(it - 1, RING - 1, False)
                    elif not first:
                        y_add(it - 1, RING - 1, False)
                        y_copy(it - 1, RING - 2, False)

            turn(0, True, False)
            with v.Fori(1, turns - 1) as it:
                turn(it, False, False)
            turn(turns - 1, False, True)
            y_add(turns - 1, RING - 1, False)
            y_copy(turns - 1, RING - 2, False)
            y_copy(turns - 1, RING - 1, False)


def combine(nc, k, out):
    N = 4
    turns = NT // N // 2
    with ExitStack() as stack:
        s = Space(nc, stack, "combine")
        y = s.sb("y", [P, 2, 2, N, D])
        part = s.sb("part", [P, 2, N, D])
        res = s.sb("res", [P, 2, N, D])
        loaded = [s.sem(f"loaded{i}") for i in range(2)]
        stored = [s.sem(f"stored{i}") for i in range(2)]
        halfway, added = s.sem("halfway"), s.sem("added")
        block = stack.enter_context(nc.Block())
        y_d = k.y_dram[:, :].rearrange("(s n p) d -> p s n d", s=2, p=P)
        out_d = out.rearrange("b (c p) d -> p (b c) d", p=P)

        @block.sync
        def _(sp):
            def turn(it, first):
                for i in range(2):
                    if not first:
                        sp.wait_ge(added, it * 2 + (i - 1))
                    for j in range(2):
                        sp.dma_start(y[:, i, j, :, :], y_d[:, j, ds(it * (2 * N) + i * N, N), :]).then_inc(loaded[i], 16)
            turn(0, True)
            with sp.Fori(1, turns) as it:
                turn(it, False)

        @block.vector
        def _(v):
            def turn(it, first):
                for i in range(2):
                    v.wait_ge(loaded[i], it * 32 + 32)
                    for n in range(N):
                        last = v.scalar_tensor_tensor(
                            part[:, i, n, :], y[:, i, 0, n, :], k.pair_weight[:, 0, ds(it * (2 * N) + (i * N + n), 1)],
                            k.qvg[:, ds(it * (2 * N) + (i * N + n), 1), 0:D].rearrange("p n d -> p (n d)"), ALU.mult, ALU.add)
                    last.then_inc(halfway, 1)
                    v.wait_ge(halfway, it * 2 + (i + 1))
                    if not first:
                        v.wait_ge(stored[i], it * 16)
                    for n in range(N):
                        last = v.scalar_tensor_tensor(
                            res[:, i, n, :], y[:, i, 1, n, :], k.pair_weight[:, 1, ds(it * (2 * N) + (i * N + n), 1)],
                            part[:, i, n, :], ALU.mult, ALU.add)
                    last.then_inc(added, 1)
            turn(0, True)
            with v.Fori(1, turns) as it:
                turn(it, False)

        @block.scalar
        def _(act):
            with act.Fori(0, turns) as it:
                for i in range(2):
                    act.wait_ge(added, it * 2 + (i + 1))
                    act.dma_start(out_d[:, ds(it * (2 * N) + i * N, N), :], res[:, i, :, :]).then_inc(stored[i], 16)
            for i in range(2):
                act.wait_ge(stored[i], 16 * turns)


class Kept:

    def __init__(self, nc, s):
        self.w_proj = s.sb("w_proj", [D, NP])
        self.wk = s.sb("wk", [D, D])
        self.wo = s.sb("wo", [D, D])
        self.b_cols = s.sb("b_cols", [P, NB1 + 2])
        self.bias3 = s.sb("bias3", [3, NBR], BF16)
        self.ident = s.sb("ident", [P, P])
        self.before = s.sb("before", [P, P], BF16)
        self.ones_bf = s.sb("ones_bf", [P, P], BF16)
        self.head_mask = s.sb("head_mask", [P, NG, HG, TOP_Q])
        self.slot_mask = s.sb("slot_mask", [SL, HG, HD])
        self.expert_id = s.sb("expert_id", [P, E])
        self.tile_start = s.sb("tile_start", [1, PT_TILES])
        self.token_id = s.sb("token_id", [P, NT, 2, 2], I32)
        self.token_in_batch = s.sb("token_in_batch", [P, TC])
        self.token_row = s.sb("token_row", [P, T])
        self.causal_ramp = s.sb("causal_ramp", [P, T])
        self.list_init = s.sb("list_init", [P, LIST // P, 2], I32)
        self.pow_mhalf = s.sb("pow_mhalf", [P, NT])
        self.pow_half = s.sb("pow_half", [P, 2 * NT])
        self.cent_sq = s.sb("cent_sq", [P, E])
        self.qvg = s.sb("qvg", [P, NT, KEEP])
        self.k_t = s.sb("k_t", [P, B * T])
        self.q_norm = s.sb("q_norm", [P, TC, B, H])
        self.norm_sq = s.sb("norm_sq", [P, NT])
        self.place = s.sb("place", [P, NT, 2], U32)
        self.tile_expert = s.sb("tile_expert", [1, PT_TILES], I32)
        self.pair_weight = s.sb("pair_weight", [P, 2, NT])
        self.idx_col = s.sb("idx_col", [SL, P])
        self.causal_off = s.sb("causal_off", [SL, P])
        self.sel_hi = s.sb("sel_hi", [SL, NG * (P + 32)], F32R)
        self.sel_lo = s.sb("sel_lo", [SL, NG * (P + 32)], F32R)
        self.carried_v, self.carried_g = s.sem("carried_v"), s.sem("carried_g")
        self.xn_dram = nc.dram_tensor("xn_scratch", (NTOK, D), F32).ap()
        self.y_dram = nc.dram_tensor("y_scratch", (2 * NTOK, D), F32).ap()
        self.list_dram = nc.dram_tensor("list_scratch", (LIST, 2), U32).ap()
        self.idx_dram = nc.dram_tensor("idx_scratch", (B * H, TOP_Q), F32).ap()

    def own(self, sel):
        return sel[:, :].rearrange("p (g w) -> p g w", w=P + 32)[:, :, 0:32]


def program(nc, a, out):
    with ExitStack() as stack:
        k = Kept(nc, Space(nc, stack, "kept"))
        prepare(nc, k, a)
        project(nc, k, a)
        route(nc, k)
        attend(nc, k, a)
        experts(nc, k, a)
        combine(nc, k, out)


_INS = ["L0_attn_x", "L0_attn_Wq", "L0_attn_bq", "L0_attn_Wk", "L0_attn_bk", "L0_attn_Wv", "L0_attn_bv", "L0_attn_Wo",
        "L0_attn_bo", "L0_ffn_centroids", "L0_ffn_Wp", "L0_ffn_bp", "L0_ffn_W1", "L0_ffn_b1", "L0_ffn_W2", "L0_ffn_b2"]


def kernel(**inputs):
    import numpy as _np
    import concourse.bacc as _bacc
    from concourse.bass_utils import run_bass_kernel_spmd as _run

    nc = _bacc.Bacc("TRN2", target_bir_lowering=False, num_devices=1)
    arrays, args = {}, {}
    for name in _INS:
        x = _np.ascontiguousarray(inputs[name])
        arrays[f"in_{name}"] = x
        args[name.split("_")[-1]] = nc.dram_tensor(f"in_{name}", x.shape, mybir.dt.from_np(x.dtype), kind="ExternalInput").ap()
    out = nc.dram_tensor("out_0", (B, T, D), F32, kind="ExternalOutput").ap()
    program(nc, args, out)
    r = _run(nc, [arrays], core_ids=[0])
    return r.results[0]["out_0"]
```

```python
import concourse.bass as bass
from concourse import mybir
from contextlib import ExitStack
import math

F32 = mybir.dt.float32
F32R = mybir.dt.float32r
BF16 = mybir.dt.bfloat16
I32 = mybir.dt.int32
U32 = mybir.dt.uint32
ALU = mybir.AluOpType
ACT = mybir.ActivationFunctionType
AX = mybir.AxisListType

P = 128
B, T, D = 32, 256, 128
H, HD = 16, 8
TOP_Q = min(int(5 * math.log(T)), T)
E, F = 8, 512
LN_EPS, EPS, MAX_NORM, MAX_SQ = 1e-5, 1e-7, 0.95, 0.99
TC = T // P
NT = B * TC
NTOK = B * T
HG = 4
NG = H // HG
SL = HG * TOP_Q
NS = H * TOP_Q
GB = P // H
QB = B // GB
FC = F // P
TILE = 256
PT_TILES = 2 * NTOK // TILE + E
LIST = PT_TILES * TILE
XW = D + 1
NOWHERE = 1 << 20
SCALE = HD ** -0.5
SHARE = E * D * F // (B // 2) // P
BIG = 1e30
G0 = 2 * D
X0 = G0 + E
NP = X0 + D
KEEP = X0
BO0 = NP
NBR = NP + D
NB1 = E * (FC + 1)


def wait_alone(eng, sem, value, carried):
    eng.wait_ge(sem, value)
    if not isinstance(value, int):
        eng.sem_inc(carried, 1)


class Chain:

    def __init__(self, eng, sem, carried=None):
        self.eng, self.sem, self.carried, self.base, self.n, self.it, self.per = eng, sem, carried, 0, 0, 0, 0

    def turn(self, it, per):
        self.it, self.per, self.n = it, per, 0

    def __call__(self, ins):
        self.n += 1
        ins.then_inc(self.sem, 1)
        wait_alone(self.eng, self.sem, self.it * self.per + (self.base + self.n), self.carried)

    def leave(self, turns):
        assert self.n == self.per or turns == 1, (self.n, self.per)
        self.base += turns * self.n
        self.turn(0, 0)


class Nth:

    def __init__(self, it, off, size, count):
        self.it, self.off, self.size, self.count = it, off, size, count
        self.n = it * size + off
        self.known = isinstance(it, int)

    def plus(self, m):
        return Nth(self.it, self.off + m, self.size, self.count)

    @property
    def exists(self):
        return not self.known or 0 <= self.n < self.count

    def mod(self, m):
        assert self.size % m == 0
        return self.off % m

    def value(self, lag=0, each=1, part=None, ring=1):
        off = self.off - lag
        if self.known and self.n < lag:
            return None
        within = each if part is None else part + 1
        return self.it * (self.size // ring * each) + (off // ring * each + within)

    def wait(self, eng, sem, lag=0, each=1, part=None, ring=1):
        value = self.value(lag, each, part, ring)
        if value is not None:
            eng.wait_ge(sem, value)

    def wait_alone(self, eng, sem, carried, lag=0, each=1, part=None, ring=1):
        value = self.value(lag, each, part, ring)
        if value is not None:
            wait_alone(eng, sem, value, carried)


class Links:

    def __init__(self, eng, sem, per, carried):
        self.eng, self.sem, self.per, self.carried = eng, sem, per, carried

    def at(self, item):
        self.item, self.k = item, 0

    def __call__(self, ins):
        ins.then_inc(self.sem, 1)
        self.item.wait_alone(self.eng, self.sem, self.carried, each=self.per, part=self.k)
        self.k += 1


class Space:

    def __init__(self, nc, stack, stage):
        self.nc, self.stack, self.stage = nc, stack, stage

    def sb(self, name, shape, dt=F32):
        return self.stack.enter_context(self.nc.sbuf_tensor(f"{self.stage}_{name}", shape, dt))

    def ps(self, name, shape, dt=F32):
        return self.stack.enter_context(self.nc.psum_tensor(f"{self.stage}_{name}", shape, dt))

    def sem(self, name):
        return self.stack.enter_context(self.nc.semaphore(f"{self.stage}_{name}"))


def ds(start, size):
    return bass.ds(start, size)


def prepare(nc, k, a):
    with ExitStack() as stack:
        s = Space(nc, stack, "prepare")
        cent = s.sb("cent", [E, D])
        cent_sq = s.sb("cent_sq", [E, D])
        cn = s.sb("cn", [E, 4])
        mhalf = s.sb("mhalf", [P, 1])
        wp_t = s.sb("wp_t", [D, D])
        c_t = s.sb("c_t", [D, E])
        c_tsq = s.sb("c_tsq", [D, E])
        bias_rows = s.sb("bias_rows", [NB1 + 2, P])
        ones_f = s.sb("ones_f", [P, P])
        row = s.sb("row", [1, NBR])
        rest = s.sb("rest", [1, NBR])
        parts = s.sb("parts", [1, 3, NBR], BF16)
        ramp_i = s.sb("ramp_i", [P, T], I32)
        ps_wt = s.ps("ps_wt", [P, P])
        ps_ct = s.ps("ps_ct", [P, E])
        ps_m = s.ps("ps_m", [P, 3, E])
        ps_b = s.ps("ps_b", [P, NB1 + 2])
        loaded, consts, chain_v, chain_g = s.sem("loaded"), s.sem("consts"), s.sem("chain_v"), s.sem("chain_g")
        cn_ready, cscale_ready, cproj_ready = s.sem("cn_ready"), s.sem("cscale_ready"), s.sem("cproj_ready")
        tposed, t_copied, products, parts_ready, parts_moved = (s.sem(n) for n in (
            "tposed", "t_copied", "products", "parts_ready", "parts_moved"))
        block = stack.enter_context(nc.Block())
        loads = [
            (cent[:, :], a["centroids"]), (k.w_proj[:, X0:NP], a["Wp"]), (k.w_proj[:, 0:D], a["Wq"]),
            (k.w_proj[:, D:2 * D], a["Wv"]), (k.wk[:, :], a["Wk"]), (k.wo[:, :], a["Wo"]),
            (bias_rows[NB1:NB1 + 1, :], a["bk"].rearrange("(o d) -> o d", o=1)),
            (bias_rows[NB1 + 1:NB1 + 2, :], a["bp"].rearrange("(o d) -> o d", o=1)),
            (row[:, 0:D], a["bq"].rearrange("(o d) -> o d", o=1)),
            (row[:, D:2 * D], a["bv"].rearrange("(o d) -> o d", o=1)),
            (row[:, X0:NP], a["bp"].rearrange("(o d) -> o d", o=1)),
            (row[:, BO0:NBR], a["bo"].rearrange("(o d) -> o d", o=1)),
        ]
        for e in range(E):
            at = e * (FC + 1)
            loads.append((bias_rows[at:at + FC, :], a["b1"][e, :].rearrange("(c p) -> c p", p=P)))
            loads.append((bias_rows[at + FC:at + FC + 1, :], a["b2"][e:e + 1, :]))

        @block.sync
        def _(sp):
            for dst, src in loads:
                sp.dma_start(dst, src).then_inc(loaded, 16)
            sp.wait_ge(loaded, 16 * len(loads))
            sp.wait_ge(parts_ready, 1)
            for j in range(3):
                sp.dma_start(k.bias3[j:j + 1, :], parts[:, j, :]).then_inc(parts_moved, 16)
            sp.wait_ge(parts_moved, 48)

        @block.gpsimd
        def _(g):
            chain = Chain(g, chain_g)
            g.memset(mhalf[:, :], -0.5)
            g.memset(k.pow_mhalf[:, :], -0.5)
            g.memset(k.pow_half[:, :], 0.5)
            g.memset(ones_f[:, :], 1.0)
            g.memset(k.ident[:, :], 0.0)
            g.memset(k.head_mask[:, :, :, :], 1.0)
            g.memset(k.slot_mask[:, :, :], 1.0)
            g.memset(k.before[:, :], 1.0)
            g.memset(k.ones_bf[:, :], 1.0)
            g.iota(ramp_i[:, :], pattern=[[1, T]], base=0, channel_multiplier=0)
            g.iota(k.expert_id[:, :], pattern=[[1, E]], base=0, channel_multiplier=0,
                   allow_small_or_imprecise_dtypes=True)
            g.iota(k.tile_start[:, :], pattern=[[TILE, PT_TILES]], base=0, channel_multiplier=0,
                   allow_small_or_imprecise_dtypes=True)
            g.iota(k.token_id[:, :, :], pattern=[[P, NT], [NTOK, 2]], base=0, channel_multiplier=1)
            g.iota(k.token_in_batch[:, :], pattern=[[P, TC]], base=0, channel_multiplier=1,
                   allow_small_or_imprecise_dtypes=True)
            g.memset(k.unused[:, :, 0:D], 0.0)
            chain(g.iota(k.unused[:, :, D].bitcast(I32), pattern=[[0, 8]], base=NOWHERE, channel_multiplier=0))
            g.tensor_copy(k.token_row[:, :], ramp_i[:, :])
            g.tensor_scalar(k.causal_ramp[:, :], ramp_i[:, :], -BIG, None, ALU.mult)
            g.affine_select(out=k.ident[:, :], in_=k.ident[:, :], compare_op=ALU.not_equal, fill=1.0,
                            base=0, pattern=[[-1, P]], channel_multiplier=1)
            g.affine_select(out=k.before[:, :], in_=k.before[:, :], compare_op=ALU.is_gt, fill=0.0,
                            base=0, pattern=[[1, P]], channel_multiplier=-1)
            g.affine_select(out=k.head_mask[:, :, :, :], in_=k.head_mask[:, :, :, :], compare_op=ALU.is_ge, fill=0.0,
                            base=0, pattern=[[-HD * HG, NG], [-HD, HG], [0, TOP_Q]], channel_multiplier=1)
            chain(g.affine_select(out=k.slot_mask[:, :, :], in_=k.slot_mask[:, :, :], compare_op=ALU.is_ge, fill=0.0,
                                  base=0, pattern=[[-TOP_Q, HG], [0, HD]], channel_multiplier=1))
            g.affine_select(out=k.head_mask[:, :, :, :], in_=k.head_mask[:, :, :, :], compare_op=ALU.is_ge, fill=0.0,
                            base=HD - 1, pattern=[[HD * HG, NG], [HD, HG], [0, TOP_Q]], channel_multiplier=-1)
            g.affine_select(out=k.slot_mask[:, :, :], in_=k.slot_mask[:, :, :], compare_op=ALU.is_ge, fill=0.0,
                            base=TOP_Q - 1, pattern=[[TOP_Q, HG], [0, HD]], channel_multiplier=-1).then_inc(consts, 1)
            g.wait_ge(cn_ready, 1)
            g.tensor_tensor(cn[:, 2:3], cn[:, 1:2], mhalf[0:E, :], ALU.pow).then_inc(cscale_ready, 1)

        @block.vector
        def _(v):
            chain = Chain(v, chain_v, k.carried_v)
            v.wait_ge(loaded, 16 * len(loads))
            chain(v.tensor_tensor(cent_sq[:, :], cent[:, :], cent[:, :], ALU.mult))
            chain(v.tensor_reduce(cn[:, 0:1], cent_sq[:, :], AX.X, ALU.add))
            v.tensor_scalar(cn[:, 1:2], cn[:, 0:1], EPS * EPS, None, ALU.max).then_inc(cn_ready, 1)
            v.wait_ge(cscale_ready, 1)
            chain(v.tensor_scalar(cn[:, 3:4], cn[:, 2:3], MAX_NORM, 1.0, ALU.mult, ALU.min))
            v.tensor_scalar(cent_sq[:, :], cent[:, :], cn[:, 3:4], None, ALU.mult).then_inc(cproj_ready, 1)
            v.wait_ge(tposed, 1)
            v.tensor_copy(wp_t[:, :], ps_wt[:, :])
            v.tensor_copy(k.b_cols[:, :], ps_b[:, :])
            chain(v.tensor_copy(c_t[:, :], ps_ct[:, :]))
            v.tensor_tensor(c_tsq[:, :], c_t[:, :], c_t[:, :], ALU.mult).then_inc(t_copied, 1)
            v.wait_ge(products, 1)
            v.tensor_copy(k.w_proj[:, G0:X0], ps_m[:, 0, :])
            v.tensor_scalar(k.cent_sq[:, :], ps_m[:, 1, :], MAX_SQ, None, ALU.min)
            chain(v.tensor_copy(row[:, G0:X0], ps_m[0:1, 2, :]))
            chain(v.tensor_copy(parts[:, 0, :], row[:, :]))
            chain(v.tensor_tensor(rest[:, :], row[:, :], parts[:, 0, :], ALU.subtract))
            chain(v.tensor_copy(parts[:, 1, :], rest[:, :]))
            chain(v.tensor_tensor(rest[:, :], rest[:, :], parts[:, 1, :], ALU.subtract))
            v.tensor_copy(parts[:, 2, :], rest[:, :]).then_inc(parts_ready, 1)
            v.memset(k.sel_hi[:, :].bitcast(U32), 0)
            v.memset(k.sel_lo[:, :].bitcast(U32), 0)

        @block.tensor
        def _(pe):
            pe.wait_ge(consts, 1)
            pe.wait_ge(loaded, 16 * len(loads))
            pe.wait_ge(cproj_ready, 1)
            pe.transpose(ps_wt[:, :], k.w_proj[:, X0:NP], k.ident[:, :])
            pe.transpose(ps_b[:, :], bias_rows[:, :], k.ident[0:NB1 + 2, 0:NB1 + 2])
            pe.transpose(ps_ct[:, :], cent_sq[:, :], k.ident[0:E, 0:E]).then_inc(tposed, 1)
            pe.wait_ge(t_copied, 1)
            pe.matmul(ps_m[:, 0, :], wp_t[:, :], c_t[:, :], start=True, stop=True)
            pe.matmul(ps_m[:, 1, :], ones_f[:, :], c_tsq[:, :], start=True, stop=True)
            pe.matmul(ps_m[0:1, 2, :], k.b_cols[:, NB1 + 1:NB1 + 2], c_t[:, :], start=True, stop=True).then_inc(products, 1)


def project(nc, k, a):
    turns = B // 2
    with ExitStack() as stack:
        s = Space(nc, stack, "project")
        x_in = s.sb("x_in", [P, 2, TC, D])
        xn = s.sb("xn", [P, 2, TC, D])
        xn_t = s.sb("xn_t", [P, 2, T])
        stats = s.sb("stats", [P, 2, TC, 6])
        mv = s.sb("mv", [P, 2, TC, 2])
        var = s.sb("var", [P, 2, TC])
        rstd = s.sb("rstd", [P, 2, TC])
        sq = s.sb("sq", [P, 2, TC, D])
        w_raw = s.sb("w_raw", [P, 2, SHARE])
        w_split = s.sb("w_split", [P, 2, 2, SHARE], F32R)
        ps_xt = [s.ps(f"ps_xt{i}", [P, T]) for i in range(2)]
        ps_pr = [s.ps(f"ps_pr{i}", [P, TC, 512]) for i in range(2)]
        ps_k = [s.ps(f"ps_k{i}", [P, T]) for i in range(2)]
        x_loaded = [s.sem(f"x_loaded{i}") for i in range(2)]
        xn_stored = [s.sem(f"xn_stored{i}") for i in range(2)]
        w_loaded, w_hi_made, w_made, w_stored, rows_inited = (s.sem(n) for n in (
            "w_loaded", "w_hi_made", "w_made", "w_stored", "rows_inited"))
        var_ready, rstd_ready, xn_made, x_tposed, xt_copied, projected, kept, chain_v = (s.sem(n) for n in (
            "var_ready", "rstd_ready", "xn_made", "x_tposed", "xt_copied", "projected", "kept", "chain_v"))
        block = stack.enter_context(nc.Block())
        x_d = a["x"].rearrange("b (c p) d -> p b c d", p=P)
        xn_d = k.xn_dram[:, :].rearrange("(b c p) d -> p b c d", p=P, c=TC)
        w1_d = a["W1"].rearrange("e (u d) (x f) -> (d x) (e u) f", u=2, x=2)
        w2_d = a["W2"].rearrange("e (u p c) d -> p (e u) (c d)", u=2, c=2)
        ws_d = k.w_dram[:, :].rearrange("q (t p m) -> p t q m", p=P, t=turns)
        rows_d = k.rows_dram[:, :].rearrange("(t n p) c -> p t n c", p=P, n=8)
        rows_turns = LIST // P // 8

        @block.sync
        def _(sp):
            def load_w(it):
                for n, w_d in enumerate((w1_d, w2_d)):
                    sp.dma_start(w_raw[:, n, :], w_d[:, ds(it, 1), :].rearrange("p t m -> p (t m)")).then_inc(w_loaded, 16)

            for t in range(rows_turns):
                sp.dma_start(rows_d[:, t, :, :], k.unused[:, :, :]).then_inc(rows_inited, 16)
            load_w(0)
            for i in range(2):
                sp.dma_start(x_in[:, i, :, :], x_d[:, i, :, :]).then_inc(x_loaded[i], 16)

            def turn(it, more):
                for i in range(2):
                    sp.wait_ge(xn_made, it * 2 + (i + 1))
                    sp.dma_start(xn_d[:, ds(it * 2 + i, 1), :, :].rearrange("p b c d -> p (b c) d"),
                                 xn[:, i, :, :]).then_inc(xn_stored[i], 16)
                    if more:
                        sp.dma_start(x_in[:, i, :, :], x_d[:, ds(it * 2 + (i + 2), 1), :, :].rearrange("p b c d -> p (b c) d")
                                     ).then_inc(x_loaded[i], 16)
                sp.wait_ge(w_made, it + 1)
                sp.dma_start(ws_d[:, ds(it, 1), :, :].rearrange("p t q m -> p (t q) m"),
                             w_split[:, :, :, :].rearrange("p n a m -> p (n a) m").bitcast(F32)).then_inc(w_stored, 16)
                if more:
                    load_w(it + 1)

            with sp.Fori(0, turns - 1) as it:
                turn(it, True)
            turn(turns - 1, False)
            for i in range(2):
                sp.wait_ge(xn_stored[i], 16 * turns)
            sp.wait_ge(w_stored, 16 * turns)
            sp.wait_ge(rows_inited, 16 * rows_turns)

        @block.gpsimd
        def _(g):
            with g.Fori(0, turns) as it:
                for i in range(2):
                    g.wait_ge(var_ready, it * 2 + (i + 1))
                    g.tensor_tensor(rstd[:, i, :], var[:, i, :], k.pow_mhalf[:, 0:TC], ALU.pow).then_inc(rstd_ready, 1)

        @block.vector
        def _(v):
            chain = Chain(v, chain_v, k.carried_v)
            per = 4

            def norm(it, first):
                chain.turn(it, per)
                for i in range(2):
                    v.wait_ge(x_loaded[i], it * 16 + 16)
                    for c in range(TC):
                        last = v.bn_stats(stats[:, i, c, :], x_in[:, i, c, :])
                    chain(last)
                    for c in range(TC):
                        last = v.bn_aggr(mv[:, i, c, :], stats[:, i, c, :])
                    chain(last)
                    v.tensor_scalar(var[:, i, :], mv[:, i, :, 1], LN_EPS, None, ALU.add).then_inc(var_ready, 1)
                for i in range(2):
                    if not first:
                        v.wait_ge(xn_stored[i], it * 16)
                        v.wait_ge(x_tposed, it * 2 + (i - 1))
                    v.wait_ge(rstd_ready, it * 2 + (i + 1))
                    for c in range(TC):
                        last = v.tensor_scalar(xn[:, i, c, :], x_in[:, i, c, :], mv[:, i, c, 0:1], rstd[:, i, c:c + 1],
                                               ALU.subtract, ALU.mult)
                    last.then_inc(xn_made, 1)

            def sums(it):
                for i in range(2):
                    v.wait_ge(kept, it * 2 + (i + 1))
                    q = k.qvg[:, ds(it * 4 + 2 * i, 2), 0:D].rearrange("p c (h d) -> p c h d", d=HD)
                    v.tensor_reduce(k.q_norm[:, :, ds(it * 2 + i, 1), :].rearrange("p c b h -> p (c b) h"), q, AX.X, ALU.add,
                                    apply_absolute_value=True)

            def w_low(it):
                v.wait_ge(w_hi_made, it + 1)
                v.tensor_tensor(w_split[:, :, 1, :], w_raw[:, :, :], w_split[:, :, 0, :].bitcast(F32), ALU.subtract).then_inc(w_made, 1)

            norm(0, True)
            with v.Fori(0, turns - 1) as it:
                norm(it + 1, False)
                w_low(it)
                sums(it)
            w_low(turns - 1)
            sums(turns - 1)

        @block.tensor
        def _(pe):
            def turn(it, first):
                for i in range(2):
                    pe.wait_ge(xn_made, it * 2 + (i + 1))
                    if not first:
                        pe.wait_ge(xt_copied, it * 2 + (i - 1))
                    for c in range(TC):
                        last = pe.transpose(ps_xt[i][:, c * P:(c + 1) * P], xn[:, i, c, :], k.ident[:, :])
                    last.then_inc(x_tposed, 1)
                for i in range(2):
                    pe.wait_ge(xt_copied, it * 2 + (i + 1))
                    if not first:
                        pe.wait_ge(kept, it * 2 + (i - 1))
                    for c in range(TC):
                        pe.matmul(ps_pr[i][:, c, 0:NP], k.ones_bf[0:3, :], k.bias3[:, 0:NP], start=True, stop=False)
                        pe.matmul(ps_pr[i][:, c, 0:NP], xn_t[:, i, c * P:(c + 1) * P], k.w_proj[:, :], start=False, stop=True)
                    pe.matmul(ps_k[i][:, :], k.wk[:, :], xn_t[:, i, :], start=True, stop=True).then_inc(projected, 1)

            turn(0, True)
            with pe.Fori(1, turns) as it:
                turn(it, False)

        @block.scalar
        def _(act):
            def turn(it, first):
                for i in range(2):
                    act.wait_ge(x_tposed, it * 2 + (i + 1))
                    if not first:
                        act.wait_ge(projected, it * 2 + (i - 1))
                    act.activation(xn_t[:, i, :], ps_xt[i][:, :], ACT.Copy).then_inc(xt_copied, 1)
                for i in range(2):
                    act.wait_ge(projected, it * 2 + (i + 1))
                    act.activation(k.qvg[:, ds(it * 4 + 2 * i, 2), :], ps_pr[i][:, :, 0:KEEP], ACT.Copy)
                    act.activation(k.k_t[:, ds(it * (2 * T) + i * T, T)], ps_k[i][:, :], ACT.Identity, bias=k.b_cols[:, NB1:NB1 + 1])
                    for c in range(TC):
                        last = act.activation(sq[:, i, c, :], ps_pr[i][:, c, X0:NP], ACT.Square,
                                              accum_out=k.norm_sq[:, ds(it * 4 + (2 * i + c), 1)])
                    last.then_inc(kept, 1)

            def w_high(it, first):
                act.wait_ge(w_loaded, it * 32 + 32)
                if not first:
                    act.wait_ge(w_stored, it * 16)
                act.activation(w_split[:, :, 0, :], w_raw[:, :, :], ACT.Copy).then_inc(w_hi_made, 1)

            w_high(0, True)
            turn(0, True)
            with act.Fori(1, turns) as it:
                w_high(it, False)
                turn(it, False)


def route(nc, k):
    with ExitStack() as stack:
        s = Space(nc, stack, "route")
        qn_t = s.sb("qn_t", [P, QB, T])
        top8 = s.sb("top8", [P, QB, 8])
        idx_u = s.sb("idx_u", [P, QB, 32], U32)
        idx_f = s.sb("idx_f", [P, QB, TOP_Q])
        idx_rows = s.sb("idx_rows", [P, SL])
        n2 = s.sb("n2", [P, NT])
        xs = s.sb("xs", [P, NT])
        xsq = s.sb("xsq", [P, NT])
        omx = s.sb("omx", [P, NT])
        omc = s.sb("omc", [P, E])
        t1 = s.sb("t1", [P, NT, E])
        t2 = s.sb("t2", [P, NT, E])
        nega = s.sb("nega", [P, NT, E])
        best = s.sb("best", [P, 2, NT])
        pick = s.sb("pick", [P, 2, NT])
        hot = s.sb("hot", [P, 2, NT, E])
        both = s.sb("both", [P, NT, E], BF16)
        rad = s.sb("rad", [P, 2, NT])
        root = s.sb("root", [P, 2, NT])
        u = s.sb("u", [P, 2, NT])
        usum = s.sb("usum", [P, NT])
        cnt = s.sb("cnt", [P, NT, E])
        run = s.sb("run", [P, E, NT])
        zero64 = s.sb("zero64", [P, NT])
        tiles_i = s.sb("tiles_i", [P, E], I32)
        tiles_f = s.sb("tiles_f", [P, E])
        ends = s.sb("ends", [P, E])
        starts = s.sb("starts", [P, E])
        ge = s.sb("ge", [1, PT_TILES, E])
        te_f = s.sb("te_f", [1, PT_TILES])
        ps_qn = s.ps("ps_qn", [P, QB, T])
        ps_idx = s.ps("ps_idx", [P, P])
        ps_rank = s.ps("ps_rank", [P, NT * E])
        ps_cnt = s.ps("ps_cnt", [P, NT * E])
        qn_tposed, qn_copied, idx_made, idx_stored, idx_loaded, idx_tposed, chain_v = (s.sem(n) for n in (
            "qn_tposed", "qn_copied", "idx_made", "idx_stored", "idx_loaded", "idx_tposed", "chain_v"))
        n2_ready, xs_ready, rad_ready, root_ready, both_ready, ranked = (s.sem(n) for n in (
            "n2_ready", "xs_ready", "rad_ready", "root_ready", "both_ready", "ranked"))
        block = stack.enter_context(nc.Block())

        @block.sync
        def _(sp):
            sp.wait_ge(idx_made, 1)
            sp.dma_start(k.idx_dram[:, :].rearrange("(g p) r -> p g r", p=P), idx_f[:, :, :]).then_inc(idx_stored, 16)
            sp.wait_ge(idx_stored, 16)
            sp.dma_start(idx_rows[:, :], k.idx_dram[:, :].rearrange("(n j) r -> n (j r)", j=HG)).then_inc(idx_loaded, 16)
            sp.wait_ge(idx_loaded, 16)

        @block.tensor
        def _(pe):
            for g in range(QB):
                for c in range(TC):
                    last = pe.transpose(ps_qn[:, g, c * P:(c + 1) * P],
                                        k.q_norm[:, c, g * GB:(g + 1) * GB, :].rearrange("p b h -> p (b h)"), k.ident[:, :])
            last.then_inc(qn_tposed, 1)
            pe.wait_ge(both_ready, 1)
            pair_mask = both[:, :, :].rearrange("p n e -> p (n e)")
            pe.matmul(ps_rank[:, :], k.before[:, :], pair_mask, start=True, stop=True)
            pe.matmul(ps_cnt[:, :], k.ones_bf[:, :], pair_mask, start=True, stop=True).then_inc(ranked, 1)
            pe.wait_ge(idx_loaded, 16)
            pe.transpose(ps_idx[0:SL, :], idx_rows[:, :], k.ident[:, :]).then_inc(idx_tposed, 1)

        @block.scalar
        def _(act):
            act.wait_ge(qn_tposed, 1)
            act.activation(qn_t[:, :, :], ps_qn[:, :, :], ACT.Copy).then_inc(qn_copied, 1)

        @block.gpsimd
        def _(g):
            g.wait_ge(n2_ready, 1)
            g.tensor_tensor(xs[:, :], n2[:, :], k.pow_mhalf[:, 0:NT], ALU.pow).then_inc(xs_ready, 1)
            g.wait_ge(rad_ready, 1)
            g.tensor_tensor(root[:, :, :].rearrange("p s n -> p (s n)"), rad[:, :, :].rearrange("p s n -> p (s n)"),
                            k.pow_half[:, :], ALU.pow).then_inc(root_ready, 1)

        @block.vector
        def _(v):
            chain = Chain(v, chain_v, k.carried_v)
            dots = k.qvg[:, :, G0:X0]

            def over_experts(ap):
                return ap.unsqueeze(2).to_broadcast([P, NT, E])

            def over_tokens(ap):
                return ap.unsqueeze(1).to_broadcast([P, NT, E])

            v.tensor_scalar(n2[:, :], k.norm_sq[:, :], EPS * EPS, None, ALU.max).then_inc(n2_ready, 1)
            v.wait_ge(qn_copied, 1)
            for r in range(0, TOP_Q, 8):
                for g in range(QB):
                    chain(v.max(top8[:, g, :], qn_t[:, g, :]))
                    last = v.max_index(idx_u[:, g, r:r + 8], top8[:, g, :], qn_t[:, g, :])
                    chain(last)
                    if r + 8 < TOP_Q:
                        chain(v.match_replace(qn_t[:, g, :], top8[:, g, :], qn_t[:, g, :], -1.0))
            v.tensor_copy(idx_f[:, :, :], idx_u[:, :, 0:TOP_Q]).then_inc(idx_made, 1)
            v.wait_ge(xs_ready, 1)
            chain(v.tensor_scalar(xs[:, :], xs[:, :], MAX_NORM, 1.0, ALU.mult, ALU.min))
            chain(v.tensor_tensor(xsq[:, :], xs[:, :], xs[:, :], ALU.mult))
            chain(v.tensor_tensor(xsq[:, :], xsq[:, :], k.norm_sq[:, :], ALU.mult))
            chain(v.tensor_scalar(xsq[:, :], xsq[:, :], MAX_SQ, None, ALU.min))
            v.tensor_scalar(omx[:, :], xsq[:, :], -1.0, 1.0, ALU.mult, ALU.add)
            v.tensor_scalar(omc[:, :], k.cent_sq[:, :], -1.0, 1.0, ALU.mult, ALU.add)
            v.tensor_tensor(t2[:, :, :], over_experts(xsq[:, :]), over_tokens(k.cent_sq[:, :]), ALU.add)
            chain(v.tensor_tensor(t1[:, :, :], dots, over_experts(xs[:, :]), ALU.mult))
            chain(v.scalar_tensor_tensor(t2[:, :, :], t1[:, :, :], -2.0, t2[:, :, :], ALU.mult, ALU.add))
            v.tensor_scalar(t2[:, :, :], t2[:, :, :], 0.0, 2.0, ALU.max, ALU.mult)
            chain(v.tensor_tensor(t1[:, :, :], over_experts(omx[:, :]), over_tokens(omc[:, :]), ALU.mult))
            chain(v.tensor_scalar(t1[:, :, :], t1[:, :, :], EPS, None, ALU.add))
            chain(v.reciprocal(t1[:, :, :], t1[:, :, :]))
            chain(v.tensor_tensor(t1[:, :, :], t1[:, :, :], t2[:, :, :], ALU.mult))
            chain(v.tensor_scalar(t1[:, :, :], t1[:, :, :], 1.0, 1.0 + EPS, ALU.add, ALU.max))
            chain(v.tensor_scalar(nega[:, :, :], t1[:, :, :], -1.0, None, ALU.mult))
            for j in range(2):
                chain(v.tensor_reduce(best[:, j, :], nega[:, :, :], AX.X, ALU.max))
                chain(v.tensor_tensor(t2[:, :, :], nega[:, :, :], over_experts(best[:, j, :]), ALU.is_equal))
                chain(v.scalar_tensor_tensor(t2[:, :, :], t2[:, :, :], -float(E), over_tokens(k.expert_id[:, :]), ALU.mult, ALU.add))
                chain(v.tensor_reduce(pick[:, j, :], t2[:, :, :], AX.X, ALU.min))
                chain(v.tensor_scalar(pick[:, j, :], pick[:, j, :], float(E), None, ALU.add))
                chain(v.tensor_tensor(hot[:, j, :, :], over_experts(pick[:, j, :]), over_tokens(k.expert_id[:, :]), ALU.is_equal))
                if j == 0:
                    chain(v.scalar_tensor_tensor(nega[:, :, :], hot[:, 0, :, :], -BIG, nega[:, :, :], ALU.mult, ALU.add))
            v.tensor_tensor(both[:, :, :], hot[:, 0, :, :], hot[:, 1, :, :], ALU.add).then_inc(both_ready, 1)
            chain(v.tensor_scalar(rad[:, :, :], best[:, :, :], -1.0, -1.0, ALU.mult, ALU.add))
            chain(v.tensor_scalar(u[:, :, :], best[:, :, :], -1.0, 1.0, ALU.mult, ALU.add))
            v.tensor_tensor(rad[:, :, :], rad[:, :, :], u[:, :, :], ALU.mult).then_inc(rad_ready, 1)
            v.memset(zero64[:, :], 0.0)
            v.wait_ge(ranked, 1)
            chain(v.tensor_copy(cnt[:, :, :].rearrange("p n e -> p (n e)"), ps_cnt[:, :]))
            for e in range(E):
                last = v.tensor_tensor_scan(run[:, e, :], cnt[:, :, e], zero64[:, :], 0.0, ALU.add, ALU.add)
            chain(last)
            chain(v.tensor_scalar(tiles_i[:, :], run[:, :, NT - 1], float(TILE - 1), None, ALU.add))
            chain(v.tensor_scalar(tiles_i[:, :], tiles_i[:, :], int(math.log2(TILE)), int(math.log2(TILE)),
                                  ALU.arith_shift_right, ALU.logical_shift_left))
            chain(v.tensor_copy(tiles_f[:, :], tiles_i[:, :]))
            chain(v.tensor_tensor_scan(ends[:, :], tiles_f[:, :], zero64[:, 0:E], 0.0, ALU.add, ALU.add))
            chain(v.tensor_tensor(starts[:, :], ends[:, :], tiles_f[:, :], ALU.subtract))
            chain(v.tensor_tensor(t1[:, :, :], run[:, :, :].rearrange("p e n -> p n e"), cnt[:, :, :], ALU.subtract))
            chain(v.tensor_tensor(t1[:, :, :].rearrange("p n e -> p (n e)"), t1[:, :, :].rearrange("p n e -> p (n e)"), ps_rank[:, :], ALU.add))
            chain(v.tensor_tensor(t1[:, :, :], t1[:, :, :], over_tokens(starts[:, :]), ALU.add))
            for j in range(2):
                chain(v.tensor_tensor(t2[:, :, :], t1[:, :, :], hot[:, j, :, :], ALU.mult))
                chain(v.tensor_reduce(pick[:, j, :], t2[:, :, :], AX.X, ALU.add))
            v.tensor_copy(k.place[:, :, :], pick[:, :, :].rearrange("p s n -> p n s"))
            chain(v.tensor_tensor(ge[:, :, :], k.tile_start[:, :].unsqueeze(2).to_broadcast([1, PT_TILES, E]),
                                  starts[0:1, :].unsqueeze(1).to_broadcast([1, PT_TILES, E]), ALU.is_ge))
            chain(v.tensor_reduce(te_f[:, :], ge[:, :, :], AX.X, ALU.add))
            v.memset(k.tile_expert[:, 0:2], -1)
            v.tensor_scalar(k.tile_expert[:, 2:PT_TILES + 2], te_f[:, :], -1.0, None, ALU.add)
            v.wait_ge(root_ready, 1)
            chain(v.tensor_tensor(u[:, :, :], root[:, :, :], best[:, :, :], ALU.subtract))
            chain(v.reciprocal(u[:, :, :], u[:, :, :]))
            chain(v.tensor_tensor(usum[:, :], u[:, 0, :], u[:, 1, :], ALU.add))
            chain(v.reciprocal(usum[:, :], usum[:, :]))
            for j in range(2):
                v.tensor_tensor(k.pair_weight[:, j, :], u[:, j, :], usum[:, :], ALU.mult)
            v.wait_ge(idx_tposed, 1)
            chain(v.tensor_copy(k.idx_col[:, :], ps_idx[0:SL, :]))
            v.tensor_scalar(k.causal_off[:, :], k.idx_col[:, :], 0.5, BIG, ALU.add, ALU.mult)


def attend(nc, k, a):
    with ExitStack() as stack:
        s = Space(nc, stack, "attend")
        idx_row = s.sb("idx_row", [P, 2, NS])
        q_hi = s.sb("q_hi", [P, 2, TC, D], F32R)
        q_lo = s.sb("q_lo", [P, 2, TC, D], F32R)
        v_b = s.sb("v_b", [P, 2, TC, D])
        pick = s.sb("pick_slots", [P, 2, TC, NS], F32R)
        q_sel = s.sb("q_sel", [P, 2, NS])
        masked = s.sb("masked", [SL, 2, NG, T])
        probs = s.sb("probs", [SL, 2, NG, T])
        mx = s.sb("mx", [SL, 2, NG])
        nmx = s.sb("nmx", [SL, 2, NG])
        den = s.sb("den", [SL, 2, NG])
        rden = s.sb("rden", [SL, 2, NG])
        p_t = s.sb("p_t", [P, 2, TC, NS])
        o_t = s.sb("o_t", [P, 2, NS])
        sel1 = s.sb("sel1", [SL, NG, HG * HD])
        sel2 = s.sb("sel2", [SL, NG, HG * HD])
        place_back = s.sb("place_back", [SL, 2, NG, T], F32R)
        at = s.sb("at", [P, 2, T])
        x_in = s.sb("x_again", [P, 2, TC, D])
        row_out = s.sb("row_out", [P, 2, TC, 2, XW])
        place_b = s.sb("place_b", [P, 2, TC, 2], U32)
        ps_q = s.ps("ps_q", [P, NS])
        ps_s = s.ps("ps_s", [SL, NG, T])
        ps_p = s.ps("ps_p", [P, TC, 512])
        ps_v = s.ps("ps_v", [P, NS])
        ps_o = s.ps("ps_o", [SL, 512])
        own_o = ps_o[:, :].rearrange("p (g w) -> p g w", g=NG)[:, :, 0:HG * HD]
        ps_a = s.ps("ps_a", [P, 2, T])
        ps_at = ps_a[:, 0, :]
        ps_out = ps_a[:, 1, :]
        idx_loaded, x_loaded, rows_loaded, rows_sent = ([s.sem(f"{n}{i}") for i in range(2)] for n in (
            "idx_loaded", "x_loaded", "rows_loaded", "rows_sent"))
        (q_hi_made, v_staged, q_lo_made, pick_made, q_gathered, q_masked, scored, s_masked, maxed, exped, p_tposed,
         p_copied, valued, o_copied, o_tposed, sel_made, placed, at_copied, out_made, based, back_made,
         max_links, norm_links, ids_staged) = (s.sem(n) for n in (
            "q_hi_made", "v_staged", "q_lo_made", "pick_made", "q_gathered", "q_masked", "scored", "s_masked", "maxed",
            "exped", "p_tposed", "p_copied", "valued", "o_copied", "o_tposed", "sel_made", "placed", "at_copied",
            "out_made", "based", "back_made", "max_links", "norm_links", "ids_staged"))
        block = stack.enter_context(nc.Block())
        x_d = a["x"].rearrange("b (c p) d -> p b c d", p=P)
        xn_d = k.xn_dram[:, :].rearrange("(b c p) d -> p b c d", p=P, c=TC)
        idx_d = k.idx_dram[:, :].rearrange("(b h) r -> b (h r)", h=H)

        def batches(eng, step):
            turns = B // 2
            for off in range(2):
                step(Nth(0, off, 2, B))
            with eng.Fori(1, turns - 1) as it:
                for off in range(2):
                    step(Nth(it, off, 2, B))
            for off in range(2):
                step(Nth(turns - 1, off, 2, B))

        @block.sync
        def _(sp):
            def load_x(b):
                i = b.mod(2)
                b.wait(sp, based, lag=2)
                sp.dma_start(x_in[:, i, :, :], x_d[:, ds(b.n, 1), :, :].rearrange("p b c d -> p (b c) d")
                             ).then_inc(x_loaded[i], 16)

            def step(b):
                i = b.mod(2)
                b.wait(sp, pick_made, lag=2)
                sp.dma_start(idx_row[:, i, :], idx_d[ds(b.n, 1), :].to_broadcast([P, NS])).then_inc(idx_loaded[i], 16)
                b.wait(sp, rows_sent[i], lag=2, each=64, ring=2)
                for j in range(2):
                    sp.dma_start(row_out[:, i, :, j, 0:D], xn_d[:, ds(b.n, 1), :, :].rearrange("p b c d -> p (b c) d")
                                 ).then_inc(rows_loaded[i], 16)
                if b.plus(-1).exists:
                    load_x(b.plus(-1))
            batches(sp, step)
            load_x(Nth(B // 2 - 1, 1, 2, B))

        @block.gpsimd
        def _(g):
            def low_half(b):
                i = b.mod(2)
                b.wait(g, q_gathered, lag=2)
                b.wait_alone(g, q_hi_made, k.carried_g)
                g.tensor_tensor(q_lo[:, i, :, :], k.q_of(b), q_hi[:, i, :, :].bitcast(F32), ALU.subtract).then_inc(q_lo_made, 1)

            def scatter(b):
                i = b.mod(2)
                b.wait(g, rows_sent[i], lag=2, each=64, ring=2)
                g.tensor_copy(place_b[:, i, :, :], k.place[:, ds(b.n * 2, 2), :]).then_inc(ids_staged, 1)
                g.tensor_copy(row_out[:, i, :, :, D].bitcast(U32), k.token_id[:, ds(b.n * 2, 2), :]).then_inc(ids_staged, 1)
                b.wait(g, rows_loaded[i], each=32, ring=2)
                b.wait_alone(g, ids_staged, k.carried_g, each=2)
                for c in range(TC):
                    for j in range(2):
                        g.indirect_dma_start(out=k.rows_dram[:, :], in_=row_out[:, i, c, j, :], in_offset=None,
                                             out_offset=bass.IndirectOffsetOnAxis(ap=place_b[:, i, c, j:j + 1], axis=0)
                                             ).then_inc(rows_sent[i], 16)

            low_half(Nth(0, 0, 2, B))
            low_half(Nth(0, 1, 2, B))

            def step(b):
                scatter(b)
                if b.plus(2).exists:
                    low_half(b.plus(2))

            batches(g, step)
            for i in range(2):
                g.wait_ge(rows_sent[i], 64 * (B // 2))

        @block.vector
        def _(v):
            max_link = Links(v, max_links, 1, k.carried_v)
            norm_link = Links(v, norm_links, 4, k.carried_v)

            def select(b):
                i = b.mod(2)
                b.wait(v, idx_loaded[i], each=16, ring=2)
                b.wait(v, q_gathered, lag=2)
                for c in range(TC):
                    last = v.tensor_scalar(pick[:, i, c, :], idx_row[:, i, :], k.token_in_batch[:, c:c + 1], None, ALU.is_equal)
                last.then_inc(pick_made, 1)

            def mask_q(b):
                i = b.mod(2)
                b.wait(v, q_gathered)
                b.wait(v, scored, lag=2, each=2)
                v.tensor_tensor(q_sel[:, i, :], ps_q[:, :], k.head_mask[:, :, :, :].rearrange("p g j r -> p (g j r)"),
                                ALU.mult).then_inc(q_masked, 1)

            def maxes(b):
                i = b.mod(2)
                b.wait(v, exped, lag=2)
                for g in range(NG):
                    if g % 2 == 0:
                        b.wait(v, scored, each=2, part=g // 2)
                    last = v.scalar_tensor_tensor(masked[:, i, g, :], k.causal_ramp[0:SL, :], k.causal_off[:, ds(b.n * NG + g, 1)],
                                                  ps_s[:, g, :], ALU.add, ALU.min)
                last.then_inc(s_masked, 1)
                b.wait(v, s_masked)
                max_link.at(b)
                max_link(v.tensor_reduce(mx[:, i, :], masked[:, i, :, :], AX.X, ALU.max))
                v.tensor_scalar(nmx[:, i, :], mx[:, i, :], -SCALE, None, ALU.mult).then_inc(maxed, 1)

            def back(b):
                i = b.mod(2)
                b.wait(v, placed, lag=2)
                for g in range(NG):
                    last = v.tensor_scalar(place_back[:, i, g, :], k.token_row[0:SL, :], k.idx_col[:, ds(b.n * NG + g, 1)],
                                           None, ALU.is_equal)
                last.then_inc(back_made, 1)

            def normalise(b):
                i = b.mod(2)
                norm_link.at(b)
                b.wait(v, exped)
                norm_link(v.reciprocal(rden[:, i, :], den[:, i, :]))
                b.wait(v, o_tposed)
                norm_link(v.tensor_tensor(sel1[:, :, :], own_o, rden[:, i, :].unsqueeze(2).to_broadcast([SL, NG, HG * HD]), ALU.mult))
                norm_link(v.tensor_tensor(sel2[:, :, :], sel1[:, :, :], k.slot_mask[:, :, :].rearrange("p j d -> p (j d)").unsqueeze(1)
                                          .to_broadcast([SL, NG, HG * HD]), ALU.mult))
                b.wait(v, placed, lag=1)
                norm_link(v.tensor_copy(k.own(k.sel_hi), sel2[:, :, :]))
                v.tensor_tensor(k.own(k.sel_lo), sel2[:, :, :], k.own(k.sel_hi).bitcast(F32), ALU.subtract).then_inc(sel_made, 1)

            def base(b):
                i = b.mod(2)
                b.wait(v, x_loaded[i], each=16, ring=2)
                b.wait(v, out_made)
                v.tensor_tensor(k.q_of(b), ps_out.rearrange("p (c d) -> p c d", d=D), x_in[:, i, :, :], ALU.add).then_inc(based, 1)

            select(Nth(0, 0, 2, B))
            mask_q(Nth(0, 0, 2, B))
            select(Nth(0, 1, 2, B))
            maxes(Nth(0, 0, 2, B))

            def step(b):
                if b.plus(1).exists:
                    mask_q(b.plus(1))
                back(b)
                if b.plus(1).exists:
                    maxes(b.plus(1))
                if b.plus(2).exists:
                    select(b.plus(2))
                normalise(b)
                if b.plus(-1).exists:
                    base(b.plus(-1))

            batches(v, step)
            base(Nth(B // 2 - 1, 1, 2, B))

        @block.scalar
        def _(act):
            def stage(b):
                i = b.mod(2)
                b.wait(act, q_lo_made, lag=2)
                b.wait(act, q_gathered, lag=2)
                act.activation(q_hi[:, i, :, :], k.q_of(b), ACT.Copy).then_inc(q_hi_made, 1)
                b.wait(act, valued, lag=2)
                act.activation(v_b[:, i, :, :], k.qvg[:, ds(b.n * 2, 2), D:2 * D], ACT.Copy).then_inc(v_staged, 1)

            def exps(b, groups):
                i = b.mod(2)
                b.wait(act, maxed)
                b.wait(act, p_tposed, lag=2)
                for g in groups:
                    last = act.activation(probs[:, i, g, :], masked[:, i, g, :], ACT.Exp, bias=nmx[:, i, g:g + 1], scale=SCALE,
                                          accum_out=den[:, i, g:g + 1])
                if groups[-1] == NG - 1:
                    last.then_inc(exped, 1)

            def attention(b):
                b.wait(act, placed)
                act.activation(at[:, b.mod(2), :], ps_at, ACT.Copy).then_inc(at_copied, 1)

            stage(Nth(0, 0, 2, B))
            stage(Nth(0, 1, 2, B))
            exps(Nth(0, 0, 2, B), range(NG))

            def step(b):
                i = b.mod(2)
                b.wait(act, p_tposed)
                act.activation(p_t[:, i, :, :], ps_p[:, :, 0:NS], ACT.Copy).then_inc(p_copied, 1)
                b.wait(act, valued)
                act.activation(o_t[:, i, :], ps_v[:, :], ACT.Copy).then_inc(o_copied, 1)
                if b.plus(1).exists:
                    exps(b.plus(1), range(0, 2))
                if b.plus(-1).exists:
                    attention(b.plus(-1))
                if b.plus(1).exists:
                    exps(b.plus(1), range(2, NG))
                if b.plus(2).exists:
                    stage(b.plus(2))

            batches(act, step)
            attention(Nth(B // 2 - 1, 1, 2, B))

        @block.tensor
        def _(pe):
            def gather(b):
                i = b.mod(2)
                b.wait(pe, q_lo_made)
                b.wait(pe, pick_made)
                b.wait(pe, q_masked, lag=1)
                for n, half in enumerate((q_hi, q_lo)):
                    for c in range(TC):
                        last = pe.matmul(ps_q[:, :], half[:, i, c, :], pick[:, i, c, :], start=(n + c == 0), stop=(n + c == TC))
                last.then_inc(q_gathered, 1)

            def scores(b):
                i = b.mod(2)
                b.wait(pe, q_masked)
                b.wait(pe, s_masked, lag=1)
                for g in range(NG):
                    last = pe.matmul(ps_s[:, g, :], q_sel[:, i, g * SL:(g + 1) * SL], k.k_t[:, ds(b.n * T, T)],
                                     start=True, stop=True)
                    if g % 2:
                        last.then_inc(scored, 1)

            def turn(b):
                i = b.mod(2)
                b.wait(pe, exped)
                b.wait(pe, p_copied, lag=1)
                for g in range(NG):
                    for c in range(TC):
                        last = pe.transpose(ps_p[:, c, g * SL:(g + 1) * SL], probs[:, i, g, c * P:(c + 1) * P], k.ident[0:SL, 0:SL])
                last.then_inc(p_tposed, 1)

            def values(b):
                i = b.mod(2)
                b.wait(pe, v_staged)
                b.wait(pe, p_copied)
                b.wait(pe, o_copied, lag=1)
                for c in range(TC):
                    last = pe.matmul(ps_v[:, :], v_b[:, i, c, :], p_t[:, i, c, :], start=(c == 0), stop=(c == TC - 1))
                last.then_inc(valued, 1)

            def turn_back(b):
                i = b.mod(2)
                b.wait(pe, o_copied)
                b.wait(pe, sel_made, lag=1)
                for g in range(NG):
                    last = pe.transpose(ps_o[:, 96 * g:96 * g + P], o_t[:, i, g * SL:(g + 1) * SL], k.ident[:, :])
                last.then_inc(o_tposed, 1)

            def place(b):
                i = b.mod(2)
                b.wait(pe, sel_made)
                b.wait(pe, back_made)
                b.wait(pe, based, lag=1)
                for n, half in enumerate((k.sel_hi, k.sel_lo)):
                    for g in range(NG):
                        last = pe.matmul(ps_at, half[:, g * P:(g + 1) * P], place_back[:, i, g, :],
                                         start=(n + g == 0), stop=(n == 1 and g == NG - 1))
                last.then_inc(placed, 1)

            def output(b):
                i = b.mod(2)
                b.wait(pe, at_copied)
                for c in range(TC):
                    part = ps_out[:, c * P:(c + 1) * P]
                    pe.matmul(part, k.ones_bf[0:3, :], k.bias3[:, BO0:NBR], start=True, stop=False)
                    last = pe.matmul(part, at[:, i, c * P:(c + 1) * P], k.wo[:, :], start=False, stop=True)
                last.then_inc(out_made, 1)

            gather(Nth(0, 0, 2, B))
            scores(Nth(0, 0, 2, B))

            def step(b):
                if b.plus(1).exists:
                    gather(b.plus(1))
                turn(b)
                if b.plus(1).exists:
                    scores(b.plus(1))
                values(b)
                if b.plus(-1).exists:
                    place(b.plus(-1))
                turn_back(b)
                if b.plus(-1).exists:
                    output(b.plus(-1))

            batches(pe, step)
            place(Nth(B // 2 - 1, 1, 2, B))
            output(Nth(B // 2 - 1, 1, 2, B))


def experts(nc, k, a):
    RING = 4
    with ExitStack() as stack:
        s = Space(nc, stack, "experts")
        rows = s.sb("rows", [P, RING, 2, XW])
        dest = s.sb("dest", [P, RING, 2], U32)
        w1 = s.sb("w1", [P, 2, 2, F], F32R)
        w2 = s.sb("w2", [P, 2, 2, FC, D], F32R)
        bias = s.sb("bias", [P, 2, FC + 1])
        x_hi = s.sb("x_hi", [P, 2, TILE], F32R)
        x_lo = s.sb("x_lo", [P, 2, TILE], F32R)
        h = s.sb("h", [P, 2, FC, TILE])
        h_hi = s.sb("h_hi", [P, 2, FC, TILE], F32R)
        h_lo = s.sb("h_lo", [P, 2, FC, TILE], F32R)
        y_t = s.sb("y_t", [P, 2, TILE])
        y_rows = s.sb("y_rows", [P, RING, 2, D])
        ps_x = s.ps("ps_x", [P, TILE])
        ps_h = [s.ps(f"ps_h{i}", [P, FC, TILE]) for i in range(2)]
        ps_y = s.ps("ps_y", [P, TILE])
        ps_r = s.ps("ps_r", [P, 2, D])
        rows_loaded = [s.sem(f"rows_loaded{i}") for i in range(RING)]
        scattered = [s.sem(f"scattered{i}") for i in range(RING)]
        w_loaded = [s.sem(f"w_loaded{i}") for i in range(2)]
        b_loaded = [s.sem(f"b_loaded{i}") for i in range(2)]
        x_tposed, x_hi_made, x_made, upped, gelued, h_hi_made, h_made, downed, y_made, y_tposed, y_copied = (s.sem(n) for n in (
            "x_tposed", "x_hi_made", "x_made", "upped", "gelued", "h_hi_made", "h_made", "downed", "y_made", "y_tposed",
            "y_copied"))
        block = stack.enter_context(nc.Block())
        rows_d = k.rows_dram[:, :].rearrange("(t h p) c -> p t h c", h=2, p=P)
        w1_d = k.w_dram[0:2, :].rearrange("a (e d f) -> d e a f", e=E, d=D)
        w2_d = k.w_dram[2:4, :].rearrange("a (e c p d) -> a p e c d", e=E, c=FC, p=P)

        def tiles(eng, step):
            turns = PT_TILES // RING
            for off in range(RING):
                step(Nth(0, off, RING, PT_TILES))
            with eng.Fori(1, turns - 1) as it:
                for off in range(RING):
                    step(Nth(it, off, RING, PT_TILES))
            for off in range(RING):
                step(Nth(turns - 1, off, RING, PT_TILES))

        first = Nth(0, 0, RING, PT_TILES)
        last_tile = Nth(PT_TILES // RING - 1, RING - 1, RING, PT_TILES)

        @block.sync
        def _(sp):
            def step(j):
                r, i = j.mod(RING), j.mod(2)
                j.wait(sp, y_copied, lag=RING)
                sp.dma_start(rows[:, r, :, :], rows_d[:, ds(j.n, 1), :, :].rearrange("p t h c -> p (t h) c")
                             ).then_inc(rows_loaded[r], 16)
                e = sp.value_load(k.tile_expert[:, ds(j.n + 2, 1)], min_val=0, max_val=E - 1)
                before = sp.value_load(k.tile_expert[:, ds(j.n, 1)], min_val=-1, max_val=E - 1)
                j.wait_alone(sp, y_made, k.carried_s, lag=2)
                with sp.If(e != before):
                    sp.dma_start(w1[:, i, :, :].bitcast(F32), w1_d[:, ds(e, 1), :, :].rearrange("d e a f -> d (e a) f")
                                 ).then_inc(w_loaded[i], 16)
                    for n in range(2):
                        sp.dma_start(w2[:, i, n, :, :].bitcast(F32),
                                     w2_d[n, :, ds(e, 1), :, :].rearrange("p e c d -> p (e c) d")).then_inc(w_loaded[i], 16)
                    sp.dma_start(bias[:, i, :], k.b_cols[:, ds(e * (FC + 1), FC + 1)]).then_inc(b_loaded[i], 16)
                with sp.Else():
                    sp.sem_inc(w_loaded[i], 48)
                    sp.sem_inc(b_loaded[i], 16)
            tiles(sp, step)

        @block.gpsimd
        def _(g):
            bound = g.snap(2 * NTOK - 1)

            def step(j):
                r = j.mod(RING)
                j.wait_alone(g, y_copied, k.carried_g)
                for h_ in range(2):
                    g.indirect_dma_start(out=k.y_dram[:, :], out_offset=bass.IndirectOffsetOnAxis(ap=dest[:, r, h_:h_ + 1], axis=0),
                                         in_=y_rows[:, r, h_, :], in_offset=None,
                                         bounds_check=bound, oob_is_err=False).then_inc(scattered[r], 16)
            tiles(g, step)
            for r in range(RING):
                g.wait_ge(scattered[r], 32 * (PT_TILES // RING))

        @block.tensor
        def _(pe):
            def turn_in(j):
                r = j.mod(RING)
                j.wait(pe, rows_loaded[r], each=16, ring=RING)
                j.wait(pe, x_made, lag=1)
                for h_ in range(2):
                    last = pe.transpose(ps_x[:, h_ * P:(h_ + 1) * P], rows[:, r, h_, 0:D], k.ident[:, :])
                last.then_inc(x_tposed, 1)

            def three(out, w_hi, w_lo, m_hi, m_lo, start, stop):
                pe.matmul(out, w_hi, m_hi, start=start, stop=False)
                pe.matmul(out, w_hi, m_lo, start=False, stop=False)
                return pe.matmul(out, w_lo, m_hi, start=False, stop=stop)

            def up(j):
                i = j.mod(2)
                j.wait(pe, x_made)
                j.wait(pe, w_loaded[i], each=48, ring=2)
                for c in range(FC):
                    if c % 2 == 0:
                        j.wait(pe, gelued, lag=2, each=2, part=c // 2)
                    col = slice(c * P, (c + 1) * P)
                    last = three(ps_h[i][:, c, :], w1[:, i, 0, col], w1[:, i, 1, col],
                                 x_hi[:, i, :], x_lo[:, i, :], True, True)
                    if c % 2:
                        last.then_inc(upped, 1)

            def down(j):
                i = j.mod(2)
                j.wait(pe, y_made, lag=1)
                for c in range(FC):
                    if c % 2 == 0:
                        j.wait(pe, h_made, each=2, part=c // 2)
                    last = three(ps_y[:, :], w2[:, i, 0, c, :], w2[:, i, 1, c, :],
                                 h_hi[:, i, c, :], h_lo[:, i, c, :], c == 0, c == FC - 1)
                last.then_inc(downed, 1)

            def turn_out(j):
                i = j.mod(2)
                j.wait(pe, y_made)
                j.wait(pe, y_copied, lag=1)
                for h_ in range(2):
                    last = pe.transpose(ps_r[:, h_, :], y_t[:, i, h_ * P:(h_ + 1) * P], k.ident[:, :])
                last.then_inc(y_tposed, 1)

            turn_in(first)

            def step(j):
                up(j)
                if j.plus(1).exists:
                    turn_in(j.plus(1))
                if j.plus(-1).exists:
                    down(j.plus(-1))
                if j.plus(-2).exists:
                    turn_out(j.plus(-2))

            tiles(pe, step)
            down(last_tile)
            turn_out(last_tile.plus(-1))
            turn_out(last_tile)

        @block.scalar
        def _(act):
            def step(j):
                i = j.mod(2)
                j.wait(act, b_loaded[i], each=16, ring=2)
                for half in range(2):
                    part = slice(2 * half, 2 * half + 2)
                    j.wait(act, upped, each=2, part=half)
                    j.wait(act, h_made, lag=2, each=2, part=half)
                    for c in range(2 * half, 2 * half + 2):
                        last = act.activation(h[:, i, c, :], ps_h[i][:, c, :], ACT.Gelu, bias=bias[:, i, c:c + 1])
                    last.then_inc(gelued, 1)
                    j.wait(act, gelued, each=2, part=half)
                    j.wait(act, downed, lag=2)
                    act.activation(h_hi[:, i, part, :], h[:, i, part, :], ACT.Copy).then_inc(h_hi_made, 1)
            tiles(act, step)

        @block.vector
        def _(v):
            def x_split(j):
                i = j.mod(2)
                j.wait(v, x_tposed)
                j.wait(v, upped, lag=2, each=2)
                v.tensor_copy(x_hi[:, i, :], ps_x[:, :]).then_inc(x_hi_made, 1)
                j.wait(v, x_hi_made)
                v.tensor_tensor(x_lo[:, i, :], ps_x[:, :], x_hi[:, i, :].bitcast(F32), ALU.subtract).then_inc(x_made, 1)

            def h_low(j):
                i = j.mod(2)
                for half in range(2):
                    part = slice(2 * half, 2 * half + 2)
                    j.wait(v, h_hi_made, each=2, part=half)
                    if half == 0:
                        j.wait(v, downed, lag=2)
                    v.tensor_tensor(h_lo[:, i, part, :], h[:, i, part, :], h_hi[:, i, part, :].bitcast(F32),
                                    ALU.subtract).then_inc(h_made, 1)

            def y_add(j):
                i = j.mod(2)
                j.wait(v, downed)
                j.wait(v, b_loaded[i], each=16, ring=2)
                j.wait(v, y_tposed, lag=2)
                v.tensor_scalar(y_t[:, i, :], ps_y[:, :], bias[:, i, FC:FC + 1], None, ALU.add).then_inc(y_made, 1)

            def y_copy(j):
                r = j.mod(RING)
                j.wait(v, y_tposed)
                j.wait(v, scattered[r], lag=RING, each=32, ring=RING)
                v.tensor_copy(dest[:, r, :], rows[:, r, :, D].bitcast(U32))
                v.tensor_copy(y_rows[:, r, :, :], ps_r[:, :, :]).then_inc(y_copied, 1)

            x_split(first)

            def step(j):
                if j.plus(1).exists:
                    x_split(j.plus(1))
                if j.plus(-1).exists:
                    y_add(j.plus(-1))
                h_low(j)
                if j.plus(-2).exists:
                    y_copy(j.plus(-2))

            tiles(v, step)
            y_add(last_tile)
            y_copy(last_tile.plus(-1))
            y_copy(last_tile)


def combine(nc, k, out):
    N = 4
    turns = NT // N // 2
    with ExitStack() as stack:
        s = Space(nc, stack, "combine")
        y = s.sb("y", [P, 2, 2, N, D])
        part = s.sb("part", [P, 2, N, D])
        res = s.sb("res", [P, 2, N, D])
        loaded = [s.sem(f"loaded{i}") for i in range(2)]
        stored = [s.sem(f"stored{i}") for i in range(2)]
        halfway, added = s.sem("halfway"), s.sem("added")
        block = stack.enter_context(nc.Block())
        y_d = k.y_dram[:, :].rearrange("(s n p) d -> p s n d", s=2, p=P)
        out_d = out.rearrange("b (c p) d -> p (b c) d", p=P)

        @block.sync
        def _(sp):
            def turn(it, first):
                for i in range(2):
                    if not first:
                        sp.wait_ge(added, it * 2 + (i - 1))
                    for j in range(2):
                        sp.dma_start(y[:, i, j, :, :], y_d[:, j, ds(it * (2 * N) + i * N, N), :]).then_inc(loaded[i], 16)
            turn(0, True)
            with sp.Fori(1, turns) as it:
                turn(it, False)

        @block.vector
        def _(v):
            def turn(it, first):
                for i in range(2):
                    v.wait_ge(loaded[i], it * 32 + 32)
                    for n in range(N):
                        last = v.scalar_tensor_tensor(
                            part[:, i, n, :], y[:, i, 0, n, :], k.pair_weight[:, 0, ds(it * (2 * N) + (i * N + n), 1)],
                            k.qvg[:, ds(it * (2 * N) + (i * N + n), 1), 0:D].rearrange("p n d -> p (n d)"), ALU.mult, ALU.add)
                    last.then_inc(halfway, 1)
                    v.wait_ge(halfway, it * 2 + (i + 1))
                    if not first:
                        v.wait_ge(stored[i], it * 16)
                    for n in range(N):
                        last = v.scalar_tensor_tensor(
                            res[:, i, n, :], y[:, i, 1, n, :], k.pair_weight[:, 1, ds(it * (2 * N) + (i * N + n), 1)],
                            part[:, i, n, :], ALU.mult, ALU.add)
                    last.then_inc(added, 1)
            turn(0, True)
            with v.Fori(1, turns) as it:
                turn(it, False)

        @block.scalar
        def _(act):
            with act.Fori(0, turns) as it:
                for i in range(2):
                    act.wait_ge(added, it * 2 + (i + 1))
                    act.dma_start(out_d[:, ds(it * (2 * N) + i * N, N), :], res[:, i, :, :]).then_inc(stored[i], 16)
            for i in range(2):
                act.wait_ge(stored[i], 16 * turns)


class Kept:

    def __init__(self, nc, s):
        self.w_proj = s.sb("w_proj", [D, NP])
        self.wk = s.sb("wk", [D, D])
        self.wo = s.sb("wo", [D, D])
        self.b_cols = s.sb("b_cols", [P, NB1 + 2])
        self.bias3 = s.sb("bias3", [3, NBR], BF16)
        self.ident = s.sb("ident", [P, P])
        self.before = s.sb("before", [P, P], BF16)
        self.ones_bf = s.sb("ones_bf", [P, P], BF16)
        self.head_mask = s.sb("head_mask", [P, NG, HG, TOP_Q])
        self.slot_mask = s.sb("slot_mask", [SL, HG, HD])
        self.expert_id = s.sb("expert_id", [P, E])
        self.tile_start = s.sb("tile_start", [1, PT_TILES])
        self.token_id = s.sb("token_id", [P, NT, 2], I32)
        self.token_in_batch = s.sb("token_in_batch", [P, TC])
        self.token_row = s.sb("token_row", [P, T])
        self.causal_ramp = s.sb("causal_ramp", [P, T])
        self.unused = s.sb("unused", [P, 8, XW])
        self.pow_mhalf = s.sb("pow_mhalf", [P, NT])
        self.pow_half = s.sb("pow_half", [P, 2 * NT])
        self.cent_sq = s.sb("cent_sq", [P, E])
        self.qvg = s.sb("qvg", [P, NT, KEEP])
        self.k_t = s.sb("k_t", [P, B * T])
        self.q_norm = s.sb("q_norm", [P, TC, B, H])
        self.norm_sq = s.sb("norm_sq", [P, NT])
        self.place = s.sb("place", [P, NT, 2], U32)
        self.tile_expert = s.sb("tile_expert", [1, PT_TILES + 2], I32)
        self.pair_weight = s.sb("pair_weight", [P, 2, NT])
        self.idx_col = s.sb("idx_col", [SL, P])
        self.causal_off = s.sb("causal_off", [SL, P])
        self.sel_hi = s.sb("sel_hi", [SL, NG * (P + 32)], F32R)
        self.sel_lo = s.sb("sel_lo", [SL, NG * (P + 32)], F32R)
        self.carried_v, self.carried_g, self.carried_s = s.sem("carried_v"), s.sem("carried_g"), s.sem("carried_s")
        self.xn_dram = nc.dram_tensor("xn_scratch", (NTOK, D), F32).ap()
        self.y_dram = nc.dram_tensor("y_scratch", (2 * NTOK, D), F32).ap()
        self.rows_dram = nc.dram_tensor("rows_scratch", (LIST, XW), F32).ap()
        self.w_dram = nc.dram_tensor("w_scratch", (4, E * D * F), F32).ap()
        self.idx_dram = nc.dram_tensor("idx_scratch", (B * H, TOP_Q), F32).ap()

    def q_of(self, b):
        return self.qvg[:, ds(b.n * TC, TC), 0:D]

    def own(self, sel):
        return sel[:, :].rearrange("p (g w) -> p g w", w=P + 32)[:, :, 0:32]


def program(nc, a, out):
    with ExitStack() as stack:
        k = Kept(nc, Space(nc, stack, "kept"))
        prepare(nc, k, a)
        project(nc, k, a)
        route(nc, k)
        attend(nc, k, a)
        experts(nc, k, a)
        combine(nc, k, out)


_INS = ["L0_attn_x", "L0_attn_Wq", "L0_attn_bq", "L0_attn_Wk", "L0_attn_bk", "L0_attn_Wv", "L0_attn_bv", "L0_attn_Wo",
        "L0_attn_bo", "L0_ffn_centroids", "L0_ffn_Wp", "L0_ffn_bp", "L0_ffn_W1", "L0_ffn_b1", "L0_ffn_W2", "L0_ffn_b2"]


def kernel(**inputs):
    import numpy as _np
    import concourse.bacc as _bacc
    from concourse.bass_utils import run_bass_kernel_spmd as _run

    nc = _bacc.Bacc("TRN2", target_bir_lowering=False, num_devices=1)
    arrays, args = {}, {}
    for name in _INS:
        x = _np.ascontiguousarray(inputs[name])
        arrays[f"in_{name}"] = x
        args[name.split("_")[-1]] = nc.dram_tensor(f"in_{name}", x.shape, mybir.dt.from_np(x.dtype), kind="ExternalInput").ap()
    out = nc.dram_tensor("out_0", (B, T, D), F32, kind="ExternalOutput").ap()
    program(nc, args, out)
    r = _run(nc, [arrays], core_ids=[0])
    return r.results[0]["out_0"]
```

```python
import concourse.bass as bass
from concourse import mybir
from contextlib import ExitStack
import math

F32 = mybir.dt.float32
F32R = mybir.dt.float32r
BF16 = mybir.dt.bfloat16
I32 = mybir.dt.int32
U32 = mybir.dt.uint32
ALU = mybir.AluOpType
ACT = mybir.ActivationFunctionType
AX = mybir.AxisListType

P = 128
B, T, D = 32, 256, 128
H, HD = 16, 8
TOP_Q = min(int(5 * math.log(T)), T)
E, F = 8, 512
LN_EPS, EPS, MAX_NORM, MAX_SQ = 1e-5, 1e-7, 0.95, 0.99
TC = T // P
NT = B * TC
NTOK = B * T
HG = 4
NG = H // HG
SL = HG * TOP_Q
NS = H * TOP_Q
GB = P // H
QB = B // GB
FC = F // P
TILE = 256
PT_TILES = 2 * NTOK // TILE + E
LIST = PT_TILES * TILE
XW = D + 1
NOWHERE = 1 << 20
SCALE = HD ** -0.5
BC = 8
WM = 4 * F + BC
WSLOTS = 3
INIT = 9
BIG = 1e30
G0 = 2 * D
X0 = G0 + E
NP = X0 + D
KEEP = X0
BO0 = NP
NBR = NP + D
NB1 = E * (FC + 1)
assert B == E * FC


class Chain:

    def __init__(self, eng, sem):
        self.eng, self.sem, self.n = eng, sem, 0

    def __call__(self, ins):
        self.n += 1
        ins.then_inc(self.sem, 1)
        self.eng.wait_ge(self.sem, self.n)


class Nth:

    def __init__(self, it, off, size, count):
        self.it, self.off, self.size, self.count = it, off, size, count
        self.n = it * size + off
        self.known = isinstance(it, int)

    def plus(self, m):
        return Nth(self.it, self.off + m, self.size, self.count)

    @property
    def exists(self):
        return not self.known or 0 <= self.n < self.count

    def mod(self, m):
        assert self.size % m == 0
        return self.off % m

    def after(self, lag):
        return not self.known or self.n >= lag

    def upto(self, lag=0, each=1, part=None, ring=1):
        off = self.off - lag
        within = each if part is None else part + 1
        return self.it * (self.size // ring * each) + (off // ring * each + within)

    def carry(self, eng, carried):
        if not self.known:
            eng.sem_inc(carried, 1)


class Space:

    def __init__(self, nc, stack, stage):
        self.nc, self.stack, self.stage = nc, stack, stage

    def sb(self, name, shape, dt=F32):
        return self.stack.enter_context(self.nc.sbuf_tensor(f"{self.stage}_{name}", shape, dt))

    def ps(self, name, shape, dt=F32):
        return self.stack.enter_context(self.nc.psum_tensor(f"{self.stage}_{name}", shape, dt))

    def sem(self, name):
        return self.stack.enter_context(self.nc.semaphore(f"{self.stage}_{name}"))


def ds(start, size):
    return bass.ds(start, size)


def prepare(nc, k, early, a):
    with ExitStack() as stack:
        s = Space(nc, stack, "prepare")
        cent = s.sb("cent", [E, D])
        cent_sq = s.sb("cent_sq", [E, D])
        cn = s.sb("cn", [E, 4])
        mhalf = s.sb("mhalf", [P, 1])
        wp_t = s.sb("wp_t", [D, D])
        c_t = s.sb("c_t", [D, E])
        c_tsq = s.sb("c_tsq", [D, E])
        bias_rows = s.sb("bias_rows", [NB1 + 2, P])
        ones_f = s.sb("ones_f", [P, P])
        row = s.sb("row", [1, NBR])
        rest = s.sb("rest", [1, NBR])
        parts = s.sb("parts", [1, 3, NBR], BF16)
        ramp_i = s.sb("ramp_i", [P, T], I32)
        ps_wt = s.ps("ps_wt", [P, P])
        ps_ct = s.ps("ps_ct", [P, E])
        ps_m = s.ps("ps_m", [P, 3, E])
        ps_b = s.ps("ps_b", [P, NB1 + 2])
        loaded, consts, chain_v, chain_g = s.sem("loaded"), s.sem("consts"), s.sem("chain_v"), s.sem("chain_g")
        cn_ready, cscale_ready, cproj_ready = s.sem("cn_ready"), s.sem("cscale_ready"), s.sem("cproj_ready")
        tposed, t_copied, products, parts_ready, parts_moved = (s.sem(n) for n in (
            "tposed", "t_copied", "products", "parts_ready", "parts_moved"))
        block = stack.enter_context(nc.Block())
        loads = [
            (cent[:, :], a["centroids"]), (k.w_proj[:, X0:NP], a["Wp"]), (k.w_proj[:, 0:D], a["Wq"]),
            (k.w_proj[:, D:2 * D], a["Wv"]), (k.wk[:, :], a["Wk"]), (k.wo[:, :], a["Wo"]),
            (bias_rows[NB1:NB1 + 1, :], a["bk"].rearrange("(o d) -> o d", o=1)),
            (bias_rows[NB1 + 1:NB1 + 2, :], a["bp"].rearrange("(o d) -> o d", o=1)),
            (row[:, 0:D], a["bq"].rearrange("(o d) -> o d", o=1)),
            (row[:, D:2 * D], a["bv"].rearrange("(o d) -> o d", o=1)),
            (row[:, X0:NP], a["bp"].rearrange("(o d) -> o d", o=1)),
            (row[:, BO0:NBR], a["bo"].rearrange("(o d) -> o d", o=1)),
        ]
        loads.append((bias_rows[0:E * FC, :], a["b1"].rearrange("e (c p) -> (e c) p", p=P)))
        loads.append((bias_rows[E * FC:NB1, :], a["b2"]))

        @block.sync
        def _(sp):
            for dst, src in loads:
                sp.dma_start(dst, src).then_inc(loaded, 16)
            for j in range(2):
                early.load(sp, Nth(0, j, 2, B // 2))
            sp.wait_ge(loaded, 16 * len(loads))
            sp.wait_ge(parts_ready, 1)
            for j in range(3):
                sp.dma_start(k.bias3[j:j + 1, :], parts[:, j, :]).then_inc(parts_moved, 16)
            sp.wait_ge(parts_moved, 48)

        @block.gpsimd
        def _(g):
            chain = Chain(g, chain_g)
            g.memset(k.expert_bias[:, :, FC + 1:BC], 0.0)
            g.memset(mhalf[:, :], -0.5)
            g.memset(k.pow_mhalf[:, :], -0.5)
            g.memset(k.pow_half[:, :], 0.5)
            g.memset(ones_f[:, :], 1.0)
            g.memset(k.ident[:, :], 0.0)
            g.memset(k.head_mask[:, :, :, :], SCALE)
            g.memset(k.slot_mask[:, :, :], 1.0)
            g.memset(k.minus_rest[:, :], -1.0)
            g.memset(k.ones_bf[:, :], 1.0)
            g.iota(ramp_i[:, :], pattern=[[1, T]], base=0, channel_multiplier=0)
            g.iota(k.expert_id[:, :], pattern=[[1, E]], base=0, channel_multiplier=0,
                   allow_small_or_imprecise_dtypes=True)
            g.iota(k.tile_start[:, :], pattern=[[TILE, PT_TILES]], base=0, channel_multiplier=0,
                   allow_small_or_imprecise_dtypes=True)
            g.iota(k.token_id[:, :, :], pattern=[[P, NT], [NTOK, 2]], base=0, channel_multiplier=1)
            g.iota(k.token_in_batch[:, :], pattern=[[P, TC]], base=0, channel_multiplier=1,
                   allow_small_or_imprecise_dtypes=True)
            g.memset(k.unused[:, :, 0:D], 0.0)
            chain(g.iota(k.unused[:, :, D].bitcast(I32), pattern=[[0, INIT]], base=NOWHERE, channel_multiplier=0))
            g.tensor_copy(k.token_row[:, :], ramp_i[:, :])
            g.tensor_scalar(k.causal_ramp[:, :], ramp_i[:, :], -BIG, None, ALU.mult)
            g.affine_select(out=k.ident[:, :], in_=k.ident[:, :], compare_op=ALU.not_equal, fill=1.0,
                            base=0, pattern=[[-1, P]], channel_multiplier=1)
            g.affine_select(out=k.minus_rest[:, :], in_=k.minus_rest[:, :], compare_op=ALU.is_ge, fill=0.0,
                            base=0, pattern=[[-1, P]], channel_multiplier=1)
            g.affine_select(out=k.head_mask[:, :, :, :], in_=k.head_mask[:, :, :, :], compare_op=ALU.is_ge, fill=0.0,
                            base=0, pattern=[[-HD * HG, NG], [-HD, HG], [0, TOP_Q]], channel_multiplier=1)
            chain(g.affine_select(out=k.slot_mask[:, :, :], in_=k.slot_mask[:, :, :], compare_op=ALU.is_ge, fill=0.0,
                                  base=0, pattern=[[-TOP_Q, HG], [0, HD]], channel_multiplier=1))
            g.affine_select(out=k.head_mask[:, :, :, :], in_=k.head_mask[:, :, :, :], compare_op=ALU.is_ge, fill=0.0,
                            base=HD - 1, pattern=[[HD * HG, NG], [HD, HG], [0, TOP_Q]], channel_multiplier=-1)
            g.affine_select(out=k.slot_mask[:, :, :], in_=k.slot_mask[:, :, :], compare_op=ALU.is_ge, fill=0.0,
                            base=TOP_Q - 1, pattern=[[TOP_Q, HG], [0, HD]], channel_multiplier=-1).then_inc(consts, 1)
            g.wait_ge(cn_ready, 1)
            g.tensor_tensor(cn[:, 2:3], cn[:, 1:2], mhalf[0:E, :], ALU.pow).then_inc(cscale_ready, 1)

        @block.vector
        def _(v):
            chain = Chain(v, chain_v)
            v.wait_ge(loaded, 16 * len(loads))
            chain(v.tensor_tensor(cent_sq[:, :], cent[:, :], cent[:, :], ALU.mult))
            chain(v.tensor_reduce(cn[:, 0:1], cent_sq[:, :], AX.X, ALU.add))
            v.tensor_scalar(cn[:, 1:2], cn[:, 0:1], EPS * EPS, None, ALU.max).then_inc(cn_ready, 1)
            v.wait_ge(cscale_ready, 1)
            chain(v.tensor_scalar(cn[:, 3:4], cn[:, 2:3], MAX_NORM, 1.0, ALU.mult, ALU.min))
            v.tensor_scalar(cent_sq[:, :], cent[:, :], cn[:, 3:4], None, ALU.mult).then_inc(cproj_ready, 1)
            v.wait_ge(tposed, 1)
            v.tensor_copy(wp_t[:, :], ps_wt[:, :])
            v.tensor_copy(k.expert_bias[:, :, 0:FC], ps_b[:, 0:E * FC].rearrange("p (e c) -> p e c", c=FC))
            v.tensor_copy(k.expert_bias[:, :, FC], ps_b[:, E * FC:NB1])
            v.tensor_copy(k.b_cols[:, :], ps_b[:, NB1:NB1 + 2])
            chain(v.tensor_copy(c_t[:, :], ps_ct[:, :]))
            v.tensor_tensor(c_tsq[:, :], c_t[:, :], c_t[:, :], ALU.mult).then_inc(t_copied, 1)
            v.wait_ge(products, 1)
            v.tensor_copy(k.w_proj[:, G0:X0], ps_m[:, 0, :])
            v.tensor_scalar(k.cent_sq[:, :], ps_m[:, 1, :], MAX_SQ, None, ALU.min)
            chain(v.tensor_copy(row[:, G0:X0], ps_m[0:1, 2, :]))
            chain(v.tensor_copy(parts[:, 0, :], row[:, :]))
            chain(v.tensor_tensor(rest[:, :], row[:, :], parts[:, 0, :], ALU.subtract))
            chain(v.tensor_copy(parts[:, 1, :], rest[:, :]))
            chain(v.tensor_tensor(rest[:, :], rest[:, :], parts[:, 1, :], ALU.subtract))
            v.tensor_copy(parts[:, 2, :], rest[:, :]).then_inc(parts_ready, 1)
            v.memset(k.sel_hi[:, :].bitcast(U32), 0)
            v.memset(k.sel_lo[:, :].bitcast(U32), 0)

        @block.tensor
        def _(pe):
            pe.wait_ge(consts, 1)
            pe.wait_ge(loaded, 16 * len(loads))
            pe.wait_ge(cproj_ready, 1)
            pe.transpose(ps_wt[:, :], k.w_proj[:, X0:NP], k.ident[:, :])
            pe.transpose(ps_b[:, :], bias_rows[:, :], k.ident[0:NB1 + 2, 0:NB1 + 2])
            pe.transpose(ps_ct[:, :], cent_sq[:, :], k.ident[0:E, 0:E]).then_inc(tposed, 1)
            pe.wait_ge(t_copied, 1)
            pe.matmul(ps_m[:, 0, :], wp_t[:, :], c_t[:, :], start=True, stop=True)
            pe.matmul(ps_m[:, 1, :], ones_f[:, :], c_tsq[:, :], start=True, stop=True)
            pe.matmul(ps_m[0:1, 2, :], k.b_cols[:, 1:2], c_t[:, :], start=True, stop=True).then_inc(products, 1)


class Early:

    def __init__(self, nc, s, a):
        self.x_in = s.sb("x_in", [P, 2, 2, TC, D])
        self.x_loaded = [s.sem(f"x_loaded{i}") for i in range(2)]
        self.x_d = a["x"].rearrange("(w b) (c p) d -> p w (b c) d", p=P, b=2)

    def load(self, eng, pair):
        i = pair.mod(2)
        eng.dma_start(self.x_in[:, i, :, :, :].rearrange("p b c d -> p (b c) d"),
                      self.x_d[:, ds(pair.n, 1), :, :].rearrange("p w c d -> p (w c) d")).then_inc(self.x_loaded[i], 16)


def project(nc, k, early, a):
    XR = 4
    with ExitStack() as stack:
        s = Space(nc, stack, "project")
        xn = s.sb("xn", [P, XR, TC, D])
        xn_t = s.sb("xn_t", [P, 2, T])
        stats = s.sb("stats", [P, 2, TC, 6])
        mv = s.sb("mv", [P, XR, TC, 2])
        var = s.sb("var", [P, 2, TC])
        rstd = s.sb("rstd", [P, 2, TC])
        sq = s.sb("sq", [P, 2, TC, D])
        w_raw = s.sb("w_raw", [P, 2, 2, 2 * P])
        w_split = s.sb("w_split", [P, 2, 2, 2, 2 * P], F32R)
        ps_xt = [s.ps(f"ps_xt{i}", [P, T]) for i in range(2)]
        ps_pr = [s.ps(f"ps_pr{i}", [P, TC, 512]) for i in range(2)]
        ps_k = [s.ps(f"ps_k{i}", [P, T]) for i in range(2)]
        xn_stored, w_loaded, w_stored = ([s.sem(f"{n}{i}") for i in range(2)] for n in ("xn_stored", "w_loaded", "w_stored"))
        (bias_stored, w_hi_made, w_made, stats_made, aggregated, var_ready, rstd_ready, xn_made, x_tposed, xt_copied,
         projected, kept) = (s.sem(n) for n in (
            "bias_stored", "w_hi_made", "w_made", "stats_made", "aggregated", "var_ready", "rstd_ready", "xn_made",
            "x_tposed", "xt_copied", "projected", "kept"))
        block = stack.enter_context(nc.Block())
        x_in, x_loaded = early.x_in, early.x_loaded
        xn_d = k.xn_dram[:, :].rearrange("(w c p) d -> p w c d", p=P, c=2 * TC)
        w1_d = a["W1"].rearrange("e d (u c f) -> d e u c f", u=2, c=2)
        w2_d = a["W2"].rearrange("e (u c f) d -> f e u c d", u=2, c=2)
        ws_d = k.w_dram[:, 0:4 * F].rearrange("(e p) (q u f) -> p e q u f", p=P, q=4, u=2)
        assert B // 2 == E * 2 and FC == 4
        turns = B // XR
        first, last_batch = Nth(0, 0, XR, B), Nth(turns - 1, XR - 1, XR, B)

        def pair_of(b):
            return Nth(b.it, b.off // 2, 2, B // 2)

        def batches(eng, step):
            for off in range(XR):
                step(Nth(0, off, XR, B))
            with eng.Fori(1, turns - 1) as it:
                for off in range(XR):
                    step(Nth(it, off, XR, B))
            for off in range(XR):
                step(Nth(turns - 1, off, XR, B))

        @block.sync
        def _(sp):
            def load_w(w):
                i = w.mod(2)
                if w.after(2):
                    sp.wait_ge(w_made, w.upto(lag=2))
                for n, w_d in enumerate((w1_d, w2_d)):
                    sp.dma_start(w_raw[:, i, n, :].rearrange("p (c f) -> p c f", c=2),
                                 w_d[:, ds(w.it + w.off // 2, 1), w.mod(2), :, :].rearrange("p e c f -> p (e c) f")
                                 ).then_inc(w_loaded[i], 16)

            def store_w(w):
                i = w.mod(2)
                sp.wait_ge(w_made, w.upto())
                sp.dma_start(ws_d[:, ds(w.it + w.off // 2, 1), :, w.mod(2), :].rearrange("p e q f -> p (e q) f"),
                             w_split[:, i, :, :, :].rearrange("p n a m -> p (n a) m").bitcast(F32)).then_inc(w_stored[i], 16)

            sp.dma_start(k.w_dram[:, 4 * F:WM].rearrange("(e p) m -> p e m", p=P), k.expert_bias[:, :, :]).then_inc(bias_stored, 16)
            load_w(pair_of(first))

            def step(w):
                i = w.mod(2)
                sp.wait_ge(xn_made, w.upto(each=2))
                sp.dma_start(xn_d[:, ds(w.n, 1), :, :].rearrange("p w c d -> p (w c) d"),
                             xn[:, 2 * i:2 * i + 2, :, :].rearrange("p b c d -> p (b c) d")).then_inc(xn_stored[i], 16)
                if w.plus(2).exists:
                    early.load(sp, w.plus(2))
                if w.after(1):
                    store_w(w.plus(-1))
                if w.plus(1).exists:
                    load_w(w.plus(1))

            for off in range(2):
                step(Nth(0, off, 2, B // 2))
            with sp.Fori(1, turns - 1) as it:
                for off in range(2):
                    step(Nth(it, off, 2, B // 2))
            for off in range(2):
                step(Nth(turns - 1, off, 2, B // 2))
            store_w(pair_of(last_batch))
            sp.wait_ge(bias_stored, 16)
            for i in range(2):
                sp.wait_ge(xn_stored[i], 16 * (B // 4))
                sp.wait_ge(w_stored[i], 16 * (B // 4))

        @block.gpsimd
        def _(g):
            def root(b):
                i = b.mod(2)
                g.wait_ge(var_ready, b.upto())
                b.carry(g, k.carried_g)
                if b.after(2):
                    g.wait_ge(xn_made, b.upto(lag=2))
                g.tensor_tensor(rstd[:, i, :], var[:, i, :], k.pow_mhalf[:, 0:TC], ALU.pow).then_inc(rstd_ready, 1)

            for j in range(3):
                root(first.plus(j))

            def step(b):
                if b.plus(3).exists:
                    root(b.plus(3))
                if b.mod(2) == 0:
                    w = pair_of(b)
                    i = w.mod(2)
                    g.wait_ge(w_hi_made, w.upto())
                    w.carry(g, k.carried_g)
                    if w.after(2):
                        g.wait_ge(w_stored[i], w.upto(lag=2, each=16, ring=2))
                    g.tensor_tensor(w_split[:, i, :, 1, :], w_raw[:, i, :, :], w_split[:, i, :, 0, :].bitcast(F32), ALU.subtract
                                    ).then_inc(w_made, 1)

            batches(g, step)

        @block.vector
        def _(v):
            def moments(b):
                i, x = b.mod(2), b.mod(XR)
                v.wait_ge(x_loaded[x // 2], pair_of(b).upto(each=16, ring=2))
                for c in range(TC):
                    last = v.bn_stats(stats[:, i, c, :], x_in[:, x // 2, x % 2, c, :])
                last.then_inc(stats_made, 1)
                v.wait_ge(stats_made, b.upto())
                b.carry(v, k.carried_v)
                for c in range(TC):
                    last = v.bn_aggr(mv[:, x, c, :], stats[:, i, c, :])
                last.then_inc(aggregated, 1)
                v.wait_ge(aggregated, b.upto())
                v.tensor_scalar(var[:, i, :], mv[:, x, :, 1], LN_EPS, None, ALU.add).then_inc(var_ready, 1)

            def norm(b):
                i, x = b.mod(2), b.mod(XR)
                if b.after(XR):
                    v.wait_ge(xn_stored[x // 2], pair_of(b).upto(lag=2, each=16, ring=2))
                    v.wait_ge(x_tposed, b.upto(lag=XR))
                v.wait_ge(rstd_ready, b.upto())
                for c in range(TC):
                    last = v.tensor_scalar(xn[:, x, c, :], x_in[:, x // 2, x % 2, c, :], mv[:, x, c, 0:1], rstd[:, i, c:c + 1],
                                           ALU.subtract, ALU.mult)
                last.then_inc(xn_made, 1)

            def sums(b):
                v.wait_ge(kept, b.upto())
                v.tensor_reduce(k.q_norm[:, :, ds(b.n, 1), :].rearrange("p c b h -> p (c b) h"),
                                k.q_of(b).rearrange("p c (h d) -> p c h d", d=HD), AX.X, ALU.add, apply_absolute_value=True)

            moments(first)
            for j in range(2):
                moments(first.plus(j + 1))
                norm(first.plus(j))

            def step(b):
                if b.plus(2).exists:
                    norm(b.plus(2))
                if b.plus(3).exists:
                    moments(b.plus(3))
                if b.plus(-2).exists:
                    sums(b.plus(-2))

            batches(v, step)
            sums(last_batch.plus(-1))
            sums(last_batch)

        @block.tensor
        def _(pe):
            def turn(b):
                i = b.mod(2)
                pe.wait_ge(xn_made, b.upto())
                if b.after(2):
                    pe.wait_ge(xt_copied, b.upto(lag=2))
                for c in range(TC):
                    last = pe.transpose(ps_xt[i][:, c * P:(c + 1) * P], xn[:, b.mod(XR), c, :], k.ident[:, :])
                last.then_inc(x_tposed, 1)

            turn(first)

            def step(b):
                i = b.mod(2)
                if b.plus(1).exists:
                    turn(b.plus(1))
                pe.wait_ge(xt_copied, b.upto())
                if b.after(2):
                    pe.wait_ge(kept, b.upto(lag=2))
                for c in range(TC):
                    pe.matmul(ps_pr[i][:, c, 0:NP], k.ones_bf[0:3, :], k.bias3[:, 0:NP], start=True, stop=False)
                    pe.matmul(ps_pr[i][:, c, 0:NP], xn_t[:, i, c * P:(c + 1) * P], k.w_proj[:, :], start=False, stop=True)
                pe.matmul(ps_k[i][:, :], k.wk[:, :], xn_t[:, i, :], start=True, stop=True).then_inc(projected, 1)

            batches(pe, step)

        @block.scalar
        def _(act):
            def copy_xt(b):
                i = b.mod(2)
                act.wait_ge(x_tposed, b.upto())
                if b.after(2):
                    act.wait_ge(projected, b.upto(lag=2))
                act.activation(xn_t[:, i, :], ps_xt[i][:, :], ACT.Copy).then_inc(xt_copied, 1)

            copy_xt(first)

            def step(b):
                i = b.mod(2)
                if b.plus(1).exists:
                    copy_xt(b.plus(1))
                if i == 0:
                    w = pair_of(b)
                    act.wait_ge(w_loaded[w.mod(2)], w.upto(each=32, ring=2))
                    if w.after(2):
                        act.wait_ge(w_stored[w.mod(2)], w.upto(lag=2, each=16, ring=2))
                    act.activation(w_split[:, w.mod(2), :, 0, :], w_raw[:, w.mod(2), :, :], ACT.Copy).then_inc(w_hi_made, 1)
                act.wait_ge(projected, b.upto())
                act.activation(k.qvg[:, ds(b.n * TC, TC), :], ps_pr[i][:, :, 0:KEEP], ACT.Copy)
                act.activation(k.k_t[:, ds(b.n * T, T)], ps_k[i][:, :], ACT.Identity, bias=k.b_cols[:, 0:1])
                for c in range(TC):
                    last = act.activation(sq[:, i, c, :], ps_pr[i][:, c, X0:NP], ACT.Square,
                                          accum_out=k.norm_sq[:, ds(b.n * TC + c, 1)])
                last.then_inc(kept, 1)

            batches(act, step)


def route(nc, k):
    with ExitStack() as stack:
        s = Space(nc, stack, "route")
        qn_t = s.sb("qn_t", [P, QB, T])
        top8 = s.sb("top8", [P, QB, 8])
        idx_u = s.sb("idx_u", [P, QB, 32], U32)
        idx_f = s.sb("idx_f", [P, QB, TOP_Q])
        idx_rows = s.sb("idx_rows", [P, SL])
        n2 = s.sb("n2", [P, NT])
        xs = s.sb("xs", [P, NT])
        xsq = s.sb("xsq", [P, NT])
        omx = s.sb("omx", [P, NT])
        omc = s.sb("omc", [P, E])
        t1 = s.sb("t1", [P, NT, E])
        t2 = s.sb("t2", [P, NT, E])
        dist = s.sb("dist", [P, NT, E])
        a_plus = s.sb("a_plus", [P, 2, NT])
        pick = s.sb("pick", [P, 2, NT])
        hot = s.sb("hot", [P, 2, NT, E])
        both = s.sb("both", [P, NT, E], BF16)
        run = s.sb("run", [P, E, NT])
        zero64 = s.sb("zero64", [P, NT])
        tiles_i = s.sb("tiles_i", [P, E], I32)
        tiles_f = s.sb("tiles_f", [P, E])
        ends = s.sb("ends", [P, E])
        ps_qn = s.ps("ps_qn", [P, QB, T])
        ps_idx = s.ps("ps_idx", [P, P])
        ps_rank = s.ps("ps_rank", [P, NT * E])
        ps_cnt = s.ps("ps_cnt", [P, NT * E])
        total = s.sb("total", [P, E])
        rows_inited, qn_tposed, qn_copied, idx_made, idx_stored, idx_loaded, idx_tposed, chain_v = (s.sem(n) for n in (
            "rows_inited", "qn_tposed", "qn_copied", "idx_made", "idx_stored", "idx_loaded", "idx_tposed", "chain_v"))
        n2_ready, xs_ready, both_ready, ranked = (s.sem(n) for n in ("n2_ready", "xs_ready", "both_ready", "ranked"))
        block = stack.enter_context(nc.Block())

        rows_d = k.rows_dram[:, :].rearrange("(t p n) c -> p t (n c)", p=P, n=INIT)
        shares = LIST // P // INIT

        @block.sync
        def _(sp):
            for t in range(shares):
                sp.dma_start(rows_d[:, t, :], k.unused[:, :, :].rearrange("p n c -> p (n c)")).then_inc(rows_inited, 16)
            sp.wait_ge(idx_made, 1)
            sp.dma_start(k.idx_dram[:, :].rearrange("(g p) r -> p g r", p=P), idx_f[:, :, :]).then_inc(idx_stored, 16)
            sp.wait_ge(idx_stored, 16)
            sp.dma_start(idx_rows[:, :], k.idx_dram[:, :].rearrange("(n j) r -> n (j r)", j=HG)).then_inc(idx_loaded, 16)
            sp.wait_ge(idx_loaded, 16)
            sp.wait_ge(rows_inited, 16 * shares)

        @block.tensor
        def _(pe):
            for g in range(QB):
                for c in range(TC):
                    last = pe.transpose(ps_qn[:, g, c * P:(c + 1) * P],
                                        k.q_norm[:, c, g * GB:(g + 1) * GB, :].rearrange("p b h -> p (b h)"), k.ident[:, :])
            last.then_inc(qn_tposed, 1)
            pe.wait_ge(both_ready, 1)
            pair_mask = both[:, :, :].rearrange("p n e -> p (n e)")
            pe.matmul(ps_rank[:, :], k.minus_rest[:, :], pair_mask, start=True, stop=True)
            pe.matmul(ps_cnt[:, :], k.ones_bf[:, :], pair_mask, start=True, stop=True).then_inc(ranked, 1)
            pe.wait_ge(idx_loaded, 16)
            pe.transpose(ps_idx[0:SL, :], idx_rows[:, :], k.ident[:, :]).then_inc(idx_tposed, 1)

        @block.scalar
        def _(act):
            act.wait_ge(qn_tposed, 1)
            act.activation(qn_t[:, :, :], ps_qn[:, :, :], ACT.Copy).then_inc(qn_copied, 1)

        @block.gpsimd
        def _(g):
            g.wait_ge(n2_ready, 1)
            g.tensor_tensor(xs[:, :], n2[:, :], k.pow_mhalf[:, 0:NT], ALU.pow).then_inc(xs_ready, 1)

        @block.vector
        def _(v):
            chain = Chain(v, chain_v)
            dots = k.qvg[:, :, G0:X0]

            def over_experts(ap):
                return ap.unsqueeze(2).to_broadcast([P, NT, E])

            def over_tokens(ap):
                return ap.unsqueeze(1).to_broadcast([P, NT, E])

            v.tensor_scalar(n2[:, :], k.norm_sq[:, :], EPS * EPS, None, ALU.max).then_inc(n2_ready, 1)
            v.wait_ge(qn_copied, 1)
            for r in range(0, TOP_Q, 8):
                for g in range(QB):
                    last = v.max(top8[:, g, :], qn_t[:, g, :])
                chain(last)
                for g in range(QB):
                    last = v.max_index(idx_u[:, g, r:r + 8], top8[:, g, :], qn_t[:, g, :])
                chain(last)
                if r + 8 < TOP_Q:
                    for g in range(QB):
                        last = v.match_replace(qn_t[:, g, :], top8[:, g, :], qn_t[:, g, :], -1.0)
                    chain(last)
            v.tensor_copy(idx_f[:, :, :], idx_u[:, :, 0:TOP_Q]).then_inc(idx_made, 1)
            v.wait_ge(xs_ready, 1)
            chain(v.tensor_scalar(xs[:, :], xs[:, :], MAX_NORM, 1.0, ALU.mult, ALU.min))
            chain(v.tensor_tensor(xsq[:, :], xs[:, :], xs[:, :], ALU.mult))
            chain(v.tensor_tensor(xsq[:, :], xsq[:, :], k.norm_sq[:, :], ALU.mult))
            chain(v.tensor_scalar(xsq[:, :], xsq[:, :], MAX_SQ, None, ALU.min))
            v.tensor_scalar(omx[:, :], xsq[:, :], -1.0, 1.0, ALU.mult, ALU.add)
            v.tensor_scalar(omc[:, :], k.cent_sq[:, :], -1.0, 1.0, ALU.mult, ALU.add)
            v.tensor_tensor(t2[:, :, :], over_experts(xsq[:, :]), over_tokens(k.cent_sq[:, :]), ALU.add)
            chain(v.tensor_tensor(t1[:, :, :], dots, over_experts(xs[:, :]), ALU.mult))
            chain(v.scalar_tensor_tensor(t2[:, :, :], t1[:, :, :], -2.0, t2[:, :, :], ALU.mult, ALU.add))
            v.tensor_scalar(t2[:, :, :], t2[:, :, :], 0.0, 2.0, ALU.max, ALU.mult)
            chain(v.tensor_tensor(t1[:, :, :], over_experts(omx[:, :]), over_tokens(omc[:, :]), ALU.mult))
            chain(v.tensor_scalar(t1[:, :, :], t1[:, :, :], EPS, None, ALU.add))
            chain(v.reciprocal(t1[:, :, :], t1[:, :, :]))
            chain(v.tensor_tensor(t1[:, :, :], t1[:, :, :], t2[:, :, :], ALU.mult))
            chain(v.tensor_scalar(dist[:, :, :], t1[:, :, :], 1.0, 1.0 + EPS, ALU.add, ALU.max))
            for j in range(2):
                chain(v.tensor_reduce(k.arg[:, j, :], dist[:, :, :], AX.X, ALU.min))
                chain(v.tensor_tensor(t2[:, :, :], dist[:, :, :], over_experts(k.arg[:, j, :]), ALU.is_equal))
                chain(v.scalar_tensor_tensor(t2[:, :, :], t2[:, :, :], -float(E), over_tokens(k.expert_id[:, :]), ALU.mult, ALU.add))
                chain(v.tensor_reduce(pick[:, j, :], t2[:, :, :], AX.X, ALU.min))
                chain(v.tensor_tensor(hot[:, j, :, :], t2[:, :, :], over_experts(pick[:, j, :]), ALU.is_equal))
                if j == 0:
                    chain(v.scalar_tensor_tensor(dist[:, :, :], hot[:, 0, :, :], BIG, dist[:, :, :], ALU.mult, ALU.add))
            v.tensor_tensor(both[:, :, :], hot[:, 0, :, :], hot[:, 1, :, :], ALU.add).then_inc(both_ready, 1)
            v.tensor_scalar(k.rad[:, :, :], k.arg[:, :, :], -1.0, None, ALU.add)
            v.memset(zero64[:, :], 0.0)
            chain(v.tensor_scalar(a_plus[:, :, :], k.arg[:, :, :], 1.0, None, ALU.add))
            v.tensor_tensor(k.rad[:, :, :], k.rad[:, :, :], a_plus[:, :, :], ALU.mult)
            v.wait_ge(ranked, 1)
            counts = ps_cnt[:, :].rearrange("p (n e) -> p e n", e=E)
            chain(v.tensor_reduce(total[:, :], counts, AX.X, ALU.add))
            chain(v.tensor_scalar(tiles_i[:, :], total[:, :], float(TILE - 1), None, ALU.add))
            chain(v.tensor_scalar(tiles_i[:, :], tiles_i[:, :], int(math.log2(TILE)), int(math.log2(TILE)),
                                  ALU.arith_shift_right, ALU.logical_shift_left))
            chain(v.tensor_copy(tiles_f[:, :], tiles_i[:, :]))
            chain(v.tensor_tensor_scan(ends[:, :], tiles_f[:, :], zero64[:, 0:E], 0.0, ALU.add, ALU.add))
            chain(v.tensor_tensor(k.starts[:, :], ends[:, :], tiles_f[:, :], ALU.subtract))
            for e in range(E):
                last = v.tensor_tensor_scan(run[:, e, :], counts[:, e, :], zero64[:, :], k.starts[:, e:e + 1], ALU.add, ALU.add)
            chain(last)
            chain(v.tensor_tensor(t1[:, :, :],
                                  run[:, :, :].rearrange("p e n -> p n e"),
                                  ps_rank[:, :].rearrange("p (n e) -> p n e", e=E), ALU.add))
            for j in range(2):
                chain(v.tensor_tensor(t2[:, :, :], t1[:, :, :], hot[:, j, :, :], ALU.mult))
                chain(v.tensor_reduce(pick[:, j, :], t2[:, :, :], AX.X, ALU.add))
            v.tensor_copy(k.place[:, :, :], pick[:, :, :].rearrange("p s n -> p n s"))
            v.wait_ge(idx_tposed, 1)
            chain(v.tensor_copy(k.idx_col[:, :], ps_idx[0:SL, :]))
            v.tensor_scalar(k.minus_idx[:, :], k.idx_col[:, :], -1.0, None, ALU.mult)
            v.tensor_scalar(k.causal_off[:, :], k.idx_col[:, :], 0.5, BIG, ALU.add, ALU.mult)


def attend(nc, k, a):
    with ExitStack() as stack:
        s = Space(nc, stack, "attend")
        idx_row = s.sb("idx_row", [P, 2, NS])
        q_hi = s.sb("q_hi", [P, 2, TC, D], F32R)
        q_lo = s.sb("q_lo", [P, 2, TC, D], F32R)
        pick = s.sb("pick_slots", [P, 2, TC, NS], F32R)
        q_sel = s.sb("q_sel", [P, 2, NS])
        masked = s.sb("masked", [SL, 2, NG, T])
        probs = s.sb("probs", [SL, 2, NG, T])
        minus_max = s.sb("minus_max", [SL, 2, NG])
        den = s.sb("den", [SL, 2, NG])
        rden = s.sb("rden", [SL, 2, NG])
        p_t = s.sb("p_t", [P, 2, TC, NS])
        sel1 = s.sb("sel1", [SL, NG, HG * HD])
        sel2 = s.sb("sel2", [SL, NG, HG * HD])
        place_back = s.sb("place_back", [SL, 2, NG, T], F32R)
        apart = s.sb("apart", [SL, 2, T])
        at = s.sb("at", [P, 2, T])
        x_in = s.sb("x_again", [P, 2, TC, D])
        started = s.sb("started", [1, PT_TILES, E])
        n_started = s.sb("n_started", [1, PT_TILES])
        row_out = s.sb("row_out", [P, 2, TC, 2, XW])
        place_b = s.sb("place_b", [P, 2, TC, 2], U32)
        ps_q = s.ps("ps_q", [P, NS])
        ps_s = s.ps("ps_s", [SL, NG, T])
        ps_p = s.ps("ps_p", [P, TC, 512])
        ps_o = s.ps("ps_o", [SL, NG, HG * HD])
        ps_at = s.ps("ps_at", [P, 512])[:, 0:T]
        ps_out = s.ps("ps_out", [P, 512])[:, 0:T]
        idx_loaded, x_loaded, rows_loaded, rows_sent = ([s.sem(f"{n}{i}") for i in range(2)] for n in (
            "idx_loaded", "x_loaded", "rows_loaded", "rows_sent"))
        (q_hi_made, q_lo_made, pick_made, q_gathered, q_masked, scored, s_masked, maxed, exped, p_tposed,
         p_copied, valued, sel_made, placed, at_copied, out_made, based, back_made,
         norm_links, ids_staged, tile_links, apart_made, back_too) = (s.sem(n) for n in (
            "q_hi_made", "q_lo_made", "pick_made", "q_gathered", "q_masked", "scored", "s_masked", "maxed",
            "exped", "p_tposed", "p_copied", "valued", "sel_made", "placed", "at_copied",
            "out_made", "based", "back_made", "norm_links", "ids_staged", "tile_links", "apart_made",
            "back_too"))
        block = stack.enter_context(nc.Block())
        x_d = a["x"].rearrange("b (c p) d -> p b c d", p=P)
        xn_d = k.xn_dram[:, :].rearrange("(b c p) d -> p b c d", p=P, c=TC)
        idx_d = k.idx_dram[:, :].rearrange("(b h) r -> b (h r)", h=H)

        SIZE = 4
        turns = B // SIZE
        first, last_batch = Nth(0, 0, SIZE, B), Nth(turns - 1, SIZE - 1, SIZE, B)

        def batches(eng, step):
            for off in range(SIZE):
                step(Nth(0, off, SIZE, B))
            with eng.Fori(1, turns - 1) as it:
                for off in range(SIZE):
                    step(Nth(it, off, SIZE, B))
            for off in range(SIZE):
                step(Nth(turns - 1, off, SIZE, B))

        @block.sync
        def _(sp):
            def load_x(b):
                i = b.mod(2)
                if b.after(2):
                    sp.wait_ge(based, b.upto(lag=2))
                sp.dma_start(x_in[:, i, :, :], x_d[:, ds(b.n, 1), :, :].rearrange("p b c d -> p (b c) d")
                             ).then_inc(x_loaded[i], 16)

            def load_idx(b):
                i = b.mod(2)
                if b.after(2):
                    sp.wait_ge(pick_made, b.upto(lag=2))
                sp.dma_start(idx_row[:, i, :], idx_d[ds(b.n, 1), :].to_broadcast([P, NS])).then_inc(idx_loaded[i], 16)

            def load_rows(b):
                i = b.mod(2)
                if b.after(2):
                    sp.wait_ge(rows_sent[i], b.upto(lag=2, each=64, ring=2))
                for j in range(2):
                    sp.dma_start(row_out[:, i, :, j, 0:D], xn_d[:, ds(b.n, 1), :, :].rearrange("p b c d -> p (b c) d")
                                 ).then_inc(rows_loaded[i], 16)

            load_idx(first)
            load_idx(first.plus(1))
            load_rows(first)
            load_idx(first.plus(2))
            load_idx(first.plus(3))

            def step(b):
                if b.plus(4).exists:
                    load_idx(b.plus(4))
                load_x(b)
                if b.plus(1).exists:
                    load_rows(b.plus(1))
            batches(sp, step)

        @block.gpsimd
        def _(g):
            def low_half(b):
                i = b.mod(2)
                if b.after(2):
                    g.wait_ge(q_gathered, b.upto(lag=2))
                g.wait_ge(q_hi_made, b.upto())
                b.carry(g, k.carried_g)
                g.tensor_tensor(q_lo[:, i, :, :], k.q_of(b), q_hi[:, i, :, :].bitcast(F32), ALU.subtract).then_inc(q_lo_made, 1)

            def scatter(b):
                i = b.mod(2)
                if b.after(2):
                    g.wait_ge(rows_sent[i], b.upto(lag=2, each=64, ring=2))
                g.tensor_copy(place_b[:, i, :, :], k.place[:, ds(b.n * 2, 2), :]).then_inc(ids_staged, 1)
                g.tensor_copy(row_out[:, i, :, :, D].bitcast(U32), k.token_id[:, ds(b.n * 2, 2), :]).then_inc(ids_staged, 1)
                g.wait_ge(rows_loaded[i], b.upto(each=32, ring=2))
                g.wait_ge(ids_staged, b.upto(each=2))
                b.carry(g, k.carried_g)
                for c in range(TC):
                    for j in range(2):
                        g.indirect_dma_start(out=k.rows_dram[:, :], in_=row_out[:, i, c, j, :], in_offset=None,
                                             out_offset=bass.IndirectOffsetOnAxis(ap=place_b[:, i, c, j:j + 1], axis=0)
                                             ).then_inc(rows_sent[i], 16)

            for j in range(3):
                low_half(first.plus(j))

            def step(b):
                if b.plus(3).exists:
                    low_half(b.plus(3))
                scatter(b)

            batches(g, step)
            for i in range(2):
                g.wait_ge(rows_sent[i], 64 * (B // 2))

        @block.vector
        def _(v):
            def select(b, c):
                i = b.mod(2)
                if c == 0:
                    v.wait_ge(idx_loaded[i], b.upto(each=16, ring=2))
                    if b.after(2):
                        v.wait_ge(q_gathered, b.upto(lag=2))
                last = v.tensor_scalar(pick[:, i, c, :], idx_row[:, i, :], k.token_in_batch[:, c:c + 1], None, ALU.is_equal)
                if c == TC - 1:
                    last.then_inc(pick_made, 1)

            def mask_q(b):
                i = b.mod(2)
                v.wait_ge(q_gathered, b.upto())
                if b.after(2):
                    v.wait_ge(scored, b.upto(lag=2, each=2))
                v.tensor_tensor(q_sel[:, i, :], ps_q[:, :], k.head_mask[:, :, :, :].rearrange("p g j r -> p (g j r)"),
                                ALU.mult).then_inc(q_masked, 1)

            def maxes(b):
                i = b.mod(2)
                if b.after(2):
                    v.wait_ge(exped, b.upto(lag=2, each=2))
                for half in range(2):
                    v.wait_ge(scored, b.upto(each=2, part=half))
                    for g in (2 * half, 2 * half + 1):
                        last = v.scalar_tensor_tensor(masked[:, i, g, :], k.causal_ramp[0:SL, :], k.causal_off[:, ds(b.n * NG + g, 1)],
                                                      ps_s[:, g, :], ALU.add, ALU.min)
                    last.then_inc(s_masked, 1)
                    v.wait_ge(s_masked, b.upto(each=2, part=half))
                    v.tensor_reduce(minus_max[:, i, 2 * half:2 * half + 2], masked[:, i, 2 * half:2 * half + 2, :], AX.X, ALU.max,
                                    negate=True).then_inc(maxed, 1)

            def normalise(b):
                i = b.mod(2)

                def back(g):
                    return v.tensor_scalar(place_back[:, i, g, :], k.token_row[0:SL, :], k.idx_col[:, ds(b.n * NG + g, 1)],
                                           None, ALU.is_equal)

                if b.after(2):
                    v.wait_ge(placed, b.upto(lag=2))
                v.wait_ge(exped, b.upto(each=2))
                v.reciprocal(rden[:, i, :], den[:, i, :]).then_inc(norm_links, 1)
                if b.plus(3).exists:
                    select(b.plus(3), 0)
                v.wait_ge(norm_links, b.upto(each=4, part=0))
                b.carry(v, k.carried_v)
                v.wait_ge(valued, b.upto())
                v.tensor_tensor(sel1[:, :, :], ps_o[:, :, :], rden[:, i, :].unsqueeze(2).to_broadcast([SL, NG, HG * HD]), ALU.mult
                                ).then_inc(norm_links, 1)
                back(0)
                v.wait_ge(norm_links, b.upto(each=4, part=1))
                b.carry(v, k.carried_v)
                v.tensor_tensor(sel2[:, :, :], sel1[:, :, :], k.slot_mask[:, :, :].rearrange("p j d -> p (j d)").unsqueeze(1)
                                .to_broadcast([SL, NG, HG * HD]), ALU.mult).then_inc(norm_links, 1)
                back(1).then_inc(back_made, 1)
                v.wait_ge(norm_links, b.upto(each=4, part=2))
                b.carry(v, k.carried_v)
                if b.after(1):
                    v.wait_ge(placed, b.upto(lag=1))
                v.tensor_copy(k.own(k.sel_hi), sel2[:, :, :]).then_inc(norm_links, 1)
                if b.plus(3).exists:
                    select(b.plus(3), 1)
                v.wait_ge(norm_links, b.upto(each=4, part=3))
                b.carry(v, k.carried_v)
                v.tensor_tensor(k.own(k.sel_lo), sel2[:, :, :], k.own(k.sel_hi).bitcast(F32), ALU.subtract).then_inc(sel_made, 1)

            def base(b):
                i = b.mod(2)
                v.wait_ge(x_loaded[i], b.upto(each=16, ring=2))
                v.wait_ge(out_made, b.upto())
                v.tensor_tensor(k.q_of(b), ps_out.rearrange("p (c d) -> p c d", d=D), x_in[:, i, :, :], ALU.add).then_inc(based, 1)

            for j in range(2):
                select(first.plus(j), 0)
                select(first.plus(j), 1)
            tile_link = Chain(v, tile_links)
            tile_link(v.tensor_tensor(started[:, :, :], k.tile_start[:, :].unsqueeze(2).to_broadcast([1, PT_TILES, E]),
                                      k.starts[0:1, :].unsqueeze(1).to_broadcast([1, PT_TILES, E]), ALU.is_ge))
            tile_link(v.tensor_reduce(n_started[:, :], started[:, :, :], AX.X, ALU.add))
            v.memset(k.tile_expert[:, 0:WSLOTS], -1)
            v.tensor_scalar(k.tile_expert[:, WSLOTS:PT_TILES + WSLOTS], n_started[:, :], -1.0, None, ALU.add)
            mask_q(first)
            maxes(first)
            mask_q(first.plus(1))
            select(first.plus(2), 0)
            select(first.plus(2), 1)

            def step(b):
                if b.plus(1).exists:
                    maxes(b.plus(1))
                if b.plus(-2).exists:
                    base(b.plus(-2))
                if b.plus(2).exists:
                    mask_q(b.plus(2))
                normalise(b)

            batches(v, step)
            base(last_batch.plus(-1))
            base(last_batch)

        @block.scalar
        def _(act):
            def stage_q(b):
                i = b.mod(2)
                if b.after(2):
                    act.wait_ge(q_lo_made, b.upto(lag=2))
                if b.after(2):
                    act.wait_ge(q_gathered, b.upto(lag=2))
                act.activation(q_hi[:, i, :, :], k.q_of(b), ACT.Copy).then_inc(q_hi_made, 1)

            def back(b):
                i = b.mod(2)
                if b.after(2):
                    act.wait_ge(placed, b.upto(lag=2))
                for n in range(2):
                    last = act.activation(apart[:, n, :], k.token_row[0:SL, :], ACT.Abs,
                                          bias=k.minus_idx[:, ds(b.n * NG + 2 + n, 1)])
                last.then_inc(apart_made, 1)
                act.wait_ge(apart_made, b.upto())
                act.activation(place_back[:, i, 2:4, :], apart[:, :, :], ACT.Relu, bias=1.0, scale=-1.0).then_inc(back_too, 1)

            def exps(b, half):
                i = b.mod(2)
                act.wait_ge(maxed, b.upto(each=2, part=half))
                if half == 0:
                    if b.after(2):
                        act.wait_ge(p_tposed, b.upto(lag=2))
                for g in (2 * half, 2 * half + 1):
                    last = act.activation(probs[:, i, g, :], masked[:, i, g, :], ACT.Exp, bias=minus_max[:, i, g:g + 1],
                                          accum_out=den[:, i, g:g + 1])
                last.then_inc(exped, 1)

            def attention(b):
                act.wait_ge(placed, b.upto())
                if b.after(2):
                    act.wait_ge(out_made, b.upto(lag=2))
                act.activation(at[:, b.mod(2), :], ps_at, ACT.Copy).then_inc(at_copied, 1)

            for j in range(2):
                stage_q(first.plus(j))
            stage_q(first.plus(2))
            for half in range(2):
                exps(first, half)

            def step(b):
                i = b.mod(2)
                if b.plus(3).exists:
                    stage_q(b.plus(3))
                act.wait_ge(p_tposed, b.upto())
                act.activation(p_t[:, i, :, :], ps_p[:, :, 0:NS], ACT.Copy).then_inc(p_copied, 1)
                back(b)
                if b.plus(1).exists:
                    exps(b.plus(1), 0)
                if b.plus(-1).exists:
                    attention(b.plus(-1))
                if b.plus(1).exists:
                    exps(b.plus(1), 1)

            batches(act, step)
            attention(last_batch)

        @block.tensor
        def _(pe):
            def gather(b):
                i = b.mod(2)
                pe.wait_ge(q_lo_made, b.upto())
                pe.wait_ge(pick_made, b.upto())
                if b.after(1):
                    pe.wait_ge(q_masked, b.upto(lag=1))
                for n, half in enumerate((q_hi, q_lo)):
                    for c in range(TC):
                        last = pe.matmul(ps_q[:, :], half[:, i, c, :], pick[:, i, c, :], start=(n + c == 0), stop=(n + c == TC))
                last.then_inc(q_gathered, 1)

            def scores(b):
                i = b.mod(2)
                pe.wait_ge(q_masked, b.upto())
                for g in range(NG):
                    if g % 2 == 0:
                        if b.after(1):
                            pe.wait_ge(s_masked, b.upto(lag=1, each=2, part=g // 2))
                    last = pe.matmul(ps_s[:, g, :], q_sel[:, i, g * SL:(g + 1) * SL], k.k_t[:, ds(b.n * T, T)],
                                     start=True, stop=True)
                    if g % 2:
                        last.then_inc(scored, 1)

            def turn(b, half):
                i = b.mod(2)
                pe.wait_ge(exped, b.upto(each=2, part=half))
                if half == 0 and b.after(1):
                    pe.wait_ge(p_copied, b.upto(lag=1))
                for g in (2 * half, 2 * half + 1):
                    for c in range(TC):
                        last = pe.transpose(ps_p[:, c, g * SL:(g + 1) * SL], probs[:, i, g, c * P:(c + 1) * P], k.ident[0:SL, 0:SL])
                if half:
                    last.then_inc(p_tposed, 1)

            def values(b):
                i = b.mod(2)
                pe.wait_ge(p_copied, b.upto())
                if b.after(1):
                    pe.wait_ge(sel_made, b.upto(lag=1))
                for g in range(NG):
                    for c in range(TC):
                        own = k.qvg[:, ds(b.n * TC + c, 1), D + g * HG * HD:D + (g + 1) * HG * HD]
                        last = pe.matmul(ps_o[:, g, :], p_t[:, i, c, g * SL:(g + 1) * SL],
                                         own.rearrange("p o d -> p (o d)"), start=(c == 0), stop=(c == TC - 1))
                last.then_inc(valued, 1)

            def place(b):
                i = b.mod(2)
                pe.wait_ge(sel_made, b.upto())
                pe.wait_ge(back_made, b.upto())
                pe.wait_ge(back_too, b.upto())
                if b.after(1):
                    pe.wait_ge(at_copied, b.upto(lag=1))
                for n, half in enumerate((k.sel_hi, k.sel_lo)):
                    for g in range(NG):
                        last = pe.matmul(ps_at, half[:, g * P:(g + 1) * P], place_back[:, i, g, :],
                                         start=(n + g == 0), stop=(n == 1 and g == NG - 1))
                last.then_inc(placed, 1)

            def output(b):
                i = b.mod(2)
                pe.wait_ge(at_copied, b.upto())
                if b.after(1):
                    pe.wait_ge(based, b.upto(lag=1))
                for c in range(TC):
                    part = ps_out[:, c * P:(c + 1) * P]
                    pe.matmul(part, k.ones_bf[0:3, :], k.bias3[:, BO0:NBR], start=True, stop=False)
                    last = pe.matmul(part, at[:, i, c * P:(c + 1) * P], k.wo[:, :], start=False, stop=True)
                last.then_inc(out_made, 1)

            gather(first)
            scores(first)
            gather(first.plus(1))

            turn(first, 0)

            def step(b):
                turn(b, 1)
                if b.plus(1).exists:
                    scores(b.plus(1))
                values(b)
                if b.plus(-1).exists:
                    place(b.plus(-1))
                if b.plus(2).exists:
                    gather(b.plus(2))
                if b.plus(1).exists:
                    turn(b.plus(1), 0)
                if b.plus(-1).exists:
                    output(b.plus(-1))

            batches(pe, step)
            place(last_batch)
            output(last_batch)


def experts(nc, k, a):
    RING = 6
    WR = WSLOTS
    with ExitStack() as stack:
        s = Space(nc, stack, "experts")
        rows = s.sb("rows", [P, RING, 2, XW])
        dest = s.sb("dest", [P, RING, 2], U32)
        u = s.sb("u", [P, 2, NT])
        usum = s.sb("usum", [P, NT])
        root_made, weight_links = s.sem("root_made"), s.sem("weight_links")
        w = s.sb("w", [P, WR, WM], F32R)
        w1 = w[:, :, 0:2 * F].rearrange("p s (a f) -> p s a f", a=2)
        w2 = w[:, :, 2 * F:4 * F].rearrange("p s (a c d) -> p s a c d", a=2, c=FC)
        bias = w[:, :, 4 * F:WM].bitcast(F32)
        x_hi = s.sb("x_hi", [P, 2, TILE], F32R)
        x_lo = s.sb("x_lo", [P, 2, TILE], F32R)
        h = s.sb("h", [P, 2, FC, TILE])
        h_hi = s.sb("h_hi", [P, 2, FC, TILE], F32R)
        h_lo = s.sb("h_lo", [P, 2, FC, TILE], F32R)
        y_t = s.sb("y_t", [P, 2, TILE])
        y_rows = s.sb("y_rows", [P, RING, 2, D])
        ps_x = s.ps("ps_x", [P, TILE])
        ps_h = [s.ps(f"ps_h{i}", [P, FC, TILE]) for i in range(2)]
        ps_y = s.ps("ps_y", [P, TILE])
        ps_r = s.ps("ps_r", [P, 2, D])
        rows_loaded = [s.sem(f"rows_loaded{i}") for i in range(RING)]
        scattered = [s.sem(f"scattered{i}") for i in range(RING)]
        w1_loaded, w2_loaded = ([s.sem(f"{n}{i}") for i in range(WR)] for n in ("w1_loaded", "w2_loaded"))
        x_tposed, x_hi_made, x_made, upped, gelued, h_hi_made, h_made, downed, y_made, y_tposed, y_copied = (s.sem(n) for n in (
            "x_tposed", "x_hi_made", "x_made", "upped", "gelued", "h_hi_made", "h_made", "downed", "y_made", "y_tposed",
            "y_copied"))
        block = stack.enter_context(nc.Block())
        rows_d = k.rows_dram[:, :].rearrange("(t h p) c -> p t h c", h=2, p=P)
        w_d = k.w_dram[:, :].rearrange("(e p) m -> p e m", p=P)

        def tiles(eng, step):
            turns = PT_TILES // RING
            for off in range(RING):
                step(Nth(0, off, RING, PT_TILES))
            with eng.Fori(1, turns - 1) as it:
                for off in range(RING):
                    step(Nth(it, off, RING, PT_TILES))
            for off in range(RING):
                step(Nth(turns - 1, off, RING, PT_TILES))

        first = Nth(0, 0, RING, PT_TILES)
        last_tile = Nth(PT_TILES // RING - 1, RING - 1, RING, PT_TILES)

        @block.sync
        def _(sp):
            def load_weights(j):
                i = j.mod(WR)
                e = sp.value_load(k.tile_expert[:, ds(j.n + WR, 1)], min_val=0, max_val=E - 1)
                before = sp.value_load(k.tile_expert[:, ds(j.n, 1)], min_val=-1, max_val=E - 1)
                if j.after(WR):
                    sp.wait_ge(upped, j.upto(lag=WR, each=2))
                    j.carry(sp, k.carried_s)
                with sp.If(e != before):
                    sp.dma_start(w[:, i, 0:2 * F].bitcast(F32),
                                 w_d[:, ds(e, 1), 0:2 * F].rearrange("p e m -> p (e m)")).then_inc(w1_loaded[i], 16)
                with sp.Else():
                    sp.sem_inc(w1_loaded[i], 16)
                if j.after(WR):
                    sp.wait_ge(y_made, j.upto(lag=WR))
                    j.carry(sp, k.carried_s)
                with sp.If(e != before):
                    sp.dma_start(w[:, i, 2 * F:WM].bitcast(F32),
                                 w_d[:, ds(e, 1), 2 * F:WM].rearrange("p e m -> p (e m)")).then_inc(w2_loaded[i], 16)
                with sp.Else():
                    sp.sem_inc(w2_loaded[i], 16)

            tiles(sp, load_weights)

        @block.gpsimd
        def _(g):
            g.tensor_tensor(k.root[:, :, :].rearrange("p s n -> p (s n)"), k.rad[:, :, :].rearrange("p s n -> p (s n)"),
                            k.pow_half[:, :], ALU.pow).then_inc(root_made, 1)
            bound = g.snap(2 * NTOK - 1)

            def step(j):
                r = j.mod(RING)
                g.wait_ge(y_copied, j.upto())
                j.carry(g, k.carried_g)
                for h_ in range(2):
                    g.indirect_dma_start(out=k.y_dram[:, :], out_offset=bass.IndirectOffsetOnAxis(ap=dest[:, r, h_:h_ + 1], axis=0),
                                         in_=y_rows[:, r, h_, :], in_offset=None,
                                         bounds_check=bound, oob_is_err=False).then_inc(scattered[r], 16)
            tiles(g, step)
            for r in range(RING):
                g.wait_ge(scattered[r], 32 * (PT_TILES // RING))

        @block.tensor
        def _(pe):
            def turn_in(j):
                r = j.mod(RING)
                pe.wait_ge(rows_loaded[r], j.upto(each=16, ring=RING))
                if j.after(1):
                    pe.wait_ge(x_made, j.upto(lag=1))
                for h_ in range(2):
                    last = pe.transpose(ps_x[:, h_ * P:(h_ + 1) * P], rows[:, r, h_, 0:D], k.ident[:, :])
                last.then_inc(x_tposed, 1)

            def three(out, w_hi, w_lo, m_hi, m_lo, start, stop):
                pe.matmul(out, w_hi, m_hi, start=start, stop=False)
                pe.matmul(out, w_hi, m_lo, start=False, stop=False)
                return pe.matmul(out, w_lo, m_hi, start=False, stop=stop)

            def up(j):
                i, n = j.mod(2), j.mod(WR)
                pe.wait_ge(x_made, j.upto())
                pe.wait_ge(w1_loaded[n], j.upto(each=16, ring=WR))
                for c in range(FC):
                    if c % 2 == 0:
                        if j.after(2):
                            pe.wait_ge(gelued, j.upto(lag=2, each=2, part=c // 2))
                    col = slice(c * P, (c + 1) * P)
                    last = three(ps_h[i][:, c, :], w1[:, n, 0, col], w1[:, n, 1, col],
                                 x_hi[:, i, :], x_lo[:, i, :], True, True)
                    if c % 2:
                        last.then_inc(upped, 1)

            def down(j):
                i, n = j.mod(2), j.mod(WR)
                if j.after(1):
                    pe.wait_ge(y_made, j.upto(lag=1))
                pe.wait_ge(w2_loaded[n], j.upto(each=16, ring=WR))
                for c in range(FC):
                    if c % 2 == 0:
                        pe.wait_ge(h_made, j.upto(each=2, part=c // 2))
                    last = three(ps_y[:, :], w2[:, n, 0, c, :], w2[:, n, 1, c, :],
                                 h_hi[:, i, c, :], h_lo[:, i, c, :], c == 0, c == FC - 1)
                last.then_inc(downed, 1)

            def turn_out(j):
                i = j.mod(2)
                pe.wait_ge(y_made, j.upto())
                if j.after(1):
                    pe.wait_ge(y_copied, j.upto(lag=1))
                for h_ in range(2):
                    last = pe.transpose(ps_r[:, h_, :], y_t[:, i, h_ * P:(h_ + 1) * P], k.ident[:, :])
                last.then_inc(y_tposed, 1)

            turn_in(first)

            def step(j):
                up(j)
                if j.plus(1).exists:
                    turn_in(j.plus(1))
                if j.plus(-1).exists:
                    down(j.plus(-1))
                if j.plus(-2).exists:
                    turn_out(j.plus(-2))

            tiles(pe, step)
            down(last_tile)
            turn_out(last_tile.plus(-1))
            turn_out(last_tile)

        @block.scalar
        def _(act):
            def load_rows(j):
                r = j.mod(RING)
                if j.after(RING):
                    act.wait_ge(y_copied, j.upto(lag=RING))
                act.dma_start(rows[:, r, :, :], rows_d[:, ds(j.n, 1), :, :].rearrange("p t h c -> p (t h) c")
                             ).then_inc(rows_loaded[r], 16)

            load_rows(first)
            load_rows(first.plus(1))

            def step(j):
                if j.plus(2).exists:
                    load_rows(j.plus(2))
                i, n = j.mod(2), j.mod(WR)
                act.wait_ge(w2_loaded[n], j.upto(each=16, ring=WR))
                for half in range(2):
                    part = slice(2 * half, 2 * half + 2)
                    act.wait_ge(upped, j.upto(each=2, part=half))
                    if j.after(2):
                        act.wait_ge(h_made, j.upto(lag=2, each=2, part=half))
                    for c in range(2 * half, 2 * half + 2):
                        last = act.activation(h[:, i, c, :], ps_h[i][:, c, :], ACT.Gelu, bias=bias[:, n, c:c + 1])
                    last.then_inc(gelued, 1)
                    act.wait_ge(gelued, j.upto(each=2, part=half))
                    if j.after(2):
                        act.wait_ge(downed, j.upto(lag=2))
                    act.activation(h_hi[:, i, part, :], h[:, i, part, :], ACT.Copy).then_inc(h_hi_made, 1)
            tiles(act, step)

        @block.vector
        def _(v):
            def x_split(j):
                i = j.mod(2)
                v.wait_ge(x_tposed, j.upto())
                if j.after(2):
                    v.wait_ge(upped, j.upto(lag=2, each=2))
                v.tensor_copy(x_hi[:, i, :], ps_x[:, :]).then_inc(x_hi_made, 1)
                v.wait_ge(x_hi_made, j.upto())
                v.tensor_tensor(x_lo[:, i, :], ps_x[:, :], x_hi[:, i, :].bitcast(F32), ALU.subtract).then_inc(x_made, 1)

            def h_low(j):
                i = j.mod(2)
                for half in range(2):
                    part = slice(2 * half, 2 * half + 2)
                    v.wait_ge(h_hi_made, j.upto(each=2, part=half))
                    if half == 0:
                        if j.after(2):
                            v.wait_ge(downed, j.upto(lag=2))
                    v.tensor_tensor(h_lo[:, i, part, :], h[:, i, part, :], h_hi[:, i, part, :].bitcast(F32),
                                    ALU.subtract).then_inc(h_made, 1)

            def y_add(j):
                i, n = j.mod(2), j.mod(WR)
                v.wait_ge(downed, j.upto())
                v.wait_ge(w2_loaded[n], j.upto(each=16, ring=WR))
                if j.after(2):
                    v.wait_ge(y_tposed, j.upto(lag=2))
                v.tensor_scalar(y_t[:, i, :], ps_y[:, :], bias[:, n, FC:FC + 1], None, ALU.add).then_inc(y_made, 1)

            def y_copy(j):
                r = j.mod(RING)
                v.wait_ge(y_tposed, j.upto())
                if j.after(RING):
                    v.wait_ge(scattered[r], j.upto(lag=RING, each=32, ring=RING))
                v.tensor_copy(dest[:, r, :], rows[:, r, :, D].bitcast(U32))
                v.tensor_copy(y_rows[:, r, :, :], ps_r[:, :, :]).then_inc(y_copied, 1)

            x_split(first)

            def step(j):
                if j.plus(1).exists:
                    x_split(j.plus(1))
                if j.plus(-1).exists:
                    y_add(j.plus(-1))
                h_low(j)
                if j.plus(-2).exists:
                    y_copy(j.plus(-2))

            tiles(v, step)
            y_add(last_tile)
            y_copy(last_tile.plus(-1))
            y_copy(last_tile)
            chain = Chain(v, weight_links)
            v.wait_ge(root_made, 1)
            chain(v.tensor_tensor(u[:, :, :], k.root[:, :, :], k.arg[:, :, :], ALU.add))
            chain(v.reciprocal(u[:, :, :], u[:, :, :]))
            chain(v.tensor_tensor(usum[:, :], u[:, 0, :], u[:, 1, :], ALU.add))
            chain(v.reciprocal(usum[:, :], usum[:, :]))
            for j in range(2):
                v.tensor_tensor(k.pair_weight[:, j, :], u[:, j, :], usum[:, :], ALU.mult)


def combine(nc, k, out):
    N = 4
    steps, YR = NT // N, 4
    with ExitStack() as stack:
        s = Space(nc, stack, "combine")
        y = s.sb("y", [P, YR, 2, N, D])
        part = s.sb("part", [P, 2, N, D])
        part2 = s.sb("part2", [P, 2, N, D])
        res = s.sb("res", [P, YR, N, D])
        loaded = [s.sem(f"loaded{i}") for i in range(YR)]
        stored = [s.sem(f"stored{i}") for i in range(YR)]
        first_made, both_made, added = (s.sem(n) for n in ("first_made", "both_made", "added"))
        block = stack.enter_context(nc.Block())
        y_d = k.y_dram[:, :].rearrange("(s n p) d -> p s n d", s=2, p=P)
        out_d = out.rearrange("b (c p) d -> p (b c) d", p=P)

        def each_step(eng, step):
            for off in range(YR):
                step(Nth(0, off, YR, steps))
            with eng.Fori(1, steps // YR) as it:
                for off in range(YR):
                    step(Nth(it, off, YR, steps))

        @block.sync
        def _(sp):
            def step(b):
                i = b.mod(YR)
                if b.after(YR):
                    sp.wait_ge(added, b.upto(lag=YR))
                for j in range(2):
                    sp.dma_start(y[:, i, j, :, :], y_d[:, j, ds(b.n * N, N), :]).then_inc(loaded[i], 16)
            each_step(sp, step)

        @block.vector
        def _(v):
            def step(b):
                i = b.mod(YR)
                v.wait_ge(loaded[i], b.upto(each=32, ring=YR))
                v.wait_ge(first_made, b.upto())
                for n in range(N):
                    last = v.scalar_tensor_tensor(
                        part2[:, b.mod(2), n, :], y[:, i, 1, n, :], k.pair_weight[:, 1, ds(b.n * N + n, 1)],
                        part[:, b.mod(2), n, :], ALU.mult, ALU.add)
                last.then_inc(both_made, 1)
                v.wait_ge(both_made, b.upto())
                if b.after(YR):
                    v.wait_ge(stored[i], b.upto(lag=YR, each=16, ring=YR))
                v.tensor_tensor(res[:, i, :, :], part2[:, b.mod(2), :, :], k.qvg[:, ds(b.n * N, N), 0:D], ALU.add
                                ).then_inc(added, 1)
            each_step(v, step)

        @block.scalar
        def _(act):
            def step(b):
                i = b.mod(YR)
                act.wait_ge(loaded[i], b.upto(each=32, ring=YR))
                if b.after(2):
                    act.wait_ge(both_made, b.upto(lag=2))
                for n in range(N):
                    last = act.activation(part[:, b.mod(2), n, :], y[:, i, 0, n, :], ACT.Copy,
                                          scale=k.pair_weight[:, 0, ds(b.n * N + n, 1)])
                last.then_inc(first_made, 1)
                if b.after(1):
                    store(b.plus(-1))

            def store(b):
                i = b.mod(YR)
                act.wait_ge(added, b.upto())
                act.dma_start(out_d[:, ds(b.n * N, N), :], res[:, i, :, :]).then_inc(stored[i], 16)
            each_step(act, step)
            store(Nth(steps // YR - 1, YR - 1, YR, steps))
            for i in range(YR):
                act.wait_ge(stored[i], 16 * (steps // YR))


class Kept:

    def __init__(self, nc, s):
        self.w_proj = s.sb("w_proj", [D, NP])
        self.wk = s.sb("wk", [D, D])
        self.wo = s.sb("wo", [D, D])
        self.b_cols = s.sb("b_cols", [P, 2])
        self.expert_bias = s.sb("expert_bias", [P, E, BC])
        self.bias3 = s.sb("bias3", [3, NBR], BF16)
        self.ident = s.sb("ident", [P, P])
        self.minus_rest = s.sb("minus_rest", [P, P], BF16)
        self.ones_bf = s.sb("ones_bf", [P, P], BF16)
        self.head_mask = s.sb("head_mask", [P, NG, HG, TOP_Q])
        self.slot_mask = s.sb("slot_mask", [SL, HG, HD])
        self.expert_id = s.sb("expert_id", [P, E])
        self.tile_start = s.sb("tile_start", [1, PT_TILES])
        self.token_id = s.sb("token_id", [P, NT, 2], I32)
        self.token_in_batch = s.sb("token_in_batch", [P, TC])
        self.token_row = s.sb("token_row", [P, T])
        self.causal_ramp = s.sb("causal_ramp", [P, T])
        self.unused = s.sb("unused", [P, INIT, XW])
        self.pow_mhalf = s.sb("pow_mhalf", [P, NT])
        self.pow_half = s.sb("pow_half", [P, 2 * NT])
        self.cent_sq = s.sb("cent_sq", [P, E])
        self.qvg = s.sb("qvg", [P, NT, KEEP])
        self.k_t = s.sb("k_t", [P, B * T])
        self.q_norm = s.sb("q_norm", [P, TC, B, H])
        self.norm_sq = s.sb("norm_sq", [P, NT])
        self.place = s.sb("place", [P, NT, 2], U32)
        self.tile_expert = s.sb("tile_expert", [1, PT_TILES + WSLOTS], I32)
        self.pair_weight = s.sb("pair_weight", [P, 2, NT])
        self.arg = s.sb("arg", [P, 2, NT])
        self.rad = s.sb("rad", [P, 2, NT])
        self.root = s.sb("root", [P, 2, NT])
        self.starts = s.sb("starts", [P, E])
        self.idx_col = s.sb("idx_col", [SL, P])
        self.minus_idx = s.sb("minus_idx", [SL, P])
        self.causal_off = s.sb("causal_off", [SL, P])
        self.sel_hi = s.sb("sel_hi", [SL, NG * (P + 32)], F32R)
        self.sel_lo = s.sb("sel_lo", [SL, NG * (P + 32)], F32R)
        self.carried_v, self.carried_g, self.carried_s = s.sem("carried_v"), s.sem("carried_g"), s.sem("carried_s")
        self.xn_dram = nc.dram_tensor("xn_scratch", (NTOK, D), F32).ap()
        self.y_dram = nc.dram_tensor("y_scratch", (2 * NTOK, D), F32).ap()
        self.rows_dram = nc.dram_tensor("rows_scratch", (LIST, XW), F32).ap()
        self.w_dram = nc.dram_tensor("w_scratch", (E * P, WM), F32).ap()
        self.idx_dram = nc.dram_tensor("idx_scratch", (B * H, TOP_Q), F32).ap()

    def q_of(self, b):
        return self.qvg[:, ds(b.n * TC, TC), 0:D]

    def own(self, sel):
        return sel[:, :].rearrange("p (g w) -> p g w", w=P + 32)[:, :, 0:32]


def program(nc, a, out):
    with ExitStack() as stack:
        k = Kept(nc, Space(nc, stack, "kept"))
        with ExitStack() as inner:
            early = Early(nc, Space(nc, inner, "early"), a)
            prepare(nc, k, early, a)
            project(nc, k, early, a)
        route(nc, k)
        attend(nc, k, a)
        experts(nc, k, a)
        combine(nc, k, out)


_INS = ["L0_attn_x", "L0_attn_Wq", "L0_attn_bq", "L0_attn_Wk", "L0_attn_bk", "L0_attn_Wv", "L0_attn_bv", "L0_attn_Wo",
        "L0_attn_bo", "L0_ffn_centroids", "L0_ffn_Wp", "L0_ffn_bp", "L0_ffn_W1", "L0_ffn_b1", "L0_ffn_W2", "L0_ffn_b2"]


def kernel(**inputs):
    import numpy as _np
    import concourse.bacc as _bacc
    from concourse.bass_utils import run_bass_kernel_spmd as _run

    nc = _bacc.Bacc("TRN2", target_bir_lowering=False, num_devices=1)
    arrays, args = {}, {}
    for name in _INS:
        x = _np.ascontiguousarray(inputs[name])
        arrays[f"in_{name}"] = x
        args[name.split("_")[-1]] = nc.dram_tensor(f"in_{name}", x.shape, mybir.dt.from_np(x.dtype), kind="ExternalInput").ap()
    out = nc.dram_tensor("out_0", (B, T, D), F32, kind="ExternalOutput").ap()
    program(nc, args, out)
    r = _run(nc, [arrays], core_ids=[0])
    return r.results[0]["out_0"]
```
